# Optimizing a Trainium2 kernel written in Bass

```python
import numpy as np
import jax
import jax.numpy as jnp

def _softmax(x, axis=-1):
    return jax.nn.softmax(x, axis=axis)

def _gelu(x):
    return jax.nn.gelu(x, approximate=True)

def _silu(x):
    return jax.nn.silu(x)

def _sigmoid(x):
    return jax.nn.sigmoid(x)

def _layernorm(x, axis=-1, eps=1e-05):
    m = jnp.mean(x, axis=axis, keepdims=True)
    v = jnp.var(x, axis=axis, keepdims=True)
    return (x - m) / jnp.sqrt(v + eps)

def _scatter_add(tgt, idx, src, axis=0):
    return tgt.at[idx].add(src)

def _segment_sum(src, seg, n):
    return jax.ops.segment_sum(src, seg, n)
kernel_name = 'mk_prb_d2_jaxref_r8_6604c0'

def setup_inputs(seed: int=0):
    np.random.seed(seed)
    _w = jnp.asarray

    def _L0_attn_setup():
        import jax, jax.numpy as jnp
        import numpy as np
        LN_EPS = 1e-05

        def _rmsnorm(x, w):
            eps = jnp.finfo(x.dtype).eps
            return x * jax.lax.rsqrt(jnp.mean(x * x, axis=-1, keepdims=True) + eps) * w

        def _layernorm(x, w, b):
            mu = jnp.mean(x, axis=-1, keepdims=True)
            var = jnp.mean((x - mu) ** 2, axis=-1, keepdims=True)
            return (x - mu) * jax.lax.rsqrt(var + LN_EPS) * w + b

        def _gated_delta_rule_scan(q, k, v, lam_h, beta_h):
            B, L, H, d = q.shape
            qT = jnp.moveaxis(q, 1, 0)
            kT = jnp.moveaxis(k, 1, 0)
            vT = jnp.moveaxis(v, 1, 0)
            lam = lam_h[None, :, None, None]
            beta = beta_h[None, :, None, None]

            def step(S, inp):
                q_t, k_t, v_t = inp
                S = S * lam
                err = v_t - jnp.einsum('bhk,bhkv->bhv', k_t, S)
                S = S + beta * (k_t[..., :, None] * err[..., None, :])
                o_t = jnp.einsum('bhk,bhkv->bhv', q_t, S)
                return (S, o_t)
            S0 = jnp.zeros((B, H, d, d), dtype=q.dtype)
            _, o = jax.lax.scan(step, S0, (qT, kT, vT))
            return jnp.moveaxis(o, 0, 1)

        def _apan_forward(x, W, k_norm_w, o_norm_w, o_norm_b, eta_raw, lam_logit):
            B, L, D = x.shape
            H = eta_raw.shape[0]
            d = D // H
            lam = jax.nn.sigmoid(lam_logit)
            eta = jnp.tanh(eta_raw)
            x_act = x
            static_out = x_act @ W.T
            k = _rmsnorm(x_act.reshape(B, L, H, d), k_norm_w)
            q = k
            v_neg = -static_out.reshape(B, L, H, d)
            beta_neg = -(eta * (1.0 - lam) / d)
            o_dyn = _gated_delta_rule_scan(q, k, v_neg, lam, beta_neg)
            return _layernorm(static_out + o_dyn.reshape(B, L, D), o_norm_w, o_norm_b)
        key = jax.random.key(seed)
        k0, k1 = jax.random.split(key)
        B, L, D, H = (4, 256, 128, 16)
        x = jax.random.normal(k0, (B, L, D), dtype=jnp.float32)
        W = jax.random.normal(k1, (D, D), dtype=jnp.float32) / np.sqrt(D)
        k_norm_w = jnp.ones((D // H,), dtype=jnp.float32)
        o_norm_w = jnp.ones((D,), dtype=jnp.float32)
        o_norm_b = jnp.zeros((D,), dtype=jnp.float32)
        eta_raw = jnp.full((H,), float(np.arctanh(0.5)), dtype=jnp.float32)
        lam_logit = jnp.full((H,), float(np.log(0.99 / 0.01)), dtype=jnp.float32)
        return {'x': x, 'W': W, 'k_norm_w': k_norm_w, 'o_norm_w': o_norm_w, 'o_norm_b': o_norm_b, 'eta_raw': eta_raw, 'lam_logit': lam_logit}
    _L0_attn_in = _L0_attn_setup()

    def _L0_ffn_setup():
        import jax, jax.numpy as jnp
        import numpy as np
        D_IN, D_HID = (128, 512)

        def _ternary(key, shape):
            return jax.random.randint(key, shape, -1, 2).astype(jnp.float32)

        def _tlin(x, w, s):
            return jnp.einsum('bsi,oi->bso', x, w) * s
        key = jax.random.key(seed)
        ks = jax.random.split(key, 12)
        inv = lambda fan: 1.0 / np.sqrt(fan).astype(np.float32)
        return {'x': jax.random.normal(ks[0], (4, 256, D_IN), dtype=jnp.float32), 'w1_w': _ternary(ks[1], (D_HID, D_IN)), 'w1_s': jax.random.uniform(ks[2], (D_HID,), dtype=jnp.float32) * inv(D_IN), 'w2_w': _ternary(ks[3], (D_HID, D_IN)), 'w2_s': jax.random.uniform(ks[4], (D_HID,), dtype=jnp.float32) * inv(D_IN), 'h1_w': _ternary(ks[5], (D_HID, D_HID)), 'h1_s': jax.random.uniform(ks[6], (D_HID,), dtype=jnp.float32) * inv(D_HID), 'h2_w': _ternary(ks[7], (D_HID, D_HID)), 'h2_s': jax.random.uniform(ks[8], (D_HID,), dtype=jnp.float32) * inv(D_HID), 'w3_w': _ternary(ks[9], (D_IN, D_HID)), 'w3_s': jax.random.uniform(ks[10], (D_IN,), dtype=jnp.float32) * inv(D_HID)}
    _L0_ffn_in = _L0_ffn_setup()

    def _L1_attn_setup():
        import jax, jax.numpy as jnp
        import numpy as np
        D_MODEL = 128
        NUM_HEADS = 16
        HEAD_DIM = D_MODEL // NUM_HEADS
        key = jax.random.key(seed)
        ks = jax.random.split(key, 10)
        B, L = (2, 256)
        s = 1.0 / np.sqrt(D_MODEL)
        x = jax.random.normal(ks[0], (B, L, D_MODEL), dtype=jnp.float32)
        Wq = jax.random.normal(ks[1], (D_MODEL, D_MODEL), dtype=jnp.float32) * s
        bq = jnp.zeros((D_MODEL,), dtype=jnp.float32)
        Wk = jax.random.normal(ks[2], (D_MODEL, D_MODEL), dtype=jnp.float32) * s
        bk = jnp.zeros((D_MODEL,), dtype=jnp.float32)
        Wv = jax.random.normal(ks[3], (D_MODEL, D_MODEL), dtype=jnp.float32) * s
        bv = jnp.zeros((D_MODEL,), dtype=jnp.float32)
        Wo = jax.random.normal(ks[4], (D_MODEL, D_MODEL), dtype=jnp.float32) * s
        bo = jnp.zeros((D_MODEL,), dtype=jnp.float32)
        gamma = jax.random.uniform(ks[5], (NUM_HEADS,), dtype=jnp.float32, minval=0.95, maxval=1.0)
        return {'x': x, 'Wq': Wq, 'bq': bq, 'Wk': Wk, 'bk': bk, 'Wv': Wv, 'bv': bv, 'Wo': Wo, 'bo': bo, 'gamma': gamma}
    _L1_attn_in = _L1_attn_setup()

    def _L1_ffn_setup():
        import jax, jax.numpy as jnp
        import numpy as np
        key = jax.random.key(seed)
        k1, k2, k3, k4, k5 = jax.random.split(key, 5)
        d_in, d_out, r = (128, 128, 32)
        x = jax.random.normal(k1, (8, 1024, d_in), dtype=jnp.float32)
        W = jax.random.normal(k2, (d_out, d_in), dtype=jnp.float32) * (1.0 / np.sqrt(d_in))
        b = jax.random.normal(k3, (d_out,), dtype=jnp.float32) * 0.01
        V_r = jax.random.normal(k4, (d_in, r), dtype=jnp.float32) * (1.0 / np.sqrt(d_in))
        C = jax.random.normal(k5, (d_out, r), dtype=jnp.float32) * (1.0 / np.sqrt(r))
        return {'x': x, 'W': W, 'b': b, 'V_r': V_r, 'C': C}
    _L1_ffn_in = _L1_ffn_setup()
    _d = {'L0_attn_x': _L0_attn_in['x'], 'L0_attn_W': _L0_attn_in['W'], 'L0_attn_k_norm_w': _L0_attn_in['k_norm_w'], 'L0_attn_o_norm_w': _L0_attn_in['o_norm_w'], 'L0_attn_o_norm_b': _L0_attn_in['o_norm_b'], 'L0_attn_eta_raw': _L0_attn_in['eta_raw'], 'L0_attn_lam_logit': _L0_attn_in['lam_logit'], 'L0_ffn_w1_w': _L0_ffn_in['w1_w'], 'L0_ffn_w1_s': _L0_ffn_in['w1_s'], 'L0_ffn_w2_w': _L0_ffn_in['w2_w'], 'L0_ffn_w2_s': _L0_ffn_in['w2_s'], 'L0_ffn_h1_w': _L0_ffn_in['h1_w'], 'L0_ffn_h1_s': _L0_ffn_in['h1_s'], 'L0_ffn_h2_w': _L0_ffn_in['h2_w'], 'L0_ffn_h2_s': _L0_ffn_in['h2_s'], 'L0_ffn_w3_w': _L0_ffn_in['w3_w'], 'L0_ffn_w3_s': _L0_ffn_in['w3_s'], 'L1_attn_Wq': _L1_attn_in['Wq'], 'L1_attn_bq': _L1_attn_in['bq'], 'L1_attn_Wk': _L1_attn_in['Wk'], 'L1_attn_bk': _L1_attn_in['bk'], 'L1_attn_Wv': _L1_attn_in['Wv'], 'L1_attn_bv': _L1_attn_in['bv'], 'L1_attn_Wo': _L1_attn_in['Wo'], 'L1_attn_bo': _L1_attn_in['bo'], 'L1_attn_gamma': _L1_attn_in['gamma'], 'L1_ffn_W': _L1_ffn_in['W'], 'L1_ffn_b': _L1_ffn_in['b'], 'L1_ffn_V_r': _L1_ffn_in['V_r'], 'L1_ffn_C': _L1_ffn_in['C']}
    _x0 = _d['L0_attn_x']
    _d['L0_attn_x'] = jax.random.normal(jax.random.fold_in(jax.random.key(seed), 1), (16, 512, 128), dtype=_x0.dtype)
    del _x0
    return _d

def reference(L0_attn_x, L0_attn_W, L0_attn_k_norm_w, L0_attn_o_norm_w, L0_attn_o_norm_b, L0_attn_eta_raw, L0_attn_lam_logit, L0_ffn_w1_w, L0_ffn_w1_s, L0_ffn_w2_w, L0_ffn_w2_s, L0_ffn_h1_w, L0_ffn_h1_s, L0_ffn_h2_w, L0_ffn_h2_s, L0_ffn_w3_w, L0_ffn_w3_s, L1_attn_Wq, L1_attn_bq, L1_attn_Wk, L1_attn_bk, L1_attn_Wv, L1_attn_bv, L1_attn_Wo, L1_attn_bo, L1_attn_gamma, L1_ffn_W, L1_ffn_b, L1_ffn_V_r, L1_ffn_C):

    def _L0_attn_ref(x, W, k_norm_w, o_norm_w, o_norm_b, eta_raw, lam_logit):
        import jax, jax.numpy as jnp
        import numpy as np
        LN_EPS = 1e-05

        def _rmsnorm(x, w):
            eps = jnp.finfo(x.dtype).eps
            return x * jax.lax.rsqrt(jnp.mean(x * x, axis=-1, keepdims=True) + eps) * w

        def _layernorm(x, w, b):
            mu = jnp.mean(x, axis=-1, keepdims=True)
            var = jnp.mean((x - mu) ** 2, axis=-1, keepdims=True)
            return (x - mu) * jax.lax.rsqrt(var + LN_EPS) * w + b

        def _gated_delta_rule_scan(q, k, v, lam_h, beta_h):
            B, L, H, d = q.shape
            qT = jnp.moveaxis(q, 1, 0)
            kT = jnp.moveaxis(k, 1, 0)
            vT = jnp.moveaxis(v, 1, 0)
            lam = lam_h[None, :, None, None]
            beta = beta_h[None, :, None, None]

            def step(S, inp):
                q_t, k_t, v_t = inp
                S = S * lam
                err = v_t - jnp.einsum('bhk,bhkv->bhv', k_t, S)
                S = S + beta * (k_t[..., :, None] * err[..., None, :])
                o_t = jnp.einsum('bhk,bhkv->bhv', q_t, S)
                return (S, o_t)
            S0 = jnp.zeros((B, H, d, d), dtype=q.dtype)
            _, o = jax.lax.scan(step, S0, (qT, kT, vT))
            return jnp.moveaxis(o, 0, 1)

        def _apan_forward(x, W, k_norm_w, o_norm_w, o_norm_b, eta_raw, lam_logit):
            B, L, D = x.shape
            H = eta_raw.shape[0]
            d = D // H
            lam = jax.nn.sigmoid(lam_logit)
            eta = jnp.tanh(eta_raw)
            x_act = x
            static_out = x_act @ W.T
            k = _rmsnorm(x_act.reshape(B, L, H, d), k_norm_w)
            q = k
            v_neg = -static_out.reshape(B, L, H, d)
            beta_neg = -(eta * (1.0 - lam) / d)
            o_dyn = _gated_delta_rule_scan(q, k, v_neg, lam, beta_neg)
            return _layernorm(static_out + o_dyn.reshape(B, L, D), o_norm_w, o_norm_b)
        return _apan_forward(x, W, k_norm_w, o_norm_w, o_norm_b, eta_raw, lam_logit)

    def _L0_ffn_ref(x, w1_w, w1_s, w2_w, w2_s, h1_w, h1_s, h2_w, h2_s, w3_w, w3_s):
        import jax, jax.numpy as jnp
        import numpy as np
        D_IN, D_HID = (128, 512)

        def _ternary(key, shape):
            return jax.random.randint(key, shape, -1, 2).astype(jnp.float32)

        def _tlin(x, w, s):
            return jnp.einsum('bsi,oi->bso', x, w) * s
        h = jax.nn.silu(_tlin(x, w1_w, w1_s)) * _tlin(x, w2_w, w2_s)
        h = jax.nn.gelu(_tlin(h, h1_w, h1_s), approximate=False)
        h = jax.nn.gelu(_tlin(h, h2_w, h2_s), approximate=False)
        return _tlin(h, w3_w, w3_s)

    def _L1_attn_ref(x, Wq, bq, Wk, bk, Wv, bv, Wo, bo, gamma):
        import jax, jax.numpy as jnp
        import numpy as np
        D_MODEL = 128
        NUM_HEADS = 16
        HEAD_DIM = D_MODEL // NUM_HEADS
        B, L, D = x.shape
        H, hd = (NUM_HEADS, HEAD_DIM)
        q = (x @ Wq.T + bq).reshape(B, L, H, hd).transpose(0, 2, 1, 3)
        k = (x @ Wk.T + bk).reshape(B, L, H, hd).transpose(0, 2, 1, 3)
        v = (x @ Wv.T + bv).reshape(B, L, H, hd).transpose(0, 2, 1, 3)
        idx = jnp.arange(L, dtype=x.dtype)
        decay = gamma[None, :, None, None] ** idx[None, None, :, None]
        scores = jnp.einsum('bhqd,bhkd->bhqk', q, k)
        causal = jnp.tril(jnp.ones((L, L), dtype=x.dtype))
        scores = scores * causal[None, None] * decay
        out = jnp.einsum('bhqk,bhkd->bhqd', scores, v)
        out = out.transpose(0, 2, 1, 3).reshape(B, L, D)
        return out @ Wo.T + bo

    def _L1_ffn_ref(x, W, b, V_r, C):
        import jax, jax.numpy as jnp
        import numpy as np
        base = jnp.einsum('bsd,od->bso', x, W) + b
        correction = jnp.einsum('bsr,or->bso', jnp.einsum('bsd,dr->bsr', x, V_r), C)
        return base + correction
    x = L0_attn_x
    xn = _layernorm(x, axis=-1)
    x = x + _L0_attn_ref(xn, L0_attn_W, L0_attn_k_norm_w, L0_attn_o_norm_w, L0_attn_o_norm_b, L0_attn_eta_raw, L0_attn_lam_logit) + _L0_ffn_ref(xn, L0_ffn_w1_w, L0_ffn_w1_s, L0_ffn_w2_w, L0_ffn_w2_s, L0_ffn_h1_w, L0_ffn_h1_s, L0_ffn_h2_w, L0_ffn_h2_s, L0_ffn_w3_w, L0_ffn_w3_s)
    xn = _layernorm(x, axis=-1)
    x = x + _L1_attn_ref(xn, L1_attn_Wq, L1_attn_bq, L1_attn_Wk, L1_attn_bk, L1_attn_Wv, L1_attn_bv, L1_attn_Wo, L1_attn_bo, L1_attn_gamma) + _L1_ffn_ref(xn, L1_ffn_W, L1_ffn_b, L1_ffn_V_r, L1_ffn_C)
    return x

_drawn_inputs = setup_inputs


def setup_inputs(seed=0):
    import zlib

    import numpy as np

    out = dict(_drawn_inputs(seed))
    spreads = {'L0_attn_k_norm_w': (1.0, 0.2),
     'L0_attn_o_norm_w': (1.0, 0.2),
     'L0_attn_o_norm_b': (0.0, 0.1),
     'L0_attn_eta_raw': (0.5493061542510986, 0.2),
     'L0_attn_lam_logit': (4.595119953155518, 0.2),
     'L1_attn_bq': (0.0, 0.1),
     'L1_attn_bk': (0.0, 0.1),
     'L1_attn_bv': (0.0, 0.1),
     'L1_attn_bo': (0.0, 0.1)}
    factors = {}
    for name, (base, spread) in spreads.items():
        noise = np.random.default_rng([zlib.crc32(name.encode()), seed]).standard_normal(out[name].shape)
        drawn = base * np.exp(spread * noise) if base else spread * noise
        out[name] = jnp.asarray(drawn.astype(out[name].dtype))
    for name, factor in factors.items():
        out[name] = (out[name] * factor).astype(out[name].dtype)
    return out
```

```python
import concourse.bass as bass
from concourse import mybir
from contextlib import ExitStack

F32 = mybir.dt.float32
F32R = mybir.dt.float32r
I32 = mybir.dt.int32
ALU = mybir.AluOpType
ACT = mybir.ActivationFunctionType
AX = mybir.AxisListType

B, L, D = 16, 512, 128
H, DH = 16, 8
HID = 512
P = 128
NT = L // P
NB = HID // P
RANK = 32
G = B * H // P
BG = B // G
BLK = 4
PAIRS = BLK * (BLK - 1) // 2
SEG = 64
LN_EPS = 1e-5
F32_EPS = 1.1920928955078125e-07

W1, W2, H1, H2, W3 = 0, NB, 2 * NB, 2 * NB + NB * NB, 2 * NB + 2 * NB * NB
NW = W3 + NB


def build(nc, io, out):
    scr = {}
    for name in ("xnT", "P", "K", "R", "fac", "W", "ffnT"):
        rows = B + 1 if name in ("xnT", "ffnT") else B
        scr[name] = nc.dram_tensor("scratch_" + name, [rows, P, L], F32).ap()
    with ExitStack() as ctx:
        c = constants(nc, ctx)
        setup(nc, io, c)
        prepare(nc, io, scr, c)
        recur_and_feed_forward(nc, io, scr, c)
        second_layer(nc, io, scr, c, out)


class Tiles:
    pass


def constants(nc, ctx):
    c = Tiles()

    def sb(name, shape, dt=F32):
        return ctx.enter_context(nc.sbuf_tensor(name, shape, dt))

    c.ident = sb("ident", [P, P])
    c.head_ones = sb("head_ones", [P, P])
    c.tri = sb("tri", [P, P])
    c.w_hi = sb("w_hi", [P, NW, P], F32R)
    c.w_lo = sb("w_lo", [P, NW, P], F32R)
    c.ws_t = sb("ws_t", [P, P])
    c.wqkv_t = sb("wqkv_t", [P, 3 * P])
    c.wo_t = sb("wo_t", [P, P])
    c.weff_t = sb("weff_t", [P, P])
    c.s1 = sb("s1", [P, NB])
    c.s2 = sb("s2", [P, NB])
    c.t1 = sb("t1", [P, NB])
    c.t2 = sb("t2", [P, NB])
    c.s3 = sb("s3", [P, 1])
    c.knw = sb("knw", [P, 1])
    c.gate = sb("gate", [P, 1])
    c.pfac = sb("pfac", [P, BLK])
    c.kfac = sb("kfac", [P, BLK])
    c.lam4 = sb("lam4", [P, 1])
    c.dec = sb("dec", [P, NT, P])
    c.bqkv = sb("bqkv", [P, 3 * P])
    c.bo = sb("bo", [P, P])
    c.ow = sb("ow", [P, P])
    c.ob = sb("ob", [P, 1])
    c.eps_ln = sb("eps_ln", [P, 1])
    c.eps_rms = sb("eps_rms", [P, 1])
    c.flag = sb("flag", [1, 1], I32)
    return c


def setup(nc, io, c):
    ctx = ExitStack()
    with ctx:
        def sb(name, shape, dt=F32):
            return ctx.enter_context(nc.sbuf_tensor(name, shape, dt))

        def sem(name):
            return ctx.enter_context(nc.semaphore(name))

        nat12 = sb("nat12", [P, 2, NB, P])
        nath = sb("nath", [P, 2, NB, HID])
        nat3 = sb("nat3", [P, HID])
        nats = sb("nats", [P, 6, P])
        natr = sb("natr", [P, 2, RANK])
        vr_t = sb("vr_t", [RANK, 2, P])
        par = sb("par", [P, 4])
        work = sb("work", [P, 16])
        dec_t = sb("dec_t", [P, L])
        ones = sb("ones", [P, L])
        bf = sb("bf", [P, P])
        peaks = sb("peaks", [P, NW // NB])
        peak = sb("peak", [P, 1])
        ftmp = sb("ftmp", [1, 2])
        ps = [ctx.enter_context(nc.psum_tensor(f"ps_set{i}", [P, 4, P], F32)) for i in range(2)]
        ps_s = ctx.enter_context(nc.psum_tensor("ps_small", [P, 4, P], F32))
        ps_d = ctx.enter_context(nc.psum_tensor("ps_dec", [P, 4, P], F32))

        loaded = sem("s_loaded")
        const_done = sem("s_const")
        pool_chain = sem("s_pool_chain")
        tr_done = sem("s_tr")
        hi_done = sem("s_hi")
        lo_done = sem("s_lo")
        small_tr = sem("s_small_tr")
        small_cp = sem("s_small_cp")
        vec = sem("s_vec")
        exps = sem("s_exps")
        peak_done = sem("s_peak")
        peak_tr = sem("s_peak_tr")
        dec_ready = sem("s_dec_ready")
        dec_tr = sem("s_dec_tr")
        weff = sem("s_weff")

        groups = [[nat12[:, 0, j, :] for j in range(NB)], [nat12[:, 1, j, :] for j in range(NB)]]
        for w in range(2):
            groups += [[nath[:, w, o, i * P:(i + 1) * P] for o in range(NB)] for i in range(NB)]
        groups += [[nat3[:, i * P:(i + 1) * P] for i in range(NB)]]
        NG = len(groups)

        loads = []

        def add(dst, src):
            loads.append((dst, src))

        add(nat12[:, 0, :, :], io["L0_ffn_w1_w"].rearrange("(o p) i -> p o i", p=P))
        add(nat12[:, 1, :, :], io["L0_ffn_w2_w"].rearrange("(o p) i -> p o i", p=P))
        add(nath[:, 0, :, :], io["L0_ffn_h1_w"].rearrange("(o p) i -> p o i", p=P))
        add(nath[:, 1, :, :], io["L0_ffn_h2_w"].rearrange("(o p) i -> p o i", p=P))
        add(nat3[:, :], io["L0_ffn_w3_w"])
        for n, name in enumerate(("L0_attn_W", "L1_attn_Wq", "L1_attn_Wk", "L1_attn_Wv", "L1_attn_Wo", "L1_ffn_W")):
            add(nats[:, n, :], io[name])
        add(natr[:, 0, :], io["L1_ffn_V_r"])
        add(natr[:, 1, :], io["L1_ffn_C"])
        for dst, name in ((c.s1, "L0_ffn_w1_s"), (c.s2, "L0_ffn_w2_s"), (c.t1, "L0_ffn_h1_s"), (c.t2, "L0_ffn_h2_s")):
            add(dst[:, :], io[name].rearrange("(o p) -> p o", p=P))
        add(c.s3[:, :], io["L0_ffn_w3_s"].rearrange("(p o) -> p o", o=1))
        for n, name in enumerate(("L1_attn_bq", "L1_attn_bk", "L1_attn_bv")):
            add(c.bqkv[:, n * P:(n + 1) * P], io[name].partition_broadcast(P))
        add(c.bo[:, :], io["L1_attn_bo"].partition_broadcast(P))
        add(bf[:, :], io["L1_ffn_b"].partition_broadcast(P))
        add(c.ow[:, :], io["L0_attn_o_norm_w"].partition_broadcast(P))
        add(c.ob[:, :], io["L0_attn_o_norm_b"].rearrange("(p o) -> p o", o=1))
        by_head = lambda name: io[name].rearrange("(h o) -> h o", o=1)
        for d in range(DH):
            for n, name in enumerate(("L0_attn_lam_logit", "L0_attn_eta_raw", "L1_attn_gamma")):
                add(par[d:P:DH, n:n + 1], by_head(name))
            add(par[d * H:(d + 1) * H, 3:4], by_head("L0_attn_lam_logit"))
        for h in range(H):
            add(c.knw[h * DH:(h + 1) * DH, 0:1], io["L0_attn_k_norm_w"].rearrange("(d o) -> d o", o=1))
        NL = 16 * len(loads)

        with nc.allow_non_contiguous_dma(reason='a few hundred words of scales and per-head factors'), nc.Block() as block:
            @block.sync
            def _(sp):
                for dst, src in loads[0::2]:
                    sp.dma_start(dst, src).then_inc(loaded, 16)

            @block.gpsimd
            def _(pool):
                pool.memset(c.ident[:, :], 0.0).then_inc(pool_chain, 1)
                pool.memset(c.head_ones[:, :], 1.0).then_inc(pool_chain, 1)
                pool.memset(c.tri[:, :], 1.0).then_inc(pool_chain, 1)
                pool.memset(c.eps_ln[:, :], LN_EPS)
                pool.memset(c.eps_rms[:, :], F32_EPS).then_inc(pool_chain, 1)
                pool.wait_ge(pool_chain, 4)
                pool.affine_select(out=c.ident[:, :], in_=c.ident[:, :], compare_op=ALU.not_equal, fill=1.0,
                                   base=0, pattern=[[-1, P]], channel_multiplier=1).then_inc(const_done, 1)
                pool.affine_select(out=c.tri[:, :], in_=c.tri[:, :], compare_op=ALU.is_ge, fill=0.0,
                                   base=0, pattern=[[1, P]], channel_multiplier=-1).then_inc(const_done, 1)
                heads = c.head_ones[:, :].rearrange("p (h k) -> p h k", k=DH)
                pool.affine_select(out=heads, in_=heads, compare_op=ALU.is_ge, fill=0.0,
                                   base=0, pattern=[[-DH, H], [0, DH]], channel_multiplier=1).then_inc(pool_chain, 1)
                pool.wait_ge(pool_chain, 5)
                pool.affine_select(out=heads, in_=heads, compare_op=ALU.is_ge, fill=0.0,
                                   base=DH - 1, pattern=[[DH, H], [0, DH]], channel_multiplier=-1).then_inc(const_done, 1)

            @block.tensor
            def _(pe):
                pe.wait_ge(const_done, 1)
                pe.wait_ge(loaded, NL)
                for g, blocks in enumerate(groups):
                    if g >= 2:
                        pe.wait_ge(lo_done, g - 1)
                    for n, b in enumerate(blocks):
                        last = nc.tensor.transpose(ps[g % 2][:, n, :], b, c.ident[:, :])
                    last.then_inc(tr_done, 1)
                for n in range(4):
                    last = nc.tensor.transpose(ps_s[:, n, :], nats[:, n, :], c.ident[:, :])
                last.then_inc(small_tr, 1)
                pe.wait_ge(small_cp, 2)
                nc.tensor.transpose(ps_s[:, 0, :], nats[:, 4, :], c.ident[:, :])
                nc.tensor.transpose(ps_s[0:RANK, 1, :], natr[:, 0, :], c.ident[:, :])
                nc.tensor.transpose(ps_s[0:RANK, 2, :], natr[:, 1, :], c.ident[:, :]).then_inc(small_tr, 1)
                pe.wait_ge(small_cp, 4)
                nc.tensor.matmul(ps_s[:, 3, :], nats[:, 5, :], c.ident[:, :], start=True, stop=False)
                nc.tensor.matmul(ps_s[:, 3, :], vr_t[:, 0, :], vr_t[:, 1, :], start=False, stop=True).then_inc(weff, 1)
                pe.wait_ge(dec_ready, 1)
                for n in range(NT):
                    last = nc.tensor.transpose(ps_d[:, n, :], dec_t[:, n * P:(n + 1) * P], c.ident[:, :])
                last.then_inc(dec_tr, 1)
                pe.wait_ge(peak_done, 1)
                pe.wait_ge(lo_done, NG)
                nc.tensor.transpose(ps[0][0:1, 0, :], peak[:, :], c.ident[:, :]).then_inc(peak_tr, 1)

            @block.scalar
            def _(act):
                for dst, src in loads[1::2]:
                    act.dma_start(dst, src).then_inc(loaded, 16)
                act.wait_ge(loaded, NL)
                act.activation(work[:, 0:1], par[:, 0:1], ACT.Exp, scale=-1.0)
                act.activation(work[:, 1:2], par[:, 1:2], ACT.Tanh)
                act.activation(work[:, 2:3], par[:, 3:4], ACT.Exp, scale=-1.0).then_inc(exps, 1)
                for g in range(NG):
                    act.wait_ge(tr_done, g + 1)
                    act.activation(c.w_hi[:, NB * g:NB * g + NB, :], ps[g % 2][:, :, :], ACT.Copy).then_inc(hi_done, 1)
                act.wait_ge(small_tr, 1)
                act.activation(c.ws_t[:, :], ps_s[:, 0, :], ACT.Copy).then_inc(small_cp, 1)
                act.activation(c.wqkv_t[:, :].rearrange("p (n k) -> p n k", n=3), ps_s[:, 1:4, :], ACT.Copy).then_inc(small_cp, 1)
                act.wait_ge(small_tr, 2)
                act.activation(c.wo_t[:, :], ps_s[:, 0, :], ACT.Copy).then_inc(small_cp, 1)
                act.activation(vr_t[:, :, :], ps_s[0:RANK, 1:3, :], ACT.Copy).then_inc(small_cp, 1)
                act.wait_ge(weff, 1)
                act.activation(c.weff_t[:, :], ps_s[:, 3, :], ACT.Copy)
                act.wait_ge(dec_tr, 1)
                act.activation(c.dec[:, :, :], ps_d[:, :, :], ACT.Copy)

            @block.vector
            def _(dve):
                chain = [0]

                def link(ins):
                    chain[0] += 1
                    ins.then_inc(vec, 1)
                    dve.wait_ge(vec, chain[0])

                dve.memset(ones[:, :], 1.0)
                link(dve.memset(dec_t[:, 0:1], 1.0))
                dve.wait_ge(exps, 1)
                link(dve.tensor_scalar_add(work[:, 5:6], work[:, 0:1], 1.0))
                link(dve.tensor_scalar_add(work[:, 6:7], work[:, 2:3], 1.0))
                link(dve.reciprocal(work[:, 3:4], work[:, 5:6]))
                link(dve.reciprocal(work[:, 4:5], work[:, 6:7]))
                link(dve.tensor_scalar(work[:, 7:8], work[:, 3:4], -1.0, 1.0, ALU.mult, ALU.add))
                link(dve.tensor_tensor(work[:, 8:9], work[:, 7:8], work[:, 1:2], ALU.mult))
                link(dve.tensor_scalar(c.gate[:, :], work[:, 8:9], 1.0 / DH, None, ALU.mult))
                link(dve.memset(c.kfac[:, 3:4], 1.0))
                link(dve.tensor_scalar(c.pfac[:, 0:1], c.gate[:, :], work[:, 3:4], None, ALU.mult))
                for i in range(1, BLK):
                    link(dve.tensor_scalar(c.pfac[:, i:i + 1], c.pfac[:, i - 1:i], work[:, 3:4], None, ALU.mult))
                    link(dve.tensor_scalar(c.kfac[:, 3 - i:4 - i], c.kfac[:, 4 - i:5 - i], work[:, 3:4], None, ALU.mult))
                link(dve.tensor_tensor(work[:, 9:10], work[:, 4:5], work[:, 4:5], ALU.mult))
                link(dve.tensor_tensor(c.lam4[:, :], work[:, 9:10], work[:, 9:10], ALU.mult))
                dve.tensor_tensor_scan(dec_t[:, 1:L], par[:, 2:3].to_broadcast([P, L - 1]), ones[:, 0:L - 1], 1.0,
                                       ALU.mult, ALU.mult).then_inc(dec_ready, 1)
                link(dve.tensor_tensor(c.bo[:, :], c.bo[:, :], bf[:, :], ALU.add))
                for g in range(NG):
                    dve.wait_ge(hi_done, g + 1)
                    lo = c.w_lo[:, NB * g:NB * g + NB, :]
                    ins = dve.tensor_tensor(lo, ps[g % 2][:, :, :], c.w_hi[:, NB * g:NB * g + NB, :].bitcast(F32), ALU.subtract)
                    ins.then_inc(lo_done, 1)
                    dve.wait_ge(lo_done, g + 1)
                    link(dve.tensor_reduce(peaks[:, g:g + 1], lo.bitcast(F32), AX.XY, ALU.max, apply_absolute_value=True))
                dve.tensor_reduce(peak[:, :], peaks[:, :], AX.X, ALU.max).then_inc(peak_done, 1)
                dve.wait_ge(peak_tr, 1)
                link(dve.tensor_reduce(ftmp[:, 0:1], ps[0][0:1, 0, :], AX.X, ALU.max))
                link(dve.tensor_scalar(ftmp[:, 1:2], ftmp[:, 0:1], 0.0, None, ALU.is_gt))
                dve.tensor_copy(c.flag[:, :], ftmp[:, 1:2])


def prepare(nc, io, scr, c):
    ctx = ExitStack()
    with ctx:
        def sb(name, shape, dt=F32):
            return ctx.enter_context(nc.sbuf_tensor(name, shape, dt))

        def sem(name):
            return ctx.enter_context(nc.semaphore(name))

        x_in = sb("p_x", [P, 2, NT, P])
        stats = sb("p_stats", [P, NT, 6])
        mv = sb("p_mv", [P, NT, 2])
        std = sb("p_std", [P, NT])
        rstd = sb("p_rstd", [P, NT])
        xn = sb("p_xn", [P, NT, P])
        xnT = sb("p_xnT", [P, L])
        sq = sb("p_sq", [P, L])
        rms = sb("p_rms", [P, L])
        rrms = sb("p_rrms", [P, L])
        kT = sb("p_kT", [P, L])
        k2 = sb("p_k2", [P, L])
        fac = sb("p_fac", [P, L])
        kout = sb("p_kout", [P, L])
        prod = sb("p_prod", [P, PAIRS, L // BLK])
        coup = sb("p_coup", [P, PAIRS, L // BLK])
        rp = sb("p_rp", [P, 2, L])
        tmp_r = sb("p_tmp_r", [P, 3, L // BLK])
        tmp_p = sb("p_tmp_p", [P, 3, L // BLK])
        ps_x = ctx.enter_context(nc.psum_tensor("p_ps_x", [P, L], F32))
        ps_s = ctx.enter_context(nc.psum_tensor("p_ps_s", [P, L], F32))
        ps_q = ctx.enter_context(nc.psum_tensor("p_ps_q", [P, L], F32))
        ps_k = ctx.enter_context(nc.psum_tensor("p_ps_k", [P, L], F32))
        ps_n = ctx.enter_context(nc.psum_tensor("p_ps_n", [P, 8, L // BLK], F32))

        x_ready = [sem(f"p_x_ready{u}") for u in range(2)]
        x_free = sem("p_x_free")
        stat = sem("p_stat")
        aggregating = sem("p_aggregating")
        std_ok = sem("p_std")
        xn_ok = sem("p_xn")
        x_tr = sem("p_x_tr")
        xT_ok = sem("p_xT")
        sq_ok = sem("p_sq")
        s_mm = sem("p_s_mm")
        q_mm = sem("p_q_mm")
        rms_ok = sem("p_rms")
        rr_ok = sem("p_rr")
        k_ok = sem("p_k")
        k2_ok = sem("p_k2")
        k_mm = sem("p_k_mm")
        fac_ok = sem("p_fac")
        prod_ok = sem("p_prod")
        n_mm = sem("p_n_mm")
        coup_ok = sem("p_coup")
        coup_free = sem("p_coup_free")
        r_in = sem("p_r_in")
        p_in = sem("p_p_in")
        kout_ok = sem("p_kout")
        r_step = sem("p_r_step")
        p_step = sem("p_p_step")
        st_x = sem("p_st_x")
        st_f = sem("p_st_f")
        st_k = sem("p_st_k")
        st_r = sem("p_st_r")
        st_p = sem("p_st_p")

        def by_pos(ap):
            return ap.rearrange("p (b i) -> p i b", i=BLK)

        def later(i0, ap):
            return by_pos(ap)[:, i0:BLK, :]

        def bcast(ap, n):
            return ap.to_broadcast([P, n, L // BLK])

        first = [0, 3, 5]

        def sweep(eng, ap, tmp, step, it):
            at = 0
            for j in range(BLK - 1):
                n = BLK - 1 - j
                if at:
                    eng.wait_ge(step, it * 6 + at)
                eng.tensor_tensor(tmp[:, 0:n, :], coup[:, first[j]:first[j] + n, :],
                                  bcast(by_pos(ap)[:, j:j + 1, :], n), ALU.mult).then_inc(step, 1)
                at += 1
                eng.wait_ge(step, it * 6 + at)
                last = eng.tensor_tensor(later(j + 1, ap), later(j + 1, ap), tmp[:, 0:n, :], ALU.add)
                last.then_inc(step, 1)
                at += 1

        with nc.Block() as block:
            @block.sync
            def _(sp):
                def load(n, u):
                    sp.wait_ge(x_free, n + 1)
                    sp.dma_start(x_in[:, u, :, :],
                                 io["L0_attn_x"][bass.ds(n, 1), :, :].rearrange("b (t p) d -> p (b t) d", p=P)
                                 ).then_inc(x_ready[u], 16)

                def store(n, again=False):
                    def put(name, tile, done):
                        sp.dma_start(scr[name][bass.ds(n, 1), :, :].rearrange("b p t -> p (b t)"), tile).then_inc(done, 16)
                    sp.wait_ge(xT_ok, n + 1)
                    put("xnT", xnT[:, :], st_x)
                    if again:
                        sp.dma_start(scr["xnT"][B, :, :], xnT[:, :]).then_inc(st_x, 16)
                    sp.wait_ge(kout_ok, n + 1)
                    put("K", kout[:, :], st_k)
                    sp.wait_ge(fac_ok, n + 1)
                    put("fac", fac[:, :], st_f)
                    sp.wait_ge(r_step, n * 6 + 6)
                    put("R", rp[:, 1, :], st_r)
                    sp.wait_ge(p_step, n * 6 + 6)
                    put("P", rp[:, 0, :], st_p)

                load(0, 0)
                with sp.Fori(0, B // 2 - 1) as half:
                    for u in range(2):
                        load(half * 2 + (u + 1), 1 - u)
                        store(half * 2 + u)
                load(B - 1, 1)
                store(B - 2)
                store(B - 1, again=True)
                for done in (st_x, st_k, st_f, st_r, st_p):
                    sp.wait_ge(done, 16 * B + (32 if done is st_x else 16))

            @block.gpsimd
            def _(pool):
                pool.sem_inc(coup_free, 1)
                pool.sem_inc(st_k, 16)
                pool.sem_inc(st_p, 16)
                with pool.Fori(0, B) as it:
                    pool.wait_ge(k_ok, it + 1)
                    pool.wait_ge(st_p, it * 16 + 16)
                    pool.tensor_tensor(by_pos(rp[:, 0, :]), by_pos(kT[:, :]),
                                       c.pfac[:, :].unsqueeze(2).to_broadcast([P, BLK, L // BLK]),
                                       ALU.mult).then_inc(p_in, 1)
                    pool.wait_ge(st_k, it * 16 + 16)
                    pool.tensor_tensor(by_pos(kout[:, :]), by_pos(kT[:, :]),
                                       c.kfac[:, :].unsqueeze(2).to_broadcast([P, BLK, L // BLK]),
                                       ALU.mult).then_inc(kout_ok, 1)
                    pool.wait_ge(coup_ok, it * 6 + 6)
                    pool.wait_ge(p_in, it + 1)
                    sweep(pool, rp[:, 0, :], tmp_p, p_step, it)
                    pool.wait_ge(p_step, it * 6 + 6)
                    pool.sem_inc(coup_free, 1)

            @block.scalar
            def _(act):
                act.sem_inc(st_x, 16)
                act.sem_inc(st_f, 16)
                act.sem_inc(st_r, 16)
                with act.Fori(0, B) as it:
                    act.wait_ge(stat, it * 2 + 2)
                    act.activation(std[:, :], mv[:, :, 1], ACT.Sqrt, bias=c.eps_ln[:, :]).then_inc(std_ok, 1)
                    act.wait_ge(x_tr, it + 1)
                    act.wait_ge(st_x, it * 16 + 16)
                    act.activation(xnT[:, :], ps_x[:, :], ACT.Copy).then_inc(xT_ok, 1)
                    act.activation(sq[:, :], ps_x[:, :], ACT.Square).then_inc(sq_ok, 1)
                    act.wait_ge(q_mm, it + 1)
                    act.activation(rms[:, :], ps_q[:, :], ACT.Sqrt, bias=c.eps_rms[:, :], scale=1.0 / DH).then_inc(rms_ok, 1)
                    act.wait_ge(s_mm, it + 1)
                    act.wait_ge(st_r, it * 16 + 16)
                    act.activation(rp[:, 1, :], ps_s[:, :], ACT.Copy).then_inc(r_in, 1)
                    act.wait_ge(k_ok, it + 1)
                    act.activation(k2[:, :], kT[:, :], ACT.Square).then_inc(k2_ok, 1)
                    act.wait_ge(n_mm, it + 1)
                    act.wait_ge(coup_free, it + 1)
                    at = 0
                    for j in range(BLK - 1):
                        for i in range(j + 1, BLK):
                            act.activation(coup[:, at, :], ps_n[:, at, :], ACT.Copy,
                                           scale=c.pfac[:, i - j - 1:i - j]).then_inc(coup_ok, 1)
                            at += 1
                    act.wait_ge(k_mm, it + 1)
                    act.wait_ge(st_f, it * 16 + 16)
                    act.activation(fac[:, :], ps_k[:, :], ACT.Identity, scale=c.gate[:, :], bias=1.0).then_inc(fac_ok, 1)

            @block.vector
            def _(dve):
                dve.sem_inc(x_free, 2)
                with dve.Fori(0, B // 2) as half:
                    for u in range(2):
                        it = half * 2 + u
                        dve.wait_ge(x_ready[u], half * 16 + 16)
                        for t in range(NT):
                            last = dve.bn_stats(stats[:, t, :], x_in[:, u, t, :])
                        last.then_inc(stat, 1)
                        dve.wait_ge(stat, it * 2 + 1)
                        dve.sem_inc(aggregating, 1)
                        for t in range(NT):
                            last = dve.bn_aggr(mv[:, t, :], stats[:, t, :])
                        last.then_inc(stat, 1)
                        dve.wait_ge(std_ok, it + 1)
                        dve.reciprocal(rstd[:, :], std[:, :]).then_inc(rr_ok, 1)
                        dve.wait_ge(rr_ok, it * 2 + 1)
                        for t in range(NT):
                            last = dve.tensor_scalar(xn[:, t, :], x_in[:, u, t, :], mv[:, t, 0:1], rstd[:, t:t + 1],
                                                     ALU.subtract, ALU.mult)
                        last.then_inc(xn_ok, 1)
                        dve.wait_ge(xn_ok, it + 1)
                        dve.sem_inc(x_free, 1)
                        dve.wait_ge(rms_ok, it + 1)
                        dve.reciprocal(rrms[:, :], rms[:, :]).then_inc(rr_ok, 1)
                        dve.wait_ge(rr_ok, it * 2 + 2)
                        dve.wait_ge(xT_ok, it + 1)
                        dve.scalar_tensor_tensor(out=kT[:, :], in0=xnT[:, :], scalar=c.knw[:, :], in1=rrms[:, :],
                                                 op0=ALU.mult, op1=ALU.mult).then_inc(k_ok, 1)
                        dve.wait_ge(k_ok, it + 1)
                        for j in range(BLK - 1):
                            n = BLK - 1 - j
                            last = dve.tensor_tensor(prod[:, first[j]:first[j] + n, :], later(j + 1, kT[:, :]),
                                                     bcast(by_pos(kT[:, :])[:, j:j + 1, :], n), ALU.mult)
                        last.then_inc(prod_ok, 1)
                        dve.wait_ge(coup_ok, it * 6 + 6)
                        dve.wait_ge(r_in, it + 1)
                        sweep(dve, rp[:, 1, :], tmp_r, r_step, it)
                        dve.wait_ge(kout_ok, it + 1)
                        dve.wait_ge(k2_ok, it + 1)

            @block.tensor
            def _(pe):
                with pe.Fori(0, B) as it:
                    pe.wait_ge(xn_ok, it + 1)
                    for t in range(NT):
                        last = nc.tensor.transpose(ps_x[:, t * P:(t + 1) * P], xn[:, t, :], c.ident[:, :])
                    last.then_inc(x_tr, 1)
                    pe.wait_ge(sq_ok, it + 1)
                    nc.tensor.matmul(ps_q[:, :], c.head_ones[:, :], sq[:, :], start=True, stop=True).then_inc(q_mm, 1)
                    pe.wait_ge(xT_ok, it + 1)
                    nc.tensor.matmul(ps_s[:, :], c.ws_t[:, :], xnT[:, :], start=True, stop=True).then_inc(s_mm, 1)
                    pe.wait_ge(prod_ok, it + 1)
                    nc.tensor.matmul(ps_n[:, 0:4, :], c.head_ones[:, :], prod[:, 0:4, :], start=True, stop=True)
                    nc.tensor.matmul(ps_n[:, 4:6, :], c.head_ones[:, :], prod[:, 4:6, :], start=True, stop=True).then_inc(n_mm, 1)
                    pe.wait_ge(k2_ok, it + 1)
                    nc.tensor.matmul(ps_k[:, :], c.head_ones[:, :], k2[:, :], start=True, stop=True).then_inc(k_mm, 1)


def recur_and_feed_forward(nc, io, scr, c):
    ctx = ExitStack()
    SLOTS = B
    BPS = L // BLK // SLOTS
    BSEG = SEG // BLK
    SPS = BSEG // BPS
    NSEG = L // SEG
    with ctx:
        def sb(name, shape, dt=F32):
            return ctx.enter_context(nc.sbuf_tensor(name, shape, dt))

        def sem(name):
            return ctx.enter_context(nc.semaphore(name))

        seg_p = [sb(f"r_p{u}", [P, G, DH, SEG]) for u in range(2)]
        seg_k = [sb(f"r_k{u}", [P, G, DH, SEG]) for u in range(2)]
        seg_r = [sb(f"r_r{u}", [P, G, DH, SEG]) for u in range(2)]
        seg_w = [sb(f"r_w{u}", [P, G, DH, SEG]) for u in range(2)]
        state = [sb(f"r_g{g}", [P, DH, DH]) for g in range(G)]
        pg = sb("r_pg", [P, 2, G, BLK, DH, DH + 1])
        kw = [sb(f"r_kw{g}", [P, DH * DH, BLK + 1]) for g in range(G)]

        x_f = sb("f_x", [P, L])
        x_h, x_l = sb("f_xh", [P, L], F32R), sb("f_xl", [P, L], F32R)
        a_f = sb("f_a", [P, NB, L])
        g_f = sb("f_g", [P, NB, L])
        g_h, g_l = sb("f_gh", [P, NB, L], F32R), sb("f_gl", [P, NB, L], F32R)
        h_f = sb("f_h", [P, NB, L])
        h_h, h_l = sb("f_hh", [P, NB, L], F32R), sb("f_hl", [P, NB, L], F32R)
        e_f = sb("f_e", [P, NB, L])
        e_h, e_l = sb("f_eh", [P, NB, L], F32R), sb("f_el", [P, NB, L], F32R)
        y_t = sb("f_y", [P, L])
        z_ps = [ctx.enter_context(nc.psum_tensor(f"f_z{i}", [P, L], F32)) for i in range(4)]
        h_ps = [ctx.enter_context(nc.psum_tensor(f"f_h{i}", [P, L], F32)) for i in range(4)]

        seg_in = [sem(f"r_seg_in{u}") for u in range(2)]
        seg_done = sem("r_seg_done")
        w_out = [sem(f"r_w_out{u}") for u in range(2)]
        laying = sem("r_laying")
        r_laid = sem("r_laid")
        old_laid = [sem(f"r_old_laid{g}") for g in range(G)]
        m1 = [sem(f"r_m1_{g}") for g in range(G)]
        w_ok = [sem(f"r_w_{g}") for g in range(G)]
        m2 = [sem(f"r_m2_{g}") for g in range(G)]
        g_ok = [sem(f"r_g_{g}") for g in range(G)]
        ready = sem("f_ready")

        x_in = sem("f_x_in")
        xh_ok, xl_ok = sem("f_xh"), sem("f_xl")
        z1_mm, z2_mm = sem("f_z1_mm"), sem("f_z2_mm")
        a_ok = sem("f_a_ok")
        gate_ok = sem("f_gate")
        gh_ok, gl_ok = sem("f_gh_ok"), sem("f_gl_ok")
        h1_mm, h2_mm, y_mm = sem("f_h1_mm"), sem("f_h2_mm"), sem("f_y_mm")
        hh_ok, hl_ok = sem("f_hh_ok"), sem("f_hl_ok")
        eh_ok, el_ok = sem("f_eh_ok"), sem("f_el_ok")
        y_ok = sem("f_y_ok")
        y_out = sem("f_y_out")

        def over_groups(name):
            return scr[name].rearrange("(g b) (h k) t -> (b h) g k t", g=G, h=H)

        with nc.Block() as block:
            @block.sync
            def _(sp):
                def load(seg, u):
                    sp.wait_ge(seg_done, seg + 1)
                    for tile, name in ((seg_p, "P"), (seg_k, "K"), (seg_r, "R")):
                        for g in range(G):
                            sp.dma_start(tile[u][:, g, :, :], over_groups(name)[:, g, :, bass.ds(seg * SEG, SEG)]
                                         ).then_inc(seg_in[u], 16)

                def store(seg, u):
                    sp.wait_ge(seg_done, seg + 3)
                    for g in range(G):
                        sp.dma_start(over_groups("W")[:, g, :, bass.ds(seg * SEG, SEG)], seg_w[u][:, g, :, :]
                                     ).then_inc(w_out[u], 16)

                load(0, 0)
                load(1, 1)
                with sp.Fori(0, NSEG // 2 - 1) as it:
                    for u in range(2):
                        store(it * 2 + u, u)
                        load(it * 2 + (u + 2), u)
                for u in range(2):
                    store(NSEG - 2 + u, u)
                for u in range(2):
                    sp.wait_ge(w_out[u], 16 * G * (NSEG // 2) + 16 * G)

            @block.vector
            def _(dve):
                for u in range(2):
                    dve.sem_inc(w_out[u], 16 * G)
                dve.sem_inc(seg_done, 2)
                for g in range(G):
                    dve.sem_inc(w_ok[g], 2)
                    dve.memset(state[g][:, :, :], 0.0).then_inc(g_ok[g], 1)
                with dve.Fori(0, NSEG // 2) as it:
                    for u in range(2):
                        dve.wait_ge(seg_in[u], it * (48 * G) + 48 * G)
                        dve.wait_ge(w_out[u], it * (16 * G) + 16 * G)
                        for b in range(BSEG):
                            blk = it * (2 * BSEG) + (u * BSEG + b)
                            t = slice(b * BLK, b * BLK + BLK)
                            par = b % 2
                            for g in range(G):
                                dve.wait_ge(g_ok[g], blk + 1)
                                dve.tensor_tensor(pg[:, par, g, :, :, 0:DH],
                                                  state[g][:, :, :].unsqueeze(1).to_broadcast([P, BLK, DH, DH]),
                                                  seg_p[u][:, g, :, t].rearrange("p k i -> p i k").unsqueeze(2)
                                                  .to_broadcast([P, BLK, DH, DH]),
                                                  ALU.mult).then_inc(m1[g], 1)
                            dve.wait_ge(r_laid, blk + 1)
                            for g in range(G):
                                dve.wait_ge(m1[g], blk + 1)
                                dve.tensor_reduce(seg_w[u][:, g, :, t].rearrange("p v i -> p i v"),
                                                  pg[:, par, g, :, :, :], AX.X, ALU.add).then_inc(w_ok[g], 1)
                            for g in range(G):
                                dve.wait_ge(w_ok[g], blk + 3)
                                dve.tensor_tensor(kw[g][:, :, 0:BLK].rearrange("p (v k) i -> p v k i", k=DH),
                                                  seg_w[u][:, g, :, t].unsqueeze(2).to_broadcast([P, DH, DH, BLK]),
                                                  seg_k[u][:, g, :, t].unsqueeze(1).to_broadcast([P, DH, DH, BLK]),
                                                  ALU.mult).then_inc(m2[g], 1)
                            for g in range(G):
                                dve.wait_ge(m2[g], blk + 1)
                                dve.wait_ge(old_laid[g], blk + 1)
                                last = dve.tensor_reduce(state[g][:, :, :].rearrange("p v k -> p (v k)"),
                                                         kw[g][:, :, :], AX.X, ALU.add)
                                last.then_inc(g_ok[g], 1)
                            q, at = b // BPS, b % BPS
                            slot = it * (2 * SPS) + (u * SPS + q)
                            for j in {0: (0, 1), 2: (2, 3)}.get(at, ()):
                                dve.wait_ge(z2_mm, slot * NB + (j + 1))
                                dve.wait_ge(a_ok, slot * NB + (j + 1))
                                dve.scalar_tensor_tensor(out=g_f[:, j, :], in0=z_ps[2 * (j % 2) + 1][:, :],
                                                         scalar=c.s2[:, j:j + 1], in1=a_f[:, j, :],
                                                         op0=ALU.mult, op1=ALU.mult).then_inc(gate_ok, 1)
                        for g in range(G):
                            dve.wait_ge(g_ok[g], it * (2 * BSEG) + ((u + 1) * BSEG + 1))
                        dve.sem_inc(seg_done, 1)

            @block.gpsimd
            def _(pool):
                def rest(full, upper, lower, done):
                    pool.tensor_tensor(lower, full, upper.bitcast(F32), ALU.subtract).then_inc(done, 1)

                def lay_r(blk, u, b):
                    for g in range(G):
                        pool.wait_ge(w_ok[g], blk + 1)
                    pool.sem_inc(laying, 1)
                    pool.tensor_copy(pg[:, b % 2, :, :, :, DH].rearrange("p g i v -> p g v i"),
                                     seg_r[u][:, :, :, b * BLK:b * BLK + BLK]).then_inc(r_laid, 1)

                def gate_rest(slot, j):
                    pool.wait_ge(gh_ok, slot * NB + (j + 1))
                    rest(g_f[:, j, :], g_h[:, j, :], g_l[:, j, :], gl_ok)

                def hidden1_rest(slot, o):
                    pool.wait_ge(hh_ok, slot * NB + (o + NB + 1))
                    rest(h_f[:, o, :], h_h[:, o, :], h_l[:, o, :], hl_ok)

                def hidden2_rest(slot, o):
                    pool.wait_ge(eh_ok, slot * NB + (o + 1))
                    rest(e_f[:, o, :], e_h[:, o, :], e_l[:, o, :], el_ok)

                def input_rest(slot):
                    pool.wait_ge(xh_ok, slot + 1)
                    rest(x_f[:, :], x_h[:, :], x_l[:, :], xl_ok)

                pool.memset(h_h[:, :, :].bitcast(F32), 0.0)
                pool.memset(h_l[:, :, :].bitcast(F32), 0.0).then_inc(ready, 1)
                input_rest(0)
                with pool.Fori(0, NSEG // 2) as it:
                    for u in range(2):
                        pool.wait_ge(seg_in[u], it * (48 * G) + 48 * G)
                        for q in range(SPS):
                            slot = it * (2 * SPS) + (u * SPS + q)
                            for at in range(BPS):
                                b = q * BPS + at
                                lay_r(it * (2 * BSEG) + (u * BSEG + b), u, b)
                                if at == 2:
                                    gate_rest(slot, 0)
                                    gate_rest(slot, 1)
                                if at == 3:
                                    gate_rest(slot, 2)
                                    gate_rest(slot, 3)
                                if at == 4:
                                    hidden2_rest(slot, 0)
                                    hidden2_rest(slot, 1)
                                if at == 5:
                                    hidden2_rest(slot, 2)
                                    hidden2_rest(slot, 3)
                                if at == 6:
                                    hidden1_rest(slot, 0)
                                    hidden1_rest(slot, 1)
                                if at == 7:
                                    hidden1_rest(slot, 2)
                                    input_rest(slot + 1)
                                    hidden1_rest(slot, 3)
                for o in range(NB):
                    hidden2_rest(SLOTS, o)

            @block.scalar
            def _(act):
                def load_x(slot):
                    act.dma_start(x_f[:, :], scr["xnT"][bass.ds(slot, 1), :, :].rearrange("b p t -> p (b t)")).then_inc(x_in, 16)

                def input_upper(slot):
                    act.wait_ge(x_in, slot * 16 + 16)
                    act.activation(x_h[:, :], x_f[:, :], ACT.Copy).then_inc(xh_ok, 1)

                def silu(slot, j):
                    act.wait_ge(z1_mm, slot * NB + (j + 1))
                    act.activation(a_f[:, j, :], z_ps[2 * (j % 2)][:, :], ACT.Silu, scale=c.s1[:, j:j + 1]).then_inc(a_ok, 1)

                def gate_upper(slot, j):
                    act.wait_ge(gate_ok, slot * NB + (j + 1))
                    act.activation(g_h[:, j, :], g_f[:, j, :], ACT.Copy).then_inc(gh_ok, 1)

                def gelu(src, scale, full, upper, done):
                    act.activation(full, src, ACT.Gelu, scale=scale)
                    act.activation(upper, src, ACT.Gelu, scale=scale).then_inc(done, 1)

                def hidden1(slot, o):
                    act.wait_ge(h1_mm, slot * NB + (o + 1))
                    gelu(h_ps[o][:, :], c.t1[:, o:o + 1], h_f[:, o, :], h_h[:, o, :], hh_ok)

                def hidden2(slot, o):
                    act.wait_ge(h2_mm, slot * NB + (o + 1))
                    gelu(h_ps[o][:, :], c.t2[:, o:o + 1], e_f[:, o, :], e_h[:, o, :], eh_ok)

                def result(slot):
                    act.wait_ge(y_mm, slot + 1)
                    act.wait_ge(y_out, slot * 16 + 16)
                    act.activation(y_t[:, :], z_ps[3][:, :], ACT.Identity, scale=c.s3[:, :], bias=c.ob[:, :]).then_inc(y_ok, 1)

                def store_y(slot):
                    act.wait_ge(y_ok, slot + 2)
                    act.dma_start(scr["ffnT"][bass.ds(slot, 1), :, :].rearrange("b p t -> p (b t)"), y_t[:, :]).then_inc(y_out, 16)

                act.sem_inc(y_out, 16)
                act.sem_inc(y_ok, 1)
                act.sem_inc(hh_ok, NB)
                load_x(0)
                input_upper(0)
                with act.Fori(0, SLOTS) as slot:
                    for at in range(BPS):
                        for g in range(G):
                            act.wait_ge(g_ok[g], slot * BPS + (at + 1))
                            act.activation(kw[g][:, :, BLK], state[g][:, :, :].rearrange("p v k -> p (v k)"),
                                           ACT.Copy, scale=c.lam4[:, :]).then_inc(old_laid[g], 1)
                        if at == 0:
                            silu(slot, 0)
                            silu(slot, 1)
                        if at == 1:
                            act.wait_ge(xl_ok, slot + 1)
                            load_x(slot + 1)
                            gate_upper(slot, 0)
                            gate_upper(slot, 1)
                        if at == 2:
                            silu(slot, 2)
                            silu(slot, 3)
                        if at == 3:
                            gate_upper(slot, 2)
                            gate_upper(slot, 3)
                            hidden2(slot, 0)
                        if at == 4:
                            hidden2(slot, 1)
                            hidden2(slot, 2)
                        if at == 5:
                            hidden2(slot, 3)
                            hidden1(slot, 0)
                        if at == 6:
                            hidden1(slot, 1)
                            hidden1(slot, 2)
                            act.wait_ge(z2_mm, slot * NB + NB)
                            input_upper(slot + 1)
                        if at == 7:
                            hidden1(slot, 3)
                            result(slot)
                            store_y(slot)
                for o in range(NB):
                    hidden2(SLOTS, o)
                result(SLOTS)
                store_y(SLOTS)
                act.wait_ge(y_out, 16 * SLOTS + 32)

            @block.tensor
            def _(pe):
                general = pe.value_load(c.flag[0:1, 0:1], min_val=0, max_val=1)

                def product(bank, weights, upper, lower, done):
                    n = len(weights)
                    for k in range(n):
                        nc.tensor.matmul(bank, c.w_hi[:, weights[k], :], upper[k], start=k == 0, stop=False)
                        if k < n - 1:
                            nc.tensor.matmul(bank, c.w_hi[:, weights[k], :], lower[k], start=False, stop=False)
                    with pe.If(general > 0):
                        for k in range(n):
                            nc.tensor.matmul(bank, c.w_lo[:, weights[k], :], upper[k], start=False, stop=False)
                            nc.tensor.matmul(bank, c.w_lo[:, weights[k], :], lower[k], start=False, stop=False)
                    nc.tensor.matmul(bank, c.w_hi[:, weights[n - 1], :], lower[n - 1], start=False, stop=True).then_inc(done, 1)

                def gates(slot, j):
                    if j == 0:
                        pe.wait_ge(xh_ok, slot + 1)
                        pe.wait_ge(xl_ok, slot + 1)
                        pe.wait_ge(y_ok, slot + 1)
                    if j >= 2:
                        pe.wait_ge(gate_ok, slot * NB + (j - 1))
                    product(z_ps[2 * (j % 2)][:, :], [W1 + j], [x_h[:, :]], [x_l[:, :]], z1_mm)
                    product(z_ps[2 * (j % 2) + 1][:, :], [W2 + j], [x_h[:, :]], [x_l[:, :]], z2_mm)

                parts = lambda t: [t[:, k, :] for k in range(NB)]

                def second(slot, o):
                    if o == 0:
                        pe.wait_ge(hh_ok, slot * NB + NB)
                        pe.wait_ge(hl_ok, slot * NB + NB)
                    product(h_ps[o][:, :], [H2 + NB * k + o for k in range(NB)], parts(h_h), parts(h_l), h2_mm)

                def first(slot, o):
                    if o == 0:
                        pe.wait_ge(gh_ok, slot * NB + NB)
                        pe.wait_ge(gl_ok, slot * NB + NB)
                    pe.wait_ge(eh_ok, slot * NB + (o + 1))
                    product(h_ps[o][:, :], [H1 + NB * k + o for k in range(NB)], parts(g_h), parts(g_l), h1_mm)

                def output(slot):
                    pe.wait_ge(eh_ok, slot * NB + NB)
                    pe.wait_ge(el_ok, slot * NB + NB)
                    product(z_ps[3][:, :], [W3 + k for k in range(NB)], parts(e_h), parts(e_l), y_mm)

                pe.sem_inc(hl_ok, NB)
                pe.wait_ge(ready, 1)
                with pe.Fori(0, SLOTS) as slot:
                    gates(slot, 0)
                    gates(slot, 1)
                    second(slot, 0)
                    second(slot, 1)
                    gates(slot, 2)
                    gates(slot, 3)
                    second(slot, 2)
                    second(slot, 3)
                    for o in range(NB):
                        first(slot, o)
                    output(slot)
                for o in range(NB):
                    second(SLOTS, o)
                output(SLOTS)


class Sequence:

    def __init__(self, turn, off):
        self.turn, self.off, self.slot = turn, off, off % 2

    def count(self, each, more):
        if self.turn is None:
            return self.off * each + more
        return self.turn * (2 * each) + (self.off * each + more)

    def loads(self):
        if self.turn is None:
            return 64 * (self.off // 2 + 1)
        return self.turn * 64 + 64 * (self.off // 2 + 1)

    def row(self, more=0):
        return bass.ds(self.count(1, more), 1)


def second_layer(nc, io, scr, c, out):
    ctx = ExitStack()
    HW = DH * DH * H // 2
    HEADS = H // 2
    with ctx:
        def sb(name, shape):
            return ctx.enter_context(nc.sbuf_tensor("l1_" + name, shape, F32))

        def pb(name):
            return ctx.enter_context(nc.psum_tensor("l1_" + name, [P, NT, P], F32))

        def sem(name):
            return ctx.enter_context(nc.semaphore("l1_" + name))

        def two(name, shape):
            return [sb(name + "0", shape), sb(name + "1", shape)]

        tile = [P, NT, P]
        x_in, f_in = two("x_in", tile), two("f_in", [P, L])
        w_in, fac_in = two("w_in", [P, L]), two("fac_in", [P, L])
        y_t = sb("y_t", [P, L])
        stats = sb("stats", [P, NT, 6])
        mv1, mv2 = sb("mv1", [P, NT, 2]), sb("mv2", [P, NT, 2])
        sd1, sd2 = sb("sd1", [P, NT]), sb("sd2", [P, NT])
        rs1, rs2 = sb("rs1", [P, NT]), sb("rs2", [P, NT])
        yn, yw, xf, x1, xn = sb("yn", tile), sb("yw", tile), sb("xf", tile), sb("x1", tile), sb("xn", tile)
        x1b = two("x1b", tile)
        xnT = two("xnT", tile)
        qkv = two("qkv", [P, NT, 3 * P])
        qd = two("qd", tile)
        qdT = two("qdT", tile)
        kv = two("kv", [P, 2, HW])
        qs = two("qs", [P, 2 * HW])
        o_in = sb("o_in", tile)
        past = sb("past", [P, NT - 1, P])
        oT = sb("oT", tile)
        res = sb("res", tile)

        ps_y, ps_x, ps_q, ps_o, ps_m, ps_kv = pb("ps_y"), pb("ps_x"), pb("ps_q"), pb("ps_o"), pb("ps_m"), pb("ps_kv")
        ps_s = ctx.enter_context(nc.psum_tensor("l1_ps_s", [P, 2, HW], F32))

        in_ok = [sem("in_ok0"), sem("in_ok1")]
        y_ok, y_tr, f_tr = sem("y_ok"), sem("y_tr"), sem("f_tr")
        stat, aggregating, st1, st2 = sem("stat"), sem("aggregating"), sem("st1"), sem("st2")
        sd1_ok, sd2_ok, rs1_ok, rs2_ok = sem("sd1_ok"), sem("sd2_ok"), sem("rs1_ok"), sem("rs2_ok")
        yn_ok, yw_ok, xf_ok, x1_ok, x1b_ok = sem("yn_ok"), sem("yw_ok"), sem("xf_ok"), sem("x1_ok"), sem("x1b_ok")
        xn_ok, x_tr, xT_ok = sem("xn_ok"), sem("x_tr"), sem("xT_ok")
        qkv_mm, qkv_ok, qd_ok, q_tr, qT_ok = sem("qkv_mm"), sem("qkv_ok"), sem("qd_ok"), sem("q_tr"), sem("qT_ok")
        kv_ok, tri_mm, qs_ok, o_ok = sem("kv_ok"), sem("tri_mm"), sem("qs_ok"), sem("o_ok")
        past_mm, past_ok, o_mm, oT_ok = sem("past_mm"), sem("past_ok"), sem("o_mm"), sem("oT_ok")
        out_mm, res_ok, stored = sem("out_mm"), sem("res_ok"), sem("stored")

        def walk(engine, front, step, back):
            front(Sequence(None, 0))
            with engine.Fori(0, B // 2 - 1) as turn:
                for off in range(2):
                    step(Sequence(turn, off), Sequence(turn, off + 1))
            step(Sequence(None, B - 2), Sequence(None, B - 1))
            back(Sequence(None, B - 1))

        with nc.Block() as block:
            @block.sync
            def _(sp):
                def load(m):
                    by_token = io["L0_attn_x"][m.row(), :, :].rearrange("b (t p) d -> p (b t) d", p=P)
                    sp.dma_start(w_in[m.slot][:, :], scr["W"][m.row(), :, :].rearrange("b p t -> p (b t)")).then_inc(in_ok[m.slot], 16)
                    sp.dma_start(fac_in[m.slot][:, :], scr["fac"][m.row(), :, :].rearrange("b p t -> p (b t)")).then_inc(in_ok[m.slot], 16)
                    sp.dma_start(f_in[m.slot][:, :], scr["ffnT"][m.row(1), :, :].rearrange("b p t -> p (b t)")).then_inc(in_ok[m.slot], 16)
                    sp.dma_start(x_in[m.slot][:, :, :], by_token).then_inc(in_ok[m.slot], 16)

                def store(n):
                    sp.wait_ge(res_ok, n.count(1, 1))
                    sp.dma_start(out[n.row(), :, :].rearrange("b (t p) d -> p (b t) d", p=P), res[:, :, :]).then_inc(stored, 16)

                sp.sem_inc(stored, 16)
                load(Sequence(None, 0))
                load(Sequence(None, 1))
                with sp.Fori(0, B // 2 - 1) as turn:
                    for off in range(2):
                        n, ahead = Sequence(turn, off), Sequence(turn, off + 2)
                        sp.wait_ge(xf_ok, n.count(1, 1))
                        load(ahead)
                        store(n)
                store(Sequence(None, B - 2))
                store(Sequence(None, B - 1))
                sp.wait_ge(stored, 16 * B + 16)

            @block.gpsimd
            def _(pool):
                def outputs(m):
                    pool.wait_ge(in_ok[m.slot], m.loads())
                    pool.wait_ge(y_tr, m.count(1, 1))
                    pool.tensor_tensor(y_t[:, :], w_in[m.slot][:, :], fac_in[m.slot][:, :], ALU.mult).then_inc(y_ok, 1)

                def residual(m):
                    pool.wait_ge(yn_ok, m.count(1, 2))
                    pool.tensor_tensor(yw[:, :, :], yn[:, :, :], c.ow[:, :].unsqueeze(1).to_broadcast(tile), ALU.mult).then_inc(yw_ok, 1)
                    pool.wait_ge(yw_ok, m.count(1, 2))
                    pool.wait_ge(xf_ok, m.count(1, 1))
                    pool.tensor_tensor(x1[:, :, :], yw[:, :, :], xf[:, :, :], ALU.add).then_inc(x1_ok, 1)

                def with_bias(m):
                    pool.wait_ge(x1_ok, m.count(1, 1))
                    pool.tensor_tensor(x1b[m.slot][:, :, :], x1[:, :, :], c.bo[:, :].unsqueeze(1).to_broadcast(tile), ALU.add).then_inc(x1b_ok, 1)

                def decayed(m):
                    for t in range(NT):
                        pool.wait_ge(qkv_ok, m.count(NT, t + 2))
                        ins = pool.tensor_tensor(qd[m.slot][:, t, :], qkv[m.slot][:, t, 0:P], c.dec[:, t, :], ALU.mult)
                    ins.then_inc(qd_ok, 1)

                def outer(n, t):
                    pool.wait_ge(qkv_ok, n.count(NT, t + 2))
                    pool.wait_ge(tri_mm, n.count(NT, t + 1))
                    k = qkv[n.slot][:, t, P:2 * P].rearrange("p (h k) -> p h k", h=H).unsqueeze(3).to_broadcast([P, H, DH, DH])
                    v = qkv[n.slot][:, t, 2 * P:3 * P].rearrange("p (h v) -> p h v", h=H).unsqueeze(2).to_broadcast([P, H, DH, DH])
                    dst = kv[t % 2][:, :, :].rearrange("p a (h k v) -> p (a h) k v", h=HEADS, k=DH)
                    pool.tensor_tensor(dst, k, v, ALU.mult).then_inc(kv_ok, 1)

                def front(m):
                    outputs(m)
                    residual(m)
                    with_bias(m)
                    decayed(m)
                    outer(m, 0)
                    outer(m, 1)

                def step(n, m):
                    outputs(m)
                    outer(n, 2)
                    residual(m)
                    outer(n, 3)
                    with_bias(m)
                    decayed(m)
                    outer(m, 0)
                    outer(m, 1)

                def back(n):
                    outer(n, 2)
                    outer(n, 3)

                pool.sem_inc(yw_ok, 1)
                walk(pool, front, step, back)

            @block.scalar
            def _(act):
                def root1(m):
                    act.wait_ge(st1, m.count(1, 1))
                    act.activation(sd1[:, :], mv1[:, :, 1], ACT.Sqrt, bias=c.eps_ln[:, :]).then_inc(sd1_ok, 1)

                def root2(m):
                    act.wait_ge(st2, m.count(1, 1))
                    act.activation(sd2[:, :], mv2[:, :, 1], ACT.Sqrt, bias=c.eps_ln[:, :]).then_inc(sd2_ok, 1)

                def normed(m):
                    act.wait_ge(x_tr, m.count(1, 1))
                    act.wait_ge(out_mm, m.count(1, 1))
                    act.activation(xnT[m.slot][:, :, :], ps_x[:, :, :], ACT.Copy).then_inc(xT_ok, 1)

                def attended(n):
                    act.wait_ge(o_mm, n.count(1, 2))
                    act.wait_ge(out_mm, n.count(1, 2))
                    act.activation(oT[:, :, :], ps_o[:, :, :], ACT.Copy).then_inc(oT_ok, 1)

                def queries(m):
                    act.wait_ge(q_tr, m.count(1, 1))
                    act.activation(qdT[m.slot][:, :, :], ps_m[:, :, :], ACT.Copy).then_inc(qT_ok, 1)

                def front(m):
                    root1(m)
                    root2(m)
                    normed(m)
                    queries(m)

                def step(n, m):
                    root1(m)
                    root2(m)
                    normed(m)
                    attended(n)
                    queries(m)

                act.sem_inc(xT_ok, 1)
                act.sem_inc(oT_ok, 1)
                walk(act, front, step, attended)

            @block.vector
            def _(dve):
                def statistics(m, src, mv, done, links):
                    for t in range(NT):
                        ins = dve.bn_stats(out=stats[:, t, :], in_=src[:, t, :])
                    ins.then_inc(stat, 1)
                    dve.wait_ge(stat, m.count(2, links))
                    dve.sem_inc(aggregating, 1)
                    for t in range(NT):
                        ins = dve.bn_aggr(out=mv[:, t, :], in_=stats[:, t:t + 1, :])
                    ins.then_inc(done, 1)

                def stats1(m):
                    dve.wait_ge(y_tr, m.count(1, 2))
                    statistics(m, ps_y, mv1, st1, 1)

                def norm1(m):
                    dve.wait_ge(sd1_ok, m.count(1, 1))
                    dve.reciprocal(rs1[:, :], sd1[:, :]).then_inc(rs1_ok, 1)
                    dve.wait_ge(in_ok[m.slot], m.loads())
                    dve.wait_ge(f_tr, m.count(1, 1))
                    dve.tensor_tensor(xf[:, :, :], x_in[m.slot][:, :, :], ps_x[:, :, :], ALU.add).then_inc(xf_ok, 1)
                    dve.wait_ge(rs1_ok, m.count(1, 1))
                    dve.wait_ge(yw_ok, m.count(1, 1))
                    for t in range(NT):
                        ins = dve.tensor_scalar(yn[:, t, :], ps_y[:, t, :], mv1[:, t, 0:1], rs1[:, t:t + 1], ALU.subtract, ALU.mult)
                    ins.then_inc(yn_ok, 1)

                def stats2(m):
                    dve.wait_ge(x1_ok, m.count(1, 1))
                    statistics(m, x1, mv2, st2, 2)

                def norm2(m):
                    dve.wait_ge(sd2_ok, m.count(1, 1))
                    dve.reciprocal(rs2[:, :], sd2[:, :]).then_inc(rs2_ok, 1)
                    dve.wait_ge(rs2_ok, m.count(1, 1))
                    for t in range(NT):
                        ins = dve.tensor_scalar(xn[:, t, :], x1[:, t, :], mv2[:, t, 0:1], rs2[:, t:t + 1], ALU.subtract, ALU.mult)
                    ins.then_inc(xn_ok, 1)

                def project(m):
                    for t in range(NT):
                        dve.wait_ge(qkv_mm, m.count(NT, t + 1))
                        dve.tensor_tensor(qkv[m.slot][:, t, :], ps_q[:, 0:3, :].rearrange("p a b -> p (a b)"), c.bqkv[:, :], ALU.add).then_inc(qkv_ok, 1)

                def scores(n, t):
                    dve.wait_ge(qd_ok, n.count(1, 1))
                    dve.wait_ge(tri_mm, n.count(NT, t + 3))
                    q = qd[n.slot][:, t, :].rearrange("p (h k) -> p h k", h=H).unsqueeze(3).to_broadcast([P, H, DH, DH])
                    dve.tensor_tensor(qs[t % 2][:, :].rearrange("p (h k v) -> p h k v", h=H, k=DH),
                                      ps_s[:, :, :].rearrange("p a (h k v) -> p (a h) k v", h=HEADS, k=DH), q, ALU.mult).then_inc(qs_ok, 1)
                    dve.wait_ge(qs_ok, n.count(NT, t + 2))
                    dve.wait_ge(o_mm, n.count(1, 1))
                    dve.tensor_reduce(out=o_in[:, t, :].rearrange("p (h v) -> p h v", h=H),
                                      in_=qs[t % 2][:, :].rearrange("p (h k v) -> p h v k", h=H, k=DH), axis=AX.X, op=ALU.add).then_inc(o_ok, 1)

                def state(n, t):
                    dve.wait_ge(past_mm, n.count(NT - 1, t + 1))
                    dve.tensor_tensor(past[:, t, :], ps_kv[:, 0, :], c.head_ones[:, :], ALU.mult).then_inc(past_ok, 1)

                def result(n):
                    dve.wait_ge(out_mm, n.count(1, 3))
                    dve.wait_ge(x1b_ok, n.count(1, 1))
                    dve.wait_ge(stored, n.count(16, 16))
                    dve.tensor_tensor(res[:, :, :], ps_m[:, :, :], x1b[n.slot][:, :, :], ALU.add).then_inc(res_ok, 1)

                def front(m):
                    stats1(m)
                    norm1(m)
                    stats2(m)
                    norm2(m)
                    project(m)

                def step(n, m):
                    scores(n, 0)
                    state(n, 0)
                    stats1(m)
                    scores(n, 1)
                    state(n, 1)
                    norm1(m)
                    scores(n, 2)
                    state(n, 2)
                    stats2(m)
                    scores(n, 3)
                    norm2(m)
                    project(m)
                    result(n)

                def back(n):
                    for t in range(NT):
                        scores(n, t)
                        if t < NT - 1:
                            state(n, t)
                    result(n)

                dve.sem_inc(yn_ok, 1)
                dve.sem_inc(qkv_ok, 1)
                dve.sem_inc(qs_ok, 1)
                dve.sem_inc(past_ok, 1)
                walk(dve, front, step, back)

            @block.tensor
            def _(pe):
                def outputs(m):
                    pe.wait_ge(y_ok, m.count(1, 1))
                    pe.wait_ge(yn_ok, m.count(1, 1))
                    for t in range(NT):
                        ins = nc.tensor.transpose(ps_y[:, t, :], y_t[:, t * P:(t + 1) * P], c.ident[:, :])
                    ins.then_inc(y_tr, 1)
                    pe.wait_ge(in_ok[m.slot], m.loads())
                    pe.wait_ge(xT_ok, m.count(1, 1))
                    for t in range(NT):
                        ins = nc.tensor.transpose(ps_x[:, t, :], f_in[m.slot][:, t * P:(t + 1) * P], c.ident[:, :])
                    ins.then_inc(f_tr, 1)

                def normed(m):
                    pe.wait_ge(xn_ok, m.count(1, 1))
                    pe.wait_ge(xf_ok, m.count(1, 1))
                    for t in range(NT):
                        ins = nc.tensor.transpose(ps_x[:, t, :], xn[:, t, :], c.ident[:, :])
                    ins.then_inc(x_tr, 1)

                def project(m):
                    pe.wait_ge(xT_ok, m.count(1, 2))
                    for t in range(NT):
                        pe.wait_ge(qkv_ok, m.count(NT, t + 1))
                        nc.tensor.matmul(ps_q[:, 0:3, :].rearrange("p a b -> p (a b)"), xnT[m.slot][:, t, :], c.wqkv_t[:, :],
                                         start=True, stop=True).then_inc(qkv_mm, 1)

                def queries(m, first=False):
                    pe.wait_ge(qd_ok, m.count(1, 1))
                    if not first:
                        pe.wait_ge(res_ok, m.count(1, 0))
                    for t in range(NT):
                        ins = nc.tensor.transpose(ps_m[:, t, :], qd[m.slot][:, t, :], c.ident[:, :])
                    ins.then_inc(q_tr, 1)

                def running(n, t):
                    pe.wait_ge(kv_ok, n.count(NT, t + 1))
                    pe.wait_ge(qs_ok, n.count(NT, t + 1))
                    nc.tensor.matmul(ps_s[:, 0, :], c.tri[:, :], kv[t % 2][:, 0, :], start=True, stop=True)
                    nc.tensor.matmul(ps_s[:, 1, :], c.tri[:, :], kv[t % 2][:, 1, :], start=True, stop=True).then_inc(tri_mm, 1)

                def state(n, t):
                    pe.wait_ge(past_ok, n.count(NT - 1, t + 1))
                    pe.wait_ge(qkv_ok, n.count(NT, t + 2))
                    nc.tensor.matmul(ps_kv[:, 0, :], qkv[n.slot][:, t, P:2 * P], qkv[n.slot][:, t, 2 * P:3 * P],
                                     start=t == 0, stop=True, skip_group_check=True).then_inc(past_mm, 1)

                def attended(n):
                    pe.wait_ge(qT_ok, n.count(1, 1))
                    pe.wait_ge(past_ok, n.count(NT - 1, NT))
                    pe.wait_ge(oT_ok, n.count(1, 1))
                    for t in range(NT):
                        pe.wait_ge(o_ok, n.count(NT, t + 1))
                        if t > 0:
                            nc.tensor.matmul(ps_o[:, t, :], past[:, t - 1, :], qdT[n.slot][:, t, :], start=True, stop=False)
                        ins = nc.tensor.matmul(ps_o[:, t, :], o_in[:, t, :], c.ident[:, :], start=t == 0, stop=True)
                    ins.then_inc(o_mm, 1)

                def final(n):
                    pe.wait_ge(oT_ok, n.count(1, 2))
                    for t in range(NT):
                        nc.tensor.matmul(ps_m[:, t, :], oT[:, t, :], c.wo_t[:, :], start=True, stop=False)
                        ins = nc.tensor.matmul(ps_m[:, t, :], xnT[n.slot][:, t, :], c.weff_t[:, :], start=False, stop=True)
                    ins.then_inc(out_mm, 1)

                def front(m):
                    outputs(m)
                    normed(m)
                    project(m)
                    queries(m, first=True)

                def step(n, m):
                    running(n, 0)
                    state(n, 0)
                    running(n, 1)
                    outputs(m)
                    state(n, 1)
                    running(n, 2)
                    state(n, 2)
                    running(n, 3)
                    normed(m)
                    attended(n)
                    project(m)
                    final(n)
                    queries(m)

                def back(n):
                    for t in range(NT):
                        running(n, t)
                        if t < NT - 1:
                            state(n, t)
                    attended(n)
                    final(n)

                pe.sem_inc(y_tr, 1)
                pe.sem_inc(tri_mm, 2)
                pe.sem_inc(o_mm, 1)
                pe.sem_inc(out_mm, 2)
                walk(pe, front, step, back)


_INS = ("L0_attn_x", "L0_attn_W", "L0_attn_k_norm_w", "L0_attn_o_norm_w", "L0_attn_o_norm_b", "L0_attn_eta_raw",
        "L0_attn_lam_logit", "L0_ffn_w1_w", "L0_ffn_w1_s", "L0_ffn_w2_w", "L0_ffn_w2_s", "L0_ffn_h1_w", "L0_ffn_h1_s",
        "L0_ffn_h2_w", "L0_ffn_h2_s", "L0_ffn_w3_w", "L0_ffn_w3_s", "L1_attn_Wq", "L1_attn_bq", "L1_attn_Wk",
        "L1_attn_bk", "L1_attn_Wv", "L1_attn_bv", "L1_attn_Wo", "L1_attn_bo", "L1_attn_gamma", "L1_ffn_W", "L1_ffn_b",
        "L1_ffn_V_r", "L1_ffn_C")


def kernel(**inputs):
    import numpy as _np
    import concourse.bacc as _bacc
    from concourse import mybir as _mybir
    from concourse.bass_utils import run_bass_kernel_spmd as _run

    nc = _bacc.Bacc("TRN2", target_bir_lowering=False, num_devices=1)
    arrays, io = {}, {}
    for name in _INS:
        a = _np.ascontiguousarray(inputs[name])
        arrays[f"in_{name}_dram"] = a
        io[name] = nc.dram_tensor(f"in_{name}_dram", a.shape, _mybir.dt.from_np(a.dtype), kind="ExternalInput").ap()
    out = nc.dram_tensor("out_0_dram", (B, L, D), F32, kind="ExternalOutput").ap()
    build(nc, io, out)
    r = _run(nc, [arrays], core_ids=[0])
    return r.results[0]["out_0_dram"]
```

```python
import concourse.bass as bass
from concourse import mybir
from contextlib import ExitStack

F32 = mybir.dt.float32
F32R = mybir.dt.float32r
I32 = mybir.dt.int32
ALU = mybir.AluOpType
ACT = mybir.ActivationFunctionType
AX = mybir.AxisListType

B, L, D = 16, 512, 128
H, DH = 16, 8
HID = 512
P = 128
NT = L // P
NB = HID // P
RANK = 32
G = B * H // P
BG = B // G
BLK = 4
PAIRS = BLK * (BLK - 1) // 2
SEG = 64
LN_EPS = 1e-5
F32_EPS = 1.1920928955078125e-07

W1, W2, H1, H2, W3 = 0, NB, 2 * NB, 2 * NB + NB * NB, 2 * NB + 2 * NB * NB
NW = W3 + NB


def build(nc, io, out):
    scr = {}
    for name in ("xnT", "P", "K", "R", "fac", "W", "ffnT"):
        rows = B + 1 if name in ("xnT", "ffnT") else B
        scr[name] = nc.dram_tensor("scratch_" + name, [rows, P, L], F32).ap()
    with ExitStack() as ctx:
        c = constants(nc, ctx)
        setup(nc, io, c)
        prepare(nc, io, scr, c)
        recur_and_feed_forward(nc, io, scr, c)
        second_layer(nc, io, scr, c, out)


class Tiles:
    pass


def constants(nc, ctx):
    c = Tiles()

    def sb(name, shape, dt=F32):
        return ctx.enter_context(nc.sbuf_tensor(name, shape, dt))

    c.ident = sb("ident", [P, P])
    c.head_ones = sb("head_ones", [P, P])
    c.tri = sb("tri", [P, P])
    c.w_hi = sb("w_hi", [P, NW, P], F32R)
    c.w_lo = sb("w_lo", [P, NW, P], F32R)
    c.ws_t = sb("ws_t", [P, P])
    c.w_second = sb("w_second", [P, 4 * P])
    c.wo_t = sb("wo_t", [P, P])
    c.s1 = sb("s1", [P, NB])
    c.s2 = sb("s2", [P, NB])
    c.t1 = sb("t1", [P, NB])
    c.t2 = sb("t2", [P, NB])
    c.s3 = sb("s3", [P, 1])
    c.knw = sb("knw", [P, 1])
    c.gate = sb("gate", [P, 1])
    c.pfac = sb("pfac", [P, BLK])
    c.kfac = sb("kfac", [P, BLK])
    c.lam4 = sb("lam4", [P, 1])
    c.dec = sb("dec", [P, NT, P])
    c.b_second = sb("b_second", [P, 4 * P])
    c.ow = sb("ow", [P, P])
    c.ob = sb("ob", [P, 1])
    c.eps_ln = sb("eps_ln", [P, 1])
    c.eps_rms = sb("eps_rms", [P, 1])
    c.flag = sb("flag", [1, 1], I32)
    return c


def setup(nc, io, c):
    ctx = ExitStack()
    with ctx:
        def sb(name, shape, dt=F32):
            return ctx.enter_context(nc.sbuf_tensor(name, shape, dt))

        def sem(name):
            return ctx.enter_context(nc.semaphore(name))

        nat12 = sb("nat12", [P, 2, NB, P])
        nath = sb("nath", [P, 2, NB, HID])
        nat3 = sb("nat3", [P, HID])
        nats = sb("nats", [P, 6, P])
        natr = sb("natr", [P, 2, RANK])
        vr_t = sb("vr_t", [RANK, 2, P])
        par = sb("par", [P, 4])
        work = sb("work", [P, 16])
        dec_t = sb("dec_t", [P, L])
        ones = sb("ones", [P, L])
        bf = sb("bf", [P, P])
        peaks = sb("peaks", [P, NW // NB])
        peak = sb("peak", [P, 1])
        ftmp = sb("ftmp", [1, 2])
        ps = [ctx.enter_context(nc.psum_tensor(f"ps_set{i}", [P, 4, P], F32)) for i in range(2)]
        ps_s = ctx.enter_context(nc.psum_tensor("ps_small", [P, 4, P], F32))
        ps_d = ctx.enter_context(nc.psum_tensor("ps_dec", [P, 4, P], F32))

        loaded = sem("s_loaded")
        const_done = sem("s_const")
        pool_chain = sem("s_pool_chain")
        tr_done = sem("s_tr")
        hi_done = sem("s_hi")
        lo_done = sem("s_lo")
        small_tr = sem("s_small_tr")
        small_cp = sem("s_small_cp")
        vec = sem("s_vec")
        exps = sem("s_exps")
        peak_done = sem("s_peak")
        peak_tr = sem("s_peak_tr")
        dec_ready = sem("s_dec_ready")
        dec_tr = sem("s_dec_tr")
        weff = sem("s_weff")

        groups = [[nat12[:, 0, j, :] for j in range(NB)], [nat12[:, 1, j, :] for j in range(NB)]]
        for w in range(2):
            groups += [[nath[:, w, o, i * P:(i + 1) * P] for o in range(NB)] for i in range(NB)]
        groups += [[nat3[:, i * P:(i + 1) * P] for i in range(NB)]]
        NG = len(groups)

        loads = []

        def add(dst, src):
            loads.append((dst, src))

        add(nat12[:, 0, :, :], io["L0_ffn_w1_w"].rearrange("(o p) i -> p o i", p=P))
        add(nat12[:, 1, :, :], io["L0_ffn_w2_w"].rearrange("(o p) i -> p o i", p=P))
        add(nath[:, 0, :, :], io["L0_ffn_h1_w"].rearrange("(o p) i -> p o i", p=P))
        add(nath[:, 1, :, :], io["L0_ffn_h2_w"].rearrange("(o p) i -> p o i", p=P))
        add(nat3[:, :], io["L0_ffn_w3_w"])
        for n, name in enumerate(("L0_attn_W", "L1_attn_Wq", "L1_attn_Wk", "L1_attn_Wv", "L1_attn_Wo", "L1_ffn_W")):
            add(nats[:, n, :], io[name])
        add(natr[:, 0, :], io["L1_ffn_V_r"])
        add(natr[:, 1, :], io["L1_ffn_C"])
        for dst, name in ((c.s1, "L0_ffn_w1_s"), (c.s2, "L0_ffn_w2_s"), (c.t1, "L0_ffn_h1_s"), (c.t2, "L0_ffn_h2_s")):
            add(dst[:, :], io[name].rearrange("(o p) -> p o", p=P))
        add(c.s3[:, :], io["L0_ffn_w3_s"].rearrange("(p o) -> p o", o=1))
        for n, name in enumerate(("L1_attn_bq", "L1_attn_bk", "L1_attn_bv")):
            add(c.b_second[:, n * P:(n + 1) * P], io[name].partition_broadcast(P))
        add(c.b_second[:, 3 * P:4 * P], io["L1_attn_bo"].partition_broadcast(P))
        add(bf[:, :], io["L1_ffn_b"].partition_broadcast(P))
        add(c.ow[:, :], io["L0_attn_o_norm_w"].partition_broadcast(P))
        add(c.ob[:, :], io["L0_attn_o_norm_b"].rearrange("(p o) -> p o", o=1))
        by_head = lambda name: io[name].rearrange("(h o) -> h o", o=1)
        for d in range(DH):
            for n, name in enumerate(("L0_attn_lam_logit", "L0_attn_eta_raw", "L1_attn_gamma")):
                add(par[d:P:DH, n:n + 1], by_head(name))
            add(par[d * H:(d + 1) * H, 3:4], by_head("L0_attn_lam_logit"))
        for h in range(H):
            add(c.knw[h * DH:(h + 1) * DH, 0:1], io["L0_attn_k_norm_w"].rearrange("(d o) -> d o", o=1))
        NL = 16 * len(loads)

        with nc.allow_non_contiguous_dma(reason='a few hundred words of scales and per-head factors'), nc.Block() as block:
            @block.sync
            def _(sp):
                for dst, src in loads[0::2]:
                    sp.dma_start(dst, src).then_inc(loaded, 16)

            @block.gpsimd
            def _(pool):
                pool.memset(c.ident[:, :], 0.0).then_inc(pool_chain, 1)
                pool.memset(c.head_ones[:, :], 1.0).then_inc(pool_chain, 1)
                pool.memset(c.tri[:, :], 1.0).then_inc(pool_chain, 1)
                pool.memset(c.eps_ln[:, :], LN_EPS)
                pool.memset(c.eps_rms[:, :], F32_EPS).then_inc(pool_chain, 1)
                pool.wait_ge(pool_chain, 4)
                pool.affine_select(out=c.ident[:, :], in_=c.ident[:, :], compare_op=ALU.not_equal, fill=1.0,
                                   base=0, pattern=[[-1, P]], channel_multiplier=1).then_inc(const_done, 1)
                pool.affine_select(out=c.tri[:, :], in_=c.tri[:, :], compare_op=ALU.is_ge, fill=0.0,
                                   base=0, pattern=[[1, P]], channel_multiplier=-1).then_inc(const_done, 1)
                heads = c.head_ones[:, :].rearrange("p (h k) -> p h k", k=DH)
                pool.affine_select(out=heads, in_=heads, compare_op=ALU.is_ge, fill=0.0,
                                   base=0, pattern=[[-DH, H], [0, DH]], channel_multiplier=1).then_inc(pool_chain, 1)
                pool.wait_ge(pool_chain, 5)
                pool.affine_select(out=heads, in_=heads, compare_op=ALU.is_ge, fill=0.0,
                                   base=DH - 1, pattern=[[DH, H], [0, DH]], channel_multiplier=-1).then_inc(const_done, 1)

            @block.tensor
            def _(pe):
                pe.wait_ge(const_done, 1)
                pe.wait_ge(loaded, NL)
                for g, blocks in enumerate(groups):
                    if g >= 2:
                        pe.wait_ge(lo_done, g - 1)
                    for n, b in enumerate(blocks):
                        last = nc.tensor.transpose(ps[g % 2][:, n, :], b, c.ident[:, :])
                    last.then_inc(tr_done, 1)
                for n in range(4):
                    last = nc.tensor.transpose(ps_s[:, n, :], nats[:, n, :], c.ident[:, :])
                last.then_inc(small_tr, 1)
                pe.wait_ge(small_cp, 2)
                nc.tensor.transpose(ps_s[:, 0, :], nats[:, 4, :], c.ident[:, :])
                nc.tensor.transpose(ps_s[0:RANK, 1, :], natr[:, 0, :], c.ident[:, :])
                nc.tensor.transpose(ps_s[0:RANK, 2, :], natr[:, 1, :], c.ident[:, :]).then_inc(small_tr, 1)
                pe.wait_ge(small_cp, 4)
                nc.tensor.matmul(ps_s[:, 3, :], nats[:, 5, :], c.ident[:, :], start=True, stop=False)
                nc.tensor.matmul(ps_s[:, 3, :], vr_t[:, 0, :], vr_t[:, 1, :], start=False, stop=True).then_inc(weff, 1)
                pe.wait_ge(dec_ready, 1)
                for n in range(NT):
                    last = nc.tensor.transpose(ps_d[:, n, :], dec_t[:, n * P:(n + 1) * P], c.ident[:, :])
                last.then_inc(dec_tr, 1)
                pe.wait_ge(peak_done, 1)
                pe.wait_ge(lo_done, NG)
                nc.tensor.transpose(ps[0][0:1, 0, :], peak[:, :], c.ident[:, :]).then_inc(peak_tr, 1)

            @block.scalar
            def _(act):
                for dst, src in loads[1::2]:
                    act.dma_start(dst, src).then_inc(loaded, 16)
                act.wait_ge(loaded, NL)
                act.activation(work[:, 0:1], par[:, 0:1], ACT.Exp, scale=-1.0)
                act.activation(work[:, 1:2], par[:, 1:2], ACT.Tanh)
                act.activation(work[:, 2:3], par[:, 3:4], ACT.Exp, scale=-1.0).then_inc(exps, 1)
                for g in range(NG):
                    act.wait_ge(tr_done, g + 1)
                    act.activation(c.w_hi[:, NB * g:NB * g + NB, :], ps[g % 2][:, :, :], ACT.Copy).then_inc(hi_done, 1)
                act.wait_ge(small_tr, 1)
                act.activation(c.ws_t[:, :], ps_s[:, 0, :], ACT.Copy).then_inc(small_cp, 1)
                act.activation(c.w_second[:, 0:3 * P].rearrange("p (n k) -> p n k", n=3), ps_s[:, 1:4, :], ACT.Copy).then_inc(small_cp, 1)
                act.wait_ge(small_tr, 2)
                act.activation(c.wo_t[:, :], ps_s[:, 0, :], ACT.Copy).then_inc(small_cp, 1)
                act.activation(vr_t[:, :, :], ps_s[0:RANK, 1:3, :], ACT.Copy).then_inc(small_cp, 1)
                act.wait_ge(weff, 1)
                act.activation(c.w_second[:, 3 * P:4 * P], ps_s[:, 3, :], ACT.Copy)
                act.wait_ge(dec_tr, 1)
                act.activation(c.dec[:, :, :], ps_d[:, :, :], ACT.Copy)

            @block.vector
            def _(dve):
                chain = [0]

                def link(ins):
                    chain[0] += 1
                    ins.then_inc(vec, 1)
                    dve.wait_ge(vec, chain[0])

                dve.memset(ones[:, :], 1.0)
                link(dve.memset(dec_t[:, 0:1], 1.0))
                dve.wait_ge(exps, 1)
                link(dve.tensor_scalar_add(work[:, 5:6], work[:, 0:1], 1.0))
                link(dve.tensor_scalar_add(work[:, 6:7], work[:, 2:3], 1.0))
                link(dve.reciprocal(work[:, 3:4], work[:, 5:6]))
                link(dve.reciprocal(work[:, 4:5], work[:, 6:7]))
                link(dve.tensor_scalar(work[:, 7:8], work[:, 3:4], -1.0, 1.0, ALU.mult, ALU.add))
                link(dve.tensor_tensor(work[:, 8:9], work[:, 7:8], work[:, 1:2], ALU.mult))
                link(dve.tensor_scalar(c.gate[:, :], work[:, 8:9], 1.0 / DH, None, ALU.mult))
                link(dve.memset(c.kfac[:, 3:4], 1.0))
                link(dve.tensor_scalar(c.pfac[:, 0:1], c.gate[:, :], work[:, 3:4], None, ALU.mult))
                for i in range(1, BLK):
                    link(dve.tensor_scalar(c.pfac[:, i:i + 1], c.pfac[:, i - 1:i], work[:, 3:4], None, ALU.mult))
                    link(dve.tensor_scalar(c.kfac[:, 3 - i:4 - i], c.kfac[:, 4 - i:5 - i], work[:, 3:4], None, ALU.mult))
                link(dve.tensor_tensor(work[:, 9:10], work[:, 4:5], work[:, 4:5], ALU.mult))
                link(dve.tensor_tensor(c.lam4[:, :], work[:, 9:10], work[:, 9:10], ALU.mult))
                dve.tensor_tensor_scan(dec_t[:, 1:L], par[:, 2:3].to_broadcast([P, L - 1]), ones[:, 0:L - 1], 1.0,
                                       ALU.mult, ALU.mult).then_inc(dec_ready, 1)
                link(dve.tensor_tensor(c.b_second[:, 3 * P:4 * P], c.b_second[:, 3 * P:4 * P], bf[:, :], ALU.add))
                for g in range(NG):
                    dve.wait_ge(hi_done, g + 1)
                    lo = c.w_lo[:, NB * g:NB * g + NB, :]
                    ins = dve.tensor_tensor(lo, ps[g % 2][:, :, :], c.w_hi[:, NB * g:NB * g + NB, :].bitcast(F32), ALU.subtract)
                    ins.then_inc(lo_done, 1)
                    dve.wait_ge(lo_done, g + 1)
                    link(dve.tensor_reduce(peaks[:, g:g + 1], lo.bitcast(F32), AX.XY, ALU.max, apply_absolute_value=True))
                dve.tensor_reduce(peak[:, :], peaks[:, :], AX.X, ALU.max).then_inc(peak_done, 1)
                dve.wait_ge(peak_tr, 1)
                link(dve.tensor_reduce(ftmp[:, 0:1], ps[0][0:1, 0, :], AX.X, ALU.max))
                link(dve.tensor_scalar(ftmp[:, 1:2], ftmp[:, 0:1], 0.0, None, ALU.is_gt))
                dve.tensor_copy(c.flag[:, :], ftmp[:, 1:2])


def prepare(nc, io, scr, c):
    ctx = ExitStack()
    with ctx:
        def sb(name, shape, dt=F32):
            return ctx.enter_context(nc.sbuf_tensor(name, shape, dt))

        def sem(name):
            return ctx.enter_context(nc.semaphore(name))

        x_in = sb("p_x", [P, 2, NT, P])
        stats = sb("p_stats", [P, NT, 6])
        mv = sb("p_mv", [P, NT, 2])
        std = sb("p_std", [P, NT])
        rstd = sb("p_rstd", [P, NT])
        xn = sb("p_xn", [P, NT, P])
        xnT = sb("p_xnT", [P, L])
        sq = sb("p_sq", [P, L])
        rms = sb("p_rms", [P, L])
        rrms = sb("p_rrms", [P, L])
        kT = sb("p_kT", [P, L])
        k2 = sb("p_k2", [P, L])
        fac = sb("p_fac", [P, L])
        kout = sb("p_kout", [P, L])
        prod = sb("p_prod", [P, PAIRS, L // BLK])
        coup = sb("p_coup", [P, PAIRS, L // BLK])
        rp = sb("p_rp", [P, 2, L])
        tmp_r = sb("p_tmp_r", [P, 3, L // BLK])
        tmp_p = sb("p_tmp_p", [P, 3, L // BLK])
        ps_x = ctx.enter_context(nc.psum_tensor("p_ps_x", [P, L], F32))
        ps_s = ctx.enter_context(nc.psum_tensor("p_ps_s", [P, L], F32))
        ps_q = ctx.enter_context(nc.psum_tensor("p_ps_q", [P, L], F32))
        ps_k = ctx.enter_context(nc.psum_tensor("p_ps_k", [P, L], F32))
        ps_n = ctx.enter_context(nc.psum_tensor("p_ps_n", [P, 8, L // BLK], F32))

        x_ready = [sem(f"p_x_ready{u}") for u in range(2)]
        x_free = sem("p_x_free")
        stat = sem("p_stat")
        aggregating = sem("p_aggregating")
        std_ok = sem("p_std")
        xn_ok = sem("p_xn")
        x_tr = sem("p_x_tr")
        xT_ok = sem("p_xT")
        sq_ok = sem("p_sq")
        s_mm = sem("p_s_mm")
        q_mm = sem("p_q_mm")
        rms_ok = sem("p_rms")
        rr_ok = sem("p_rr")
        k_ok = sem("p_k")
        k2_ok = sem("p_k2")
        k_mm = sem("p_k_mm")
        fac_ok = sem("p_fac")
        prod_ok = sem("p_prod")
        n_mm = sem("p_n_mm")
        coup_ok = sem("p_coup")
        coup_free = sem("p_coup_free")
        r_in = sem("p_r_in")
        p_in = sem("p_p_in")
        kout_ok = sem("p_kout")
        r_step = sem("p_r_step")
        p_step = sem("p_p_step")
        st_x = sem("p_st_x")
        st_f = sem("p_st_f")
        st_k = sem("p_st_k")
        st_r = sem("p_st_r")
        st_p = sem("p_st_p")

        def by_pos(ap):
            return ap.rearrange("p (b i) -> p i b", i=BLK)

        def later(i0, ap):
            return by_pos(ap)[:, i0:BLK, :]

        def bcast(ap, n):
            return ap.to_broadcast([P, n, L // BLK])

        first = [0, 3, 5]

        def sweep(eng, ap, tmp, step, it):
            at = 0
            for j in range(BLK - 1):
                n = BLK - 1 - j
                if at:
                    eng.wait_ge(step, it * 6 + at)
                eng.tensor_tensor(tmp[:, 0:n, :], coup[:, first[j]:first[j] + n, :],
                                  bcast(by_pos(ap)[:, j:j + 1, :], n), ALU.mult).then_inc(step, 1)
                at += 1
                eng.wait_ge(step, it * 6 + at)
                last = eng.tensor_tensor(later(j + 1, ap), later(j + 1, ap), tmp[:, 0:n, :], ALU.add)
                last.then_inc(step, 1)
                at += 1

        with nc.Block() as block:
            @block.sync
            def _(sp):
                def load(n, u):
                    sp.wait_ge(x_free, n + 1)
                    sp.dma_start(x_in[:, u, :, :],
                                 io["L0_attn_x"][bass.ds(n, 1), :, :].rearrange("b (t p) d -> p (b t) d", p=P)
                                 ).then_inc(x_ready[u], 16)

                def store(n, again=False):
                    def put(name, tile, done):
                        sp.dma_start(scr[name][bass.ds(n, 1), :, :].rearrange("b p t -> p (b t)"), tile).then_inc(done, 16)
                    sp.wait_ge(xT_ok, n + 1)
                    put("xnT", xnT[:, :], st_x)
                    if again:
                        sp.dma_start(scr["xnT"][B, :, :], xnT[:, :]).then_inc(st_x, 16)
                    sp.wait_ge(kout_ok, n + 1)
                    put("K", kout[:, :], st_k)
                    sp.wait_ge(fac_ok, n + 1)
                    put("fac", fac[:, :], st_f)
                    sp.wait_ge(r_step, n * 6 + 6)
                    put("R", rp[:, 1, :], st_r)
                    sp.wait_ge(p_step, n * 6 + 6)
                    put("P", rp[:, 0, :], st_p)

                load(0, 0)
                with sp.Fori(0, B // 2 - 1) as half:
                    for u in range(2):
                        load(half * 2 + (u + 1), 1 - u)
                        store(half * 2 + u)
                load(B - 1, 1)
                store(B - 2)
                store(B - 1, again=True)
                for done in (st_x, st_k, st_f, st_r, st_p):
                    sp.wait_ge(done, 16 * B + (32 if done is st_x else 16))

            @block.gpsimd
            def _(pool):
                pool.sem_inc(coup_free, 1)
                pool.sem_inc(st_k, 16)
                pool.sem_inc(st_p, 16)
                with pool.Fori(0, B) as it:
                    pool.wait_ge(k_ok, it + 1)
                    pool.wait_ge(st_p, it * 16 + 16)
                    pool.tensor_tensor(by_pos(rp[:, 0, :]), by_pos(kT[:, :]),
                                       c.pfac[:, :].unsqueeze(2).to_broadcast([P, BLK, L // BLK]),
                                       ALU.mult).then_inc(p_in, 1)
                    pool.wait_ge(st_k, it * 16 + 16)
                    pool.tensor_tensor(by_pos(kout[:, :]), by_pos(kT[:, :]),
                                       c.kfac[:, :].unsqueeze(2).to_broadcast([P, BLK, L // BLK]),
                                       ALU.mult).then_inc(kout_ok, 1)
                    pool.wait_ge(coup_ok, it * 6 + 6)
                    pool.wait_ge(p_in, it + 1)
                    sweep(pool, rp[:, 0, :], tmp_p, p_step, it)
                    pool.wait_ge(p_step, it * 6 + 6)
                    pool.sem_inc(coup_free, 1)

            @block.scalar
            def _(act):
                act.sem_inc(st_x, 16)
                act.sem_inc(st_f, 16)
                act.sem_inc(st_r, 16)
                with act.Fori(0, B) as it:
                    act.wait_ge(stat, it * 2 + 2)
                    act.activation(std[:, :], mv[:, :, 1], ACT.Sqrt, bias=c.eps_ln[:, :]).then_inc(std_ok, 1)
                    act.wait_ge(x_tr, it + 1)
                    act.wait_ge(st_x, it * 16 + 16)
                    act.activation(xnT[:, :], ps_x[:, :], ACT.Copy).then_inc(xT_ok, 1)
                    act.activation(sq[:, :], ps_x[:, :], ACT.Square).then_inc(sq_ok, 1)
                    act.wait_ge(q_mm, it + 1)
                    act.activation(rms[:, :], ps_q[:, :], ACT.Sqrt, bias=c.eps_rms[:, :], scale=1.0 / DH).then_inc(rms_ok, 1)
                    act.wait_ge(s_mm, it + 1)
                    act.wait_ge(st_r, it * 16 + 16)
                    act.activation(rp[:, 1, :], ps_s[:, :], ACT.Copy).then_inc(r_in, 1)
                    act.wait_ge(k_ok, it + 1)
                    act.activation(k2[:, :], kT[:, :], ACT.Square).then_inc(k2_ok, 1)
                    act.wait_ge(n_mm, it + 1)
                    act.wait_ge(coup_free, it + 1)
                    at = 0
                    for j in range(BLK - 1):
                        for i in range(j + 1, BLK):
                            act.activation(coup[:, at, :], ps_n[:, at, :], ACT.Copy,
                                           scale=c.pfac[:, i - j - 1:i - j]).then_inc(coup_ok, 1)
                            at += 1
                    act.wait_ge(k_mm, it + 1)
                    act.wait_ge(st_f, it * 16 + 16)
                    act.activation(fac[:, :], ps_k[:, :], ACT.Identity, scale=c.gate[:, :], bias=1.0).then_inc(fac_ok, 1)

            @block.vector
            def _(dve):
                dve.sem_inc(x_free, 2)
                with dve.Fori(0, B // 2) as half:
                    for u in range(2):
                        it = half * 2 + u
                        dve.wait_ge(x_ready[u], half * 16 + 16)
                        for t in range(NT):
                            last = dve.bn_stats(stats[:, t, :], x_in[:, u, t, :])
                        last.then_inc(stat, 1)
                        dve.wait_ge(stat, it * 2 + 1)
                        dve.sem_inc(aggregating, 1)
                        for t in range(NT):
                            last = dve.bn_aggr(mv[:, t, :], stats[:, t, :])
                        last.then_inc(stat, 1)
                        dve.wait_ge(std_ok, it + 1)
                        dve.reciprocal(rstd[:, :], std[:, :]).then_inc(rr_ok, 1)
                        dve.wait_ge(rr_ok, it * 2 + 1)
                        for t in range(NT):
                            last = dve.tensor_scalar(xn[:, t, :], x_in[:, u, t, :], mv[:, t, 0:1], rstd[:, t:t + 1],
                                                     ALU.subtract, ALU.mult)
                        last.then_inc(xn_ok, 1)
                        dve.wait_ge(xn_ok, it + 1)
                        dve.sem_inc(x_free, 1)
                        dve.wait_ge(rms_ok, it + 1)
                        dve.reciprocal(rrms[:, :], rms[:, :]).then_inc(rr_ok, 1)
                        dve.wait_ge(rr_ok, it * 2 + 2)
                        dve.wait_ge(xT_ok, it + 1)
                        dve.scalar_tensor_tensor(out=kT[:, :], in0=xnT[:, :], scalar=c.knw[:, :], in1=rrms[:, :],
                                                 op0=ALU.mult, op1=ALU.mult).then_inc(k_ok, 1)
                        dve.wait_ge(k_ok, it + 1)
                        for j in range(BLK - 1):
                            n = BLK - 1 - j
                            last = dve.tensor_tensor(prod[:, first[j]:first[j] + n, :], later(j + 1, kT[:, :]),
                                                     bcast(by_pos(kT[:, :])[:, j:j + 1, :], n), ALU.mult)
                        last.then_inc(prod_ok, 1)
                        dve.wait_ge(coup_ok, it * 6 + 6)
                        dve.wait_ge(r_in, it + 1)
                        sweep(dve, rp[:, 1, :], tmp_r, r_step, it)
                        dve.wait_ge(kout_ok, it + 1)
                        dve.wait_ge(k2_ok, it + 1)

            @block.tensor
            def _(pe):
                with pe.Fori(0, B) as it:
                    pe.wait_ge(xn_ok, it + 1)
                    for t in range(NT):
                        last = nc.tensor.transpose(ps_x[:, t * P:(t + 1) * P], xn[:, t, :], c.ident[:, :])
                    last.then_inc(x_tr, 1)
                    pe.wait_ge(sq_ok, it + 1)
                    nc.tensor.matmul(ps_q[:, :], c.head_ones[:, :], sq[:, :], start=True, stop=True).then_inc(q_mm, 1)
                    pe.wait_ge(xT_ok, it + 1)
                    nc.tensor.matmul(ps_s[:, :], c.ws_t[:, :], xnT[:, :], start=True, stop=True).then_inc(s_mm, 1)
                    pe.wait_ge(prod_ok, it + 1)
                    nc.tensor.matmul(ps_n[:, 0:4, :], c.head_ones[:, :], prod[:, 0:4, :], start=True, stop=True)
                    nc.tensor.matmul(ps_n[:, 4:6, :], c.head_ones[:, :], prod[:, 4:6, :], start=True, stop=True).then_inc(n_mm, 1)
                    pe.wait_ge(k2_ok, it + 1)
                    nc.tensor.matmul(ps_k[:, :], c.head_ones[:, :], k2[:, :], start=True, stop=True).then_inc(k_mm, 1)


def recur_and_feed_forward(nc, io, scr, c):
    ctx = ExitStack()
    SLOTS = B
    BPS = L // BLK // SLOTS
    BSEG = SEG // BLK
    SPS = BSEG // BPS
    NSEG = L // SEG
    with ctx:
        def sb(name, shape, dt=F32):
            return ctx.enter_context(nc.sbuf_tensor(name, shape, dt))

        def sem(name):
            return ctx.enter_context(nc.semaphore(name))

        seg_p = [sb(f"r_p{u}", [P, G, DH, SEG]) for u in range(2)]
        seg_k = [sb(f"r_k{u}", [P, G, DH, SEG]) for u in range(2)]
        seg_r = [sb(f"r_r{u}", [P, G, DH, SEG]) for u in range(2)]
        seg_w = [sb(f"r_w{u}", [P, G, DH, SEG]) for u in range(2)]
        state = [sb(f"r_g{g}", [P, DH, DH]) for g in range(G)]
        pg = sb("r_pg", [P, 2, G, BLK, DH, DH + 1])
        kw = [sb(f"r_kw{g}", [P, DH * DH, BLK + 1]) for g in range(G)]

        x_f = sb("f_x", [P, L])
        x_h, x_l = sb("f_xh", [P, L], F32R), sb("f_xl", [P, L], F32R)
        a_f = sb("f_a", [P, NB, L])
        g_f = sb("f_g", [P, NB, L])
        g_h, g_l = sb("f_gh", [P, NB, L], F32R), sb("f_gl", [P, NB, L], F32R)
        h_f = sb("f_h", [P, NB, L])
        h_h, h_l = sb("f_hh", [P, NB, L], F32R), sb("f_hl", [P, NB, L], F32R)
        e_f = sb("f_e", [P, NB, L])
        e_h, e_l = sb("f_eh", [P, NB, L], F32R), sb("f_el", [P, NB, L], F32R)
        y_t = sb("f_y", [P, L])
        z_ps = [ctx.enter_context(nc.psum_tensor(f"f_z{i}", [P, L], F32)) for i in range(4)]
        h_ps = [ctx.enter_context(nc.psum_tensor(f"f_h{i}", [P, L], F32)) for i in range(4)]

        seg_in = [sem(f"r_seg_in{u}") for u in range(2)]
        seg_done = sem("r_seg_done")
        w_out = [sem(f"r_w_out{u}") for u in range(2)]
        laying = sem("r_laying")
        r_laid = sem("r_laid")
        old_laid = [sem(f"r_old_laid{g}") for g in range(G)]
        m1 = [sem(f"r_m1_{g}") for g in range(G)]
        w_ok = [sem(f"r_w_{g}") for g in range(G)]
        m2 = [sem(f"r_m2_{g}") for g in range(G)]
        g_ok = [sem(f"r_g_{g}") for g in range(G)]
        ready = sem("f_ready")

        x_in = sem("f_x_in")
        xh_ok, xl_ok = sem("f_xh"), sem("f_xl")
        z1_mm, z2_mm = sem("f_z1_mm"), sem("f_z2_mm")
        a_ok = sem("f_a_ok")
        gate_ok = sem("f_gate")
        gh_ok, gl_ok = sem("f_gh_ok"), sem("f_gl_ok")
        h1_mm, h2_mm, y_mm = sem("f_h1_mm"), sem("f_h2_mm"), sem("f_y_mm")
        hh_ok, hl_ok = sem("f_hh_ok"), sem("f_hl_ok")
        eh_ok, el_ok = sem("f_eh_ok"), sem("f_el_ok")
        y_ok = sem("f_y_ok")
        y_out = sem("f_y_out")

        def over_groups(name):
            return scr[name].rearrange("(g b) (h k) t -> (b h) g k t", g=G, h=H)

        with nc.Block() as block:
            @block.sync
            def _(sp):
                def load(seg, u):
                    sp.wait_ge(seg_done, seg + 1)
                    for tile, name in ((seg_p, "P"), (seg_k, "K"), (seg_r, "R")):
                        for g in range(G):
                            sp.dma_start(tile[u][:, g, :, :], over_groups(name)[:, g, :, bass.ds(seg * SEG, SEG)]
                                         ).then_inc(seg_in[u], 16)

                def store(seg, u):
                    sp.wait_ge(seg_done, seg + 3)
                    for g in range(G):
                        sp.dma_start(over_groups("W")[:, g, :, bass.ds(seg * SEG, SEG)], seg_w[u][:, g, :, :]
                                     ).then_inc(w_out[u], 16)

                load(0, 0)
                load(1, 1)
                with sp.Fori(0, NSEG // 2 - 1) as it:
                    for u in range(2):
                        store(it * 2 + u, u)
                        load(it * 2 + (u + 2), u)
                for u in range(2):
                    store(NSEG - 2 + u, u)
                for u in range(2):
                    sp.wait_ge(w_out[u], 16 * G * (NSEG // 2) + 16 * G)

            @block.vector
            def _(dve):
                for u in range(2):
                    dve.sem_inc(w_out[u], 16 * G)
                dve.sem_inc(seg_done, 2)
                for g in range(G):
                    dve.sem_inc(w_ok[g], 2)
                    dve.memset(state[g][:, :, :], 0.0).then_inc(g_ok[g], 1)
                with dve.Fori(0, NSEG // 2) as it:
                    for u in range(2):
                        dve.wait_ge(seg_in[u], it * (48 * G) + 48 * G)
                        dve.wait_ge(w_out[u], it * (16 * G) + 16 * G)
                        for b in range(BSEG):
                            blk = it * (2 * BSEG) + (u * BSEG + b)
                            t = slice(b * BLK, b * BLK + BLK)
                            par = b % 2
                            for g in range(G):
                                dve.wait_ge(g_ok[g], blk + 1)
                                dve.tensor_tensor(pg[:, par, g, :, :, 0:DH],
                                                  state[g][:, :, :].unsqueeze(1).to_broadcast([P, BLK, DH, DH]),
                                                  seg_p[u][:, g, :, t].rearrange("p k i -> p i k").unsqueeze(2)
                                                  .to_broadcast([P, BLK, DH, DH]),
                                                  ALU.mult).then_inc(m1[g], 1)
                            dve.wait_ge(r_laid, blk + 1)
                            for g in range(G):
                                dve.wait_ge(m1[g], blk + 1)
                                dve.tensor_reduce(seg_w[u][:, g, :, t].rearrange("p v i -> p i v"),
                                                  pg[:, par, g, :, :, :], AX.X, ALU.add).then_inc(w_ok[g], 1)
                            for g in range(G):
                                dve.wait_ge(w_ok[g], blk + 3)
                                dve.tensor_tensor(kw[g][:, :, 0:BLK].rearrange("p (v k) i -> p v k i", k=DH),
                                                  seg_w[u][:, g, :, t].unsqueeze(2).to_broadcast([P, DH, DH, BLK]),
                                                  seg_k[u][:, g, :, t].unsqueeze(1).to_broadcast([P, DH, DH, BLK]),
                                                  ALU.mult).then_inc(m2[g], 1)
                            for g in range(G):
                                dve.wait_ge(m2[g], blk + 1)
                                dve.wait_ge(old_laid[g], blk + 1)
                                last = dve.tensor_reduce(state[g][:, :, :].rearrange("p v k -> p (v k)"),
                                                         kw[g][:, :, :], AX.X, ALU.add)
                                last.then_inc(g_ok[g], 1)
                            q, at = b // BPS, b % BPS
                            slot = it * (2 * SPS) + (u * SPS + q)
                            for j in {0: (0, 1), 2: (2, 3)}.get(at, ()):
                                dve.wait_ge(z2_mm, slot * NB + (j + 1))
                                dve.wait_ge(a_ok, slot * NB + (j + 1))
                                dve.scalar_tensor_tensor(out=g_f[:, j, :], in0=z_ps[2 * (j % 2) + 1][:, :],
                                                         scalar=c.s2[:, j:j + 1], in1=a_f[:, j, :],
                                                         op0=ALU.mult, op1=ALU.mult).then_inc(gate_ok, 1)
                        for g in range(G):
                            dve.wait_ge(g_ok[g], it * (2 * BSEG) + ((u + 1) * BSEG + 1))
                        dve.sem_inc(seg_done, 1)

            @block.gpsimd
            def _(pool):
                def rest(full, upper, lower, done):
                    pool.tensor_tensor(lower, full, upper.bitcast(F32), ALU.subtract).then_inc(done, 1)

                def lay_r(blk, u, b):
                    for g in range(G):
                        pool.wait_ge(w_ok[g], blk + 1)
                    pool.sem_inc(laying, 1)
                    pool.tensor_copy(pg[:, b % 2, :, :, :, DH].rearrange("p g i v -> p g v i"),
                                     seg_r[u][:, :, :, b * BLK:b * BLK + BLK]).then_inc(r_laid, 1)

                def gate_rest(slot, j):
                    pool.wait_ge(gh_ok, slot * NB + (j + 1))
                    rest(g_f[:, j, :], g_h[:, j, :], g_l[:, j, :], gl_ok)

                def hidden1_rest(slot, o):
                    pool.wait_ge(hh_ok, slot * NB + (o + NB + 1))
                    rest(h_f[:, o, :], h_h[:, o, :], h_l[:, o, :], hl_ok)

                def hidden2_rest(slot, o):
                    pool.wait_ge(eh_ok, slot * NB + (o + 1))
                    rest(e_f[:, o, :], e_h[:, o, :], e_l[:, o, :], el_ok)

                def input_rest(slot):
                    pool.wait_ge(xh_ok, slot + 1)
                    rest(x_f[:, :], x_h[:, :], x_l[:, :], xl_ok)

                pool.memset(h_h[:, :, :].bitcast(F32), 0.0)
                pool.memset(h_l[:, :, :].bitcast(F32), 0.0).then_inc(ready, 1)
                input_rest(0)
                with pool.Fori(0, NSEG // 2) as it:
                    for u in range(2):
                        pool.wait_ge(seg_in[u], it * (48 * G) + 48 * G)
                        for q in range(SPS):
                            slot = it * (2 * SPS) + (u * SPS + q)
                            for at in range(BPS):
                                b = q * BPS + at
                                lay_r(it * (2 * BSEG) + (u * BSEG + b), u, b)
                                if at == 2:
                                    gate_rest(slot, 0)
                                    gate_rest(slot, 1)
                                if at == 3:
                                    gate_rest(slot, 2)
                                    gate_rest(slot, 3)
                                if at == 4:
                                    hidden2_rest(slot, 0)
                                    hidden2_rest(slot, 1)
                                if at == 5:
                                    hidden2_rest(slot, 2)
                                    hidden2_rest(slot, 3)
                                if at == 6:
                                    hidden1_rest(slot, 0)
                                    hidden1_rest(slot, 1)
                                if at == 7:
                                    hidden1_rest(slot, 2)
                                    input_rest(slot + 1)
                                    hidden1_rest(slot, 3)
                for o in range(NB):
                    hidden2_rest(SLOTS, o)

            @block.scalar
            def _(act):
                def load_x(slot):
                    act.dma_start(x_f[:, :], scr["xnT"][bass.ds(slot, 1), :, :].rearrange("b p t -> p (b t)")).then_inc(x_in, 16)

                def input_upper(slot):
                    act.wait_ge(x_in, slot * 16 + 16)
                    act.activation(x_h[:, :], x_f[:, :], ACT.Copy).then_inc(xh_ok, 1)

                def silu(slot, j):
                    act.wait_ge(z1_mm, slot * NB + (j + 1))
                    act.activation(a_f[:, j, :], z_ps[2 * (j % 2)][:, :], ACT.Silu, scale=c.s1[:, j:j + 1]).then_inc(a_ok, 1)

                def gate_upper(slot, j):
                    act.wait_ge(gate_ok, slot * NB + (j + 1))
                    act.activation(g_h[:, j, :], g_f[:, j, :], ACT.Copy).then_inc(gh_ok, 1)

                def gelu(src, scale, full, upper, done):
                    act.activation(full, src, ACT.Gelu, scale=scale)
                    act.activation(upper, src, ACT.Gelu, scale=scale).then_inc(done, 1)

                def hidden1(slot, o):
                    act.wait_ge(h1_mm, slot * NB + (o + 1))
                    gelu(h_ps[o][:, :], c.t1[:, o:o + 1], h_f[:, o, :], h_h[:, o, :], hh_ok)

                def hidden2(slot, o):
                    act.wait_ge(h2_mm, slot * NB + (o + 1))
                    gelu(h_ps[o][:, :], c.t2[:, o:o + 1], e_f[:, o, :], e_h[:, o, :], eh_ok)

                def result(slot):
                    act.wait_ge(y_mm, slot + 1)
                    act.wait_ge(y_out, slot * 16 + 16)
                    act.activation(y_t[:, :], z_ps[3][:, :], ACT.Identity, scale=c.s3[:, :], bias=c.ob[:, :]).then_inc(y_ok, 1)

                def store_y(slot):
                    act.wait_ge(y_ok, slot + 2)
                    act.dma_start(scr["ffnT"][bass.ds(slot, 1), :, :].rearrange("b p t -> p (b t)"), y_t[:, :]).then_inc(y_out, 16)

                act.sem_inc(y_out, 16)
                act.sem_inc(y_ok, 1)
                act.sem_inc(hh_ok, NB)
                load_x(0)
                input_upper(0)
                with act.Fori(0, SLOTS) as slot:
                    for at in range(BPS):
                        for g in range(G):
                            act.wait_ge(g_ok[g], slot * BPS + (at + 1))
                            act.activation(kw[g][:, :, BLK], state[g][:, :, :].rearrange("p v k -> p (v k)"),
                                           ACT.Copy, scale=c.lam4[:, :]).then_inc(old_laid[g], 1)
                        if at == 0:
                            silu(slot, 0)
                            silu(slot, 1)
                        if at == 1:
                            act.wait_ge(xl_ok, slot + 1)
                            load_x(slot + 1)
                            gate_upper(slot, 0)
                            gate_upper(slot, 1)
                        if at == 2:
                            silu(slot, 2)
                            silu(slot, 3)
                        if at == 3:
                            gate_upper(slot, 2)
                            gate_upper(slot, 3)
                            hidden2(slot, 0)
                        if at == 4:
                            hidden2(slot, 1)
                            hidden2(slot, 2)
                        if at == 5:
                            hidden2(slot, 3)
                            hidden1(slot, 0)
                        if at == 6:
                            hidden1(slot, 1)
                            hidden1(slot, 2)
                            act.wait_ge(z2_mm, slot * NB + NB)
                            input_upper(slot + 1)
                        if at == 7:
                            hidden1(slot, 3)
                            result(slot)
                            store_y(slot)
                for o in range(NB):
                    hidden2(SLOTS, o)
                result(SLOTS)
                store_y(SLOTS)
                act.wait_ge(y_out, 16 * SLOTS + 32)

            @block.tensor
            def _(pe):
                general = pe.value_load(c.flag[0:1, 0:1], min_val=0, max_val=1)

                def product(bank, weights, upper, lower, done):
                    n = len(weights)
                    for k in range(n):
                        nc.tensor.matmul(bank, c.w_hi[:, weights[k], :], upper[k], start=k == 0, stop=False)
                        if k < n - 1:
                            nc.tensor.matmul(bank, c.w_hi[:, weights[k], :], lower[k], start=False, stop=False)
                    with pe.If(general > 0):
                        for k in range(n):
                            nc.tensor.matmul(bank, c.w_lo[:, weights[k], :], upper[k], start=False, stop=False)
                            nc.tensor.matmul(bank, c.w_lo[:, weights[k], :], lower[k], start=False, stop=False)
                    nc.tensor.matmul(bank, c.w_hi[:, weights[n - 1], :], lower[n - 1], start=False, stop=True).then_inc(done, 1)

                def gates(slot, j):
                    if j == 0:
                        pe.wait_ge(xh_ok, slot + 1)
                        pe.wait_ge(xl_ok, slot + 1)
                        pe.wait_ge(y_ok, slot + 1)
                    if j >= 2:
                        pe.wait_ge(gate_ok, slot * NB + (j - 1))
                    product(z_ps[2 * (j % 2)][:, :], [W1 + j], [x_h[:, :]], [x_l[:, :]], z1_mm)
                    product(z_ps[2 * (j % 2) + 1][:, :], [W2 + j], [x_h[:, :]], [x_l[:, :]], z2_mm)

                parts = lambda t: [t[:, k, :] for k in range(NB)]

                def second(slot, o):
                    if o == 0:
                        pe.wait_ge(hh_ok, slot * NB + NB)
                        pe.wait_ge(hl_ok, slot * NB + NB)
                    product(h_ps[o][:, :], [H2 + NB * k + o for k in range(NB)], parts(h_h), parts(h_l), h2_mm)

                def first(slot, o):
                    if o == 0:
                        pe.wait_ge(gh_ok, slot * NB + NB)
                        pe.wait_ge(gl_ok, slot * NB + NB)
                    pe.wait_ge(eh_ok, slot * NB + (o + 1))
                    product(h_ps[o][:, :], [H1 + NB * k + o for k in range(NB)], parts(g_h), parts(g_l), h1_mm)

                def output(slot):
                    pe.wait_ge(eh_ok, slot * NB + NB)
                    pe.wait_ge(el_ok, slot * NB + NB)
                    product(z_ps[3][:, :], [W3 + k for k in range(NB)], parts(e_h), parts(e_l), y_mm)

                pe.sem_inc(hl_ok, NB)
                pe.wait_ge(ready, 1)
                with pe.Fori(0, SLOTS) as slot:
                    gates(slot, 0)
                    gates(slot, 1)
                    second(slot, 0)
                    second(slot, 1)
                    gates(slot, 2)
                    gates(slot, 3)
                    second(slot, 2)
                    second(slot, 3)
                    for o in range(NB):
                        first(slot, o)
                    output(slot)
                for o in range(NB):
                    second(SLOTS, o)
                output(SLOTS)


class Sequence:

    def __init__(self, turn, off):
        self.turn, self.off, self.slot = turn, off, off % 2

    def count(self, each, more):
        if self.turn is None:
            return self.off * each + more
        return self.turn * (2 * each) + (self.off * each + more)

    def loads(self):
        if self.turn is None:
            return 64 * (self.off // 2 + 1)
        return self.turn * 64 + 64 * (self.off // 2 + 1)

    def row(self, more=0):
        return bass.ds(self.count(1, more), 1)


def second_layer(nc, io, scr, c, out):
    ctx = ExitStack()
    HW = DH * DH * H // 2
    HEADS = H // 2
    with ctx:
        def sb(name, shape):
            return ctx.enter_context(nc.sbuf_tensor("l1_" + name, shape, F32))

        def pb(name):
            return ctx.enter_context(nc.psum_tensor("l1_" + name, [P, NT, P], F32))

        def sem(name):
            return ctx.enter_context(nc.semaphore("l1_" + name))

        def two(name, shape):
            return [sb(name + "0", shape), sb(name + "1", shape)]

        tile = [P, NT, P]
        x_in, f_in = two("x_in", tile), two("f_in", [P, L])
        w_in, fac_in = two("w_in", [P, L]), two("fac_in", [P, L])
        y_t = sb("y_t", [P, L])
        stats = sb("stats", [P, NT, 6])
        mv1, mv2 = sb("mv1", [P, NT, 2]), sb("mv2", [P, NT, 2])
        sd1, sd2 = sb("sd1", [P, NT]), sb("sd2", [P, NT])
        rs1, rs2 = sb("rs1", [P, NT]), sb("rs2", [P, NT])
        nm1, nm2 = sb("nm1", [P, NT]), sb("nm2", [P, NT])
        yn, yw, xf, xn = sb("yn", tile), sb("yw", tile), sb("xf", tile), sb("xn", tile)
        x1 = two("x1", tile)
        x1b = two("x1b", tile)
        xnT = sb("xnT", tile)
        qkv = two("qkv", [P, NT, 4 * P])
        qd = two("qd", tile)
        qdT = two("qdT", tile)
        kv = two("kv", [P, 2, HW])
        qs = two("qs", [P, 2 * HW])
        o_in = two("o_in", tile)
        past = two("past", [P, NT - 1, P])
        oT = sb("oT", tile)
        res = sb("res", tile)

        ps_y, ps_x, ps_q, ps_o, ps_m, ps_kv = pb("ps_y"), pb("ps_x"), pb("ps_q"), pb("ps_o"), pb("ps_m"), pb("ps_kv")
        ps_s = ctx.enter_context(nc.psum_tensor("l1_ps_s", [P, 2, HW], F32))

        in_ok = [sem("in_ok0"), sem("in_ok1")]
        y_ok, y_tr, f_tr = sem("y_ok"), sem("y_tr"), sem("f_tr")
        stat, aggregating, st1, st2 = sem("stat"), sem("aggregating"), sem("st1"), sem("st2")
        sd1_ok, sd2_ok, rs1_ok, rs2_ok, nm1_ok, nm2_ok = (sem("sd1_ok"), sem("sd2_ok"), sem("rs1_ok"), sem("rs2_ok"),
                                                          sem("nm1_ok"), sem("nm2_ok"))
        yn_ok, yw_ok, xf_ok, x1_ok, x1b_ok = sem("yn_ok"), sem("yw_ok"), sem("xf_ok"), sem("x1_ok"), sem("x1b_ok")
        xn_ok, x_tr, xT_ok = sem("xn_ok"), sem("x_tr"), sem("xT_ok")
        qkv_mm, qkv_ok, qd_ok, q_tr, qT_ok = sem("qkv_mm"), sem("qkv_ok"), sem("qd_ok"), sem("q_tr"), sem("qT_ok")
        kv_ok, tri_mm, qs_ok, o_ok = sem("kv_ok"), sem("tri_mm"), sem("qs_ok"), sem("o_ok")
        past_mm, past_ok, o_mm, oT_ok = sem("past_mm"), sem("past_ok"), sem("o_mm"), sem("oT_ok")
        out_mm, res_ok, stored = sem("out_mm"), sem("res_ok"), sem("stored")

        def walk(engine, step):
            def outside(k):
                step(*[Sequence(None, k + d) if 0 <= k + d < B else None for d in (-1, 0, 1, 2)])

            for k in (-2, -1, 0):
                outside(k)
            with engine.Fori(0, B // 2 - 2) as turn:
                for k in (1, 2):
                    step(*[Sequence(turn, k + d) for d in (-1, 0, 1, 2)])
            for k in range(B - 3, B + 1):
                outside(k)

        def at(s, stage, *more):
            if s is not None:
                stage(s, *more)

        with nc.Block() as block:
            @block.sync
            def _(sp):
                def load(l):
                    by_token = io["L0_attn_x"][l.row(), :, :].rearrange("b (t p) d -> p (b t) d", p=P)
                    sp.dma_start(w_in[l.slot][:, :], scr["W"][l.row(), :, :].rearrange("b p t -> p (b t)")).then_inc(in_ok[l.slot], 16)
                    sp.dma_start(fac_in[l.slot][:, :], scr["fac"][l.row(), :, :].rearrange("b p t -> p (b t)")).then_inc(in_ok[l.slot], 16)
                    sp.dma_start(f_in[l.slot][:, :], scr["ffnT"][l.row(1), :, :].rearrange("b p t -> p (b t)")).then_inc(in_ok[l.slot], 16)
                    sp.dma_start(x_in[l.slot][:, :, :], by_token).then_inc(in_ok[l.slot], 16)

                load(Sequence(None, 0))
                load(Sequence(None, 1))
                with sp.Fori(0, B // 2 - 1) as turn:
                    for off in range(2):
                        sp.wait_ge(xf_ok, Sequence(turn, off).count(1, 1))
                        load(Sequence(turn, off + 2))

            @block.gpsimd
            def _(pool):
                def outputs(l):
                    pool.wait_ge(in_ok[l.slot], l.loads())
                    pool.wait_ge(y_tr, l.count(1, 1))
                    pool.tensor_tensor(y_t[:, :], w_in[l.slot][:, :], fac_in[l.slot][:, :], ALU.mult).then_inc(y_ok, 1)

                def weighted(l):
                    pool.wait_ge(yn_ok, l.count(1, 2))
                    pool.tensor_tensor(yw[:, :, :], yn[:, :, :], c.ow[:, :].unsqueeze(1).to_broadcast(tile), ALU.mult).then_inc(yw_ok, 1)

                def residual(l):
                    pool.wait_ge(xf_ok, l.count(1, 1))
                    pool.wait_ge(xn_ok, l.count(1, 1))
                    pool.wait_ge(yw_ok, l.count(1, 2))
                    pool.tensor_tensor(x1[l.slot][:, :, :], yw[:, :, :], xf[:, :, :], ALU.add).then_inc(x1_ok, 1)

                def straight(n):
                    pool.wait_ge(x1_ok, n.count(1, 2))
                    pool.wait_ge(qkv_ok, n.count(NT, NT + 1))
                    pool.wait_ge(res_ok, n.count(1, 1))
                    pool.tensor_tensor(x1b[n.slot][:, :, :], x1[n.slot][:, :, :], qkv[n.slot][:, :, 3 * P:4 * P], ALU.add).then_inc(x1b_ok, 1)

                def decayed(m, t):
                    pool.wait_ge(qkv_ok, m.count(NT, t + 2))
                    pool.tensor_tensor(qd[m.slot][:, t, :], qkv[m.slot][:, t, 0:P], c.dec[:, t, :], ALU.mult).then_inc(qd_ok, 1)

                def outer(n, t):
                    pool.wait_ge(qkv_ok, n.count(NT, t + 2))
                    pool.wait_ge(tri_mm, n.count(NT, t + 1))
                    k = qkv[n.slot][:, t, P:2 * P].rearrange("p (h k) -> p h k", h=H).unsqueeze(3).to_broadcast([P, H, DH, DH])
                    v = qkv[n.slot][:, t, 2 * P:3 * P].rearrange("p (h v) -> p h v", h=H).unsqueeze(2).to_broadcast([P, H, DH, DH])
                    dst = kv[t % 2][:, :, :].rearrange("p a (h k v) -> p (a h) k v", h=HEADS, k=DH)
                    pool.tensor_tensor(dst, k, v, ALU.mult).then_inc(kv_ok, 1)

                def step(f, n, m, l):
                    at(l, outputs)
                    at(n, outer, 2)
                    at(n, outer, 3)
                    at(n, straight)
                    at(l, weighted)
                    at(m, outer, 0)
                    at(l, residual)
                    at(m, decayed, 0)
                    at(m, decayed, 1)
                    at(m, outer, 1)
                    at(m, decayed, 2)
                    at(m, decayed, 3)

                pool.sem_inc(yw_ok, 1)
                pool.sem_inc(x1_ok, 1)
                walk(pool, step)

            @block.scalar
            def _(act):
                def root1(l):
                    act.wait_ge(st1, l.count(1, 1))
                    act.activation(sd1[:, :], mv1[:, :, 1], ACT.Sqrt, bias=c.eps_ln[:, :]).then_inc(sd1_ok, 1)

                def norm1(l):
                    act.wait_ge(nm1_ok, l.count(1, 1))
                    act.wait_ge(yw_ok, l.count(1, 1))
                    for t in range(NT):
                        ins = act.activation(yn[:, t, :], ps_y[:, t, :], ACT.Identity, scale=rs1[:, t:t + 1], bias=nm1[:, t:t + 1])
                    ins.then_inc(yn_ok, 1)

                def root2(l):
                    act.wait_ge(st2, l.count(1, 1))
                    act.activation(sd2[:, :], mv2[:, :, 1], ACT.Sqrt, bias=c.eps_ln[:, :]).then_inc(sd2_ok, 1)

                def norm2(m):
                    act.wait_ge(nm2_ok, m.count(1, 1))
                    act.wait_ge(x_tr, m.count(1, 1))
                    for t in range(NT):
                        ins = act.activation(xn[:, t, :], x1[m.slot][:, t, :], ACT.Identity, scale=rs2[:, t:t + 1], bias=nm2[:, t:t + 1])
                    ins.then_inc(xn_ok, 1)

                def normed(m):
                    act.wait_ge(x_tr, m.count(1, 2))
                    act.wait_ge(qkv_mm, m.count(NT, 1))
                    act.activation(xnT[:, :, :], ps_x[:, :, :], ACT.Copy).then_inc(xT_ok, 1)

                def attended(f):
                    act.wait_ge(o_mm, f.count(1, 3))
                    act.wait_ge(out_mm, f.count(1, 1))
                    act.activation(oT[:, :, :], ps_o[:, :, :], ACT.Copy).then_inc(oT_ok, 1)

                def queries(n):
                    act.wait_ge(q_tr, n.count(1, 1))
                    act.activation(qdT[n.slot][:, 1:NT, :], ps_m[:, 1:NT, :], ACT.Copy).then_inc(qT_ok, 1)

                def store(f):
                    act.wait_ge(res_ok, f.count(1, 3))
                    act.dma_start(out[f.row(), :, :].rearrange("b (t p) d -> p (b t) d", p=P), res[:, :, :]).then_inc(stored, 16)

                def step(f, n, m, l):
                    at(m, norm2)
                    at(m, normed)
                    at(l, root1)
                    at(f, attended)
                    at(l, norm1)
                    at(l, root2)
                    at(f, store)
                    at(n, queries)

                act.sem_inc(xT_ok, 1)
                act.sem_inc(oT_ok, 1)
                act.sem_inc(yn_ok, 1)
                act.sem_inc(xn_ok, 2)
                act.sem_inc(stored, 16)
                walk(act, step)
                act.wait_ge(stored, 16 * B + 16)

            @block.vector
            def _(dve):
                def statistics(l, src, mv, done, links):
                    for t in range(NT):
                        ins = dve.bn_stats(out=stats[:, t, :], in_=src[:, t, :])
                    ins.then_inc(stat, 1)
                    dve.wait_ge(stat, l.count(2, links))
                    dve.sem_inc(aggregating, 1)
                    for t in range(NT):
                        ins = dve.bn_aggr(out=mv[:, t, :], in_=stats[:, t:t + 1, :])
                    ins.then_inc(done, 1)

                def stats1(l):
                    dve.wait_ge(y_tr, l.count(1, 2))
                    statistics(l, ps_y, mv1, st1, 1)

                def scale1(l):
                    dve.wait_ge(sd1_ok, l.count(1, 1))
                    dve.wait_ge(yn_ok, l.count(1, 1))
                    dve.reciprocal(rs1[:, :], sd1[:, :]).then_inc(rs1_ok, 1)
                    dve.wait_ge(rs1_ok, l.count(1, 1))
                    dve.scalar_tensor_tensor(out=nm1[:, :], in0=mv1[:, :, 0], scalar=-1.0, in1=rs1[:, :],
                                             op0=ALU.mult, op1=ALU.mult).then_inc(nm1_ok, 1)

                def branches(l):
                    dve.wait_ge(in_ok[l.slot], l.loads())
                    dve.wait_ge(f_tr, l.count(1, 1))
                    dve.wait_ge(x1_ok, l.count(1, 1))
                    dve.tensor_tensor(xf[:, :, :], x_in[l.slot][:, :, :], ps_x[:, :, :], ALU.add).then_inc(xf_ok, 1)

                def stats2(l):
                    dve.wait_ge(x1_ok, l.count(1, 2))
                    statistics(l, x1[l.slot], mv2, st2, 2)

                def scale2(m):
                    dve.wait_ge(sd2_ok, m.count(1, 1))
                    dve.reciprocal(rs2[:, :], sd2[:, :]).then_inc(rs2_ok, 1)
                    dve.wait_ge(rs2_ok, m.count(1, 1))
                    dve.scalar_tensor_tensor(out=nm2[:, :], in0=mv2[:, :, 0], scalar=-1.0, in1=rs2[:, :],
                                             op0=ALU.mult, op1=ALU.mult).then_inc(nm2_ok, 1)

                def project(m, t):
                    dve.wait_ge(qkv_mm, m.count(NT, t + 2))
                    dve.tensor_tensor(qkv[m.slot][:, t, :], ps_q[:, :, :].rearrange("p a b -> p (a b)"), c.b_second[:, :], ALU.add).then_inc(qkv_ok, 1)

                def scores(n, t):
                    dve.wait_ge(qd_ok, n.count(NT, t + 1))
                    dve.wait_ge(tri_mm, n.count(NT, t + 3))
                    q = qd[n.slot][:, t, :].rearrange("p (h k) -> p h k", h=H).unsqueeze(3).to_broadcast([P, H, DH, DH])
                    dve.tensor_tensor(qs[t % 2][:, :].rearrange("p (h k v) -> p h k v", h=H, k=DH),
                                      ps_s[:, :, :].rearrange("p a (h k v) -> p (a h) k v", h=HEADS, k=DH), q, ALU.mult).then_inc(qs_ok, 1)
                    dve.wait_ge(qs_ok, n.count(NT, t + 2))
                    dve.wait_ge(o_mm, n.count(1, 1))
                    dve.tensor_reduce(out=o_in[n.slot][:, t, :].rearrange("p (h v) -> p h v", h=H),
                                      in_=qs[t % 2][:, :].rearrange("p (h k v) -> p h v k", h=H, k=DH), axis=AX.X, op=ALU.add).then_inc(o_ok, 1)

                def state(n, t):
                    dve.wait_ge(past_mm, n.count(NT - 1, t + 1))
                    dve.tensor_tensor(past[n.slot][:, t, :], ps_kv[:, 0, :], c.head_ones[:, :], ALU.mult).then_inc(past_ok, 1)

                def result(f):
                    dve.wait_ge(out_mm, f.count(1, 2))
                    dve.wait_ge(x1b_ok, f.count(1, 1))
                    dve.wait_ge(stored, f.count(16, 16))
                    dve.tensor_tensor(res[:, :, :], ps_m[:, :, :], x1b[f.slot][:, :, :], ALU.add).then_inc(res_ok, 1)

                def step(f, n, m, l):
                    at(m, scale2)
                    at(n, scores, 0)
                    at(n, state, 0)
                    at(l, stats1)
                    at(n, scores, 1)
                    at(n, state, 1)
                    at(m, project, 0)
                    at(l, scale1)
                    at(n, scores, 2)
                    at(n, state, 2)
                    at(l, branches)
                    at(m, project, 1)
                    at(n, scores, 3)
                    at(m, project, 2)
                    at(f, result)
                    at(l, stats2)
                    at(m, project, 3)

                dve.sem_inc(qkv_ok, 1)
                dve.sem_inc(qs_ok, 1)
                dve.sem_inc(past_ok, 1)
                dve.sem_inc(res_ok, 2)
                walk(dve, step)

            @block.tensor
            def _(pe):
                def outputs(l):
                    pe.wait_ge(y_ok, l.count(1, 1))
                    pe.wait_ge(yn_ok, l.count(1, 1))
                    for t in range(NT):
                        ins = nc.tensor.transpose(ps_y[:, t, :], y_t[:, t * P:(t + 1) * P], c.ident[:, :])
                    ins.then_inc(y_tr, 1)

                def branches(l):
                    pe.wait_ge(in_ok[l.slot], l.loads())
                    pe.wait_ge(xT_ok, l.count(1, 1))
                    for t in range(NT):
                        ins = nc.tensor.transpose(ps_x[:, t, :], f_in[l.slot][:, t * P:(t + 1) * P], c.ident[:, :])
                    ins.then_inc(f_tr, 1)

                def normed(m):
                    pe.wait_ge(xn_ok, m.count(1, 3))
                    pe.wait_ge(xf_ok, m.count(1, 1))
                    for t in range(NT):
                        ins = nc.tensor.transpose(ps_x[:, t, :], xn[:, t, :], c.ident[:, :])
                    ins.then_inc(x_tr, 1)

                def project(m, t):
                    pe.wait_ge(xT_ok, m.count(1, 2))
                    pe.wait_ge(qkv_ok, m.count(NT, t + 1))
                    nc.tensor.matmul(ps_q[:, :, :].rearrange("p a b -> p (a b)"), xnT[:, t, :], c.w_second[:, :],
                                     start=True, stop=True).then_inc(qkv_mm, 1)

                def queries(n):
                    pe.wait_ge(qd_ok, n.count(NT, NT))
                    pe.wait_ge(res_ok, n.count(1, 2))
                    for t in range(1, NT):
                        ins = nc.tensor.transpose(ps_m[:, t, :], qd[n.slot][:, t, :], c.ident[:, :])
                    ins.then_inc(q_tr, 1)

                def running(n, t):
                    pe.wait_ge(kv_ok, n.count(NT, t + 1))
                    pe.wait_ge(qs_ok, n.count(NT, t + 1))
                    nc.tensor.matmul(ps_s[:, 0, :], c.tri[:, :], kv[t % 2][:, 0, :], start=True, stop=True)
                    nc.tensor.matmul(ps_s[:, 1, :], c.tri[:, :], kv[t % 2][:, 1, :], start=True, stop=True).then_inc(tri_mm, 1)

                def state(n, t):
                    pe.wait_ge(past_ok, n.count(NT - 1, t + 1))
                    pe.wait_ge(qkv_ok, n.count(NT, t + 2))
                    nc.tensor.matmul(ps_kv[:, 0, :], qkv[n.slot][:, t, P:2 * P], qkv[n.slot][:, t, 2 * P:3 * P],
                                     start=t == 0, stop=True, skip_group_check=True).then_inc(past_mm, 1)

                def attended(f):
                    pe.wait_ge(qT_ok, f.count(1, 1))
                    pe.wait_ge(past_ok, f.count(NT - 1, NT))
                    pe.wait_ge(oT_ok, f.count(1, 1))
                    for t in range(NT):
                        pe.wait_ge(o_ok, f.count(NT, t + 1))
                        if t > 0:
                            nc.tensor.matmul(ps_o[:, t, :], past[f.slot][:, t - 1, :], qdT[f.slot][:, t, :], start=True, stop=False)
                        ins = nc.tensor.matmul(ps_o[:, t, :], o_in[f.slot][:, t, :], c.ident[:, :], start=t == 0, stop=True)
                    ins.then_inc(o_mm, 1)

                def final(f):
                    pe.wait_ge(oT_ok, f.count(1, 2))
                    for t in range(NT):
                        ins = nc.tensor.matmul(ps_m[:, t, :], oT[:, t, :], c.wo_t[:, :], start=True, stop=True)
                    ins.then_inc(out_mm, 1)

                def step(f, n, m, l):
                    at(n, running, 0)
                    at(n, state, 0)
                    at(l, outputs)
                    at(m, normed)
                    at(n, running, 1)
                    at(n, state, 1)
                    at(m, project, 0)
                    at(f, attended)
                    at(n, running, 2)
                    at(n, state, 2)
                    at(l, branches)
                    at(m, project, 1)
                    at(n, running, 3)
                    at(f, final)
                    at(m, project, 2)
                    at(m, project, 3)
                    at(n, queries)

                pe.sem_inc(y_tr, 1)
                pe.sem_inc(x_tr, 1)
                pe.sem_inc(tri_mm, 2)
                pe.sem_inc(o_mm, 2)
                pe.sem_inc(out_mm, 1)
                pe.sem_inc(qkv_mm, 1)
                walk(pe, step)


_INS = ("L0_attn_x", "L0_attn_W", "L0_attn_k_norm_w", "L0_attn_o_norm_w", "L0_attn_o_norm_b", "L0_attn_eta_raw",
        "L0_attn_lam_logit", "L0_ffn_w1_w", "L0_ffn_w1_s", "L0_ffn_w2_w", "L0_ffn_w2_s", "L0_ffn_h1_w", "L0_ffn_h1_s",
        "L0_ffn_h2_w", "L0_ffn_h2_s", "L0_ffn_w3_w", "L0_ffn_w3_s", "L1_attn_Wq", "L1_attn_bq", "L1_attn_Wk",
        "L1_attn_bk", "L1_attn_Wv", "L1_attn_bv", "L1_attn_Wo", "L1_attn_bo", "L1_attn_gamma", "L1_ffn_W", "L1_ffn_b",
        "L1_ffn_V_r", "L1_ffn_C")


def kernel(**inputs):
    import numpy as _np
    import concourse.bacc as _bacc
    from concourse import mybir as _mybir
    from concourse.bass_utils import run_bass_kernel_spmd as _run

    nc = _bacc.Bacc("TRN2", target_bir_lowering=False, num_devices=1)
    arrays, io = {}, {}
    for name in _INS:
        a = _np.ascontiguousarray(inputs[name])
        arrays[f"in_{name}_dram"] = a
        io[name] = nc.dram_tensor(f"in_{name}_dram", a.shape, _mybir.dt.from_np(a.dtype), kind="ExternalInput").ap()
    out = nc.dram_tensor("out_0_dram", (B, L, D), F32, kind="ExternalOutput").ap()
    build(nc, io, out)
    r = _run(nc, [arrays], core_ids=[0])
    return r.results[0]["out_0_dram"]
```

```python
import concourse.bass as bass
from concourse import mybir
from contextlib import ExitStack

F32 = mybir.dt.float32
F32R = mybir.dt.float32r
I32 = mybir.dt.int32
ALU = mybir.AluOpType
ACT = mybir.ActivationFunctionType
AX = mybir.AxisListType

B, L, D = 16, 512, 128
H, DH = 16, 8
HID = 512
P = 128
NT = L // P
NB = HID // P
RANK = 32
ROW = 32
G = B * H // P
BG = B // G
BLK = 4
SEG = 64
LN_EPS = 1e-5
F32_EPS = 1.1920928955078125e-07

W1, W2, H1, H2, W3 = 0, NB, 2 * NB, 2 * NB + NB * NB, 2 * NB + 2 * NB * NB
NW = W3 + NB


def build(nc, io, out):
    scr = {}
    for name in ("xnT", "P", "K", "R", "fac", "W", "ffnT"):
        rows = B + 1 if name in ("xnT", "ffnT") else B
        scr[name] = nc.dram_tensor("scratch_" + name, [rows, P, L], F32).ap()
    with ExitStack() as ctx:
        c = constants(nc, ctx)
        setup(nc, io, c)
        prepare(nc, io, scr, c)
        recur_and_feed_forward(nc, io, scr, c)
        second_layer(nc, io, scr, c, out)


class Tiles:
    pass


def constants(nc, ctx):
    c = Tiles()

    def sb(name, shape, dt=F32):
        return ctx.enter_context(nc.sbuf_tensor(name, shape, dt))

    c.ident = sb("ident", [P, P])
    c.head_ones = sb("head_ones", [P, P])
    c.tri = sb("tri", [P, P])
    c.w_hi = sb("w_hi", [P, NW, P], F32R)
    c.w_lo = sb("w_lo", [P, NW, P], F32R)
    c.ws_t = sb("ws_t", [P, P])
    c.w_second = sb("w_second", [P, 4 * P])
    c.wo_t = sb("wo_t", [P, P])
    c.s1 = sb("s1", [P, NB])
    c.s2 = sb("s2", [P, NB])
    c.t1 = sb("t1", [P, NB])
    c.t2 = sb("t2", [P, NB])
    c.s3 = sb("s3", [P, 1])
    c.knw = sb("knw", [P, 1])
    c.gate = sb("gate", [P, 1])
    c.pfac = sb("pfac", [P, BLK])
    c.kfac = sb("kfac", [P, BLK])
    c.lam4 = sb("lam4", [P, 1])
    c.dec = sb("dec", [P, NT, P])
    c.b_second = sb("b_second", [2 * ROW, 4 * P], F32R)
    c.one_rows = sb("one_rows", [2 * ROW, P], F32R)
    c.ow = sb("ow", [P, P])
    c.ob = sb("ob", [P, 1])
    c.eps_ln = sb("eps_ln", [P, 1])
    c.eps_rms = sb("eps_rms", [P, 1])
    c.flag = sb("flag", [1, 1], I32)
    return c


def setup(nc, io, c):
    ctx = ExitStack()
    with ctx:
        def sb(name, shape, dt=F32):
            return ctx.enter_context(nc.sbuf_tensor(name, shape, dt))

        def sem(name):
            return ctx.enter_context(nc.semaphore(name))

        nat12 = sb("nat12", [P, 2, NB, P])
        nath = sb("nath", [P, 2, NB, HID])
        nat3 = sb("nat3", [P, HID])
        nats = sb("nats", [P, 6, P])
        natr = sb("natr", [P, 2, RANK])
        vr_t = sb("vr_t", [RANK, 2, P])
        par = sb("par", [P, 4])
        work = sb("work", [P, 16])
        dec_t = sb("dec_t", [P, L])
        ones = sb("ones", [P, L])
        biases = sb("biases", [2 * ROW, 5, P])
        b_hi = sb("b_hi", [2 * ROW, 4 * P], F32R)
        peaks = sb("peaks", [P, NW // NB])
        peak = sb("peak", [P, 1])
        ftmp = sb("ftmp", [1, 2])
        ps = [ctx.enter_context(nc.psum_tensor(f"ps_set{i}", [P, 4, P], F32)) for i in range(2)]
        ps_s = ctx.enter_context(nc.psum_tensor("ps_small", [P, 4, P], F32))
        ps_d = ctx.enter_context(nc.psum_tensor("ps_dec", [P, 4, P], F32))

        zeroed = sem("s_zeroed")
        mat_in = [sem(f"s_mat_in{i}") for i in range(5)]
        squares_in = sem("s_squares_in")
        loaded = sem("s_loaded")
        const_done = sem("s_const")
        pool_chain = sem("s_pool_chain")
        tr_done = sem("s_tr")
        hi_done = sem("s_hi")
        lo_done = sem("s_lo")
        small_tr = sem("s_small_tr")
        small_cp = sem("s_small_cp")
        vec = sem("s_vec")
        exps = sem("s_exps")
        peak_done = sem("s_peak")
        peak_tr = sem("s_peak_tr")
        dec_ready = sem("s_dec_ready")
        dec_tr = sem("s_dec_tr")
        weff = sem("s_weff")

        groups = [[nat12[:, 0, j, :] for j in range(NB)], [nat12[:, 1, j, :] for j in range(NB)]]
        for w in range(2):
            groups += [[nath[:, w, o, i * P:(i + 1) * P] for o in range(NB)] for i in range(NB)]
        groups += [[nat3[:, i * P:(i + 1) * P] for i in range(NB)]]
        NG = len(groups)

        of_mat = [0, 1] + [2] * NB + [3] * NB + [4]

        mats, squares, loads = [], [], []

        def add(dst, src, to=loads):
            to.append((dst, src))

        add(nat12[:, 0, :, :], io["L0_ffn_w1_w"].rearrange("(o p) i -> p o i", p=P), mats)
        add(nat12[:, 1, :, :], io["L0_ffn_w2_w"].rearrange("(o p) i -> p o i", p=P), mats)
        add(nath[:, 0, :, :], io["L0_ffn_h1_w"].rearrange("(o p) i -> p o i", p=P), mats)
        add(nath[:, 1, :, :], io["L0_ffn_h2_w"].rearrange("(o p) i -> p o i", p=P), mats)
        add(nat3[:, :], io["L0_ffn_w3_w"], mats)
        for n, name in enumerate(("L0_attn_W", "L1_attn_Wq", "L1_attn_Wk", "L1_attn_Wv", "L1_attn_Wo", "L1_ffn_W")):
            add(nats[:, n, :], io[name], squares)
        add(natr[:, 0, :], io["L1_ffn_V_r"], squares)
        add(natr[:, 1, :], io["L1_ffn_C"], squares)
        for dst, name in ((c.s1, "L0_ffn_w1_s"), (c.s2, "L0_ffn_w2_s"), (c.t1, "L0_ffn_h1_s"), (c.t2, "L0_ffn_h2_s")):
            add(dst[:, :], io[name].rearrange("(o p) -> p o", p=P))
        add(c.s3[:, :], io["L0_ffn_w3_s"].rearrange("(p o) -> p o", o=1))

        add(c.ow[:, :], io["L0_attn_o_norm_w"].partition_broadcast(P))
        add(c.ob[:, :], io["L0_attn_o_norm_b"].rearrange("(p o) -> p o", o=1))
        for n, name in enumerate(("L0_attn_lam_logit", "L0_attn_eta_raw", "L1_attn_gamma")):
            add(par[:, n:n + 1], io[name].unsqueeze(1).to_broadcast([H, DH]))
        add(par[:, 3:4], io["L0_attn_lam_logit"].unsqueeze(0).to_broadcast([BG, H]))
        add(c.knw[:, :], io["L0_attn_k_norm_w"].unsqueeze(0).to_broadcast([H, DH]))
        for n, name in enumerate(("L1_attn_bq", "L1_attn_bk", "L1_attn_bv", "L1_attn_bo", "L1_ffn_b")):
            for row in (0, ROW):
                add(biases[row:row + 1, n, :], io[name].unsqueeze(0))
        NL = 16 * len(loads)
        NS = 16 * len(squares)

        with nc.allow_non_contiguous_dma(reason='a few hundred words of scales and per-head factors'), nc.Block() as block:
            @block.sync
            def _(sp):
                for i in (0, 2, 4):
                    sp.dma_start(*mats[i]).then_inc(mat_in[i], 16)
                sp.wait_ge(zeroed, 1)
                for dst, src in loads:
                    sp.dma_start(dst, src).then_inc(loaded, 16)

            @block.gpsimd
            def _(pool):
                pool.memset(c.ident[:, :], 0.0).then_inc(pool_chain, 1)
                pool.memset(c.head_ones[:, :], 1.0).then_inc(pool_chain, 1)
                pool.memset(c.tri[:, :], 1.0).then_inc(pool_chain, 1)
                pool.memset(c.eps_ln[:, :], LN_EPS)
                pool.memset(c.eps_rms[:, :], F32_EPS).then_inc(pool_chain, 1)
                pool.wait_ge(pool_chain, 4)
                pool.affine_select(out=c.ident[:, :], in_=c.ident[:, :], compare_op=ALU.not_equal, fill=1.0,
                                   base=0, pattern=[[-1, P]], channel_multiplier=1).then_inc(const_done, 1)
                pool.affine_select(out=c.tri[:, :], in_=c.tri[:, :], compare_op=ALU.is_ge, fill=0.0,
                                   base=0, pattern=[[1, P]], channel_multiplier=-1).then_inc(const_done, 1)
                heads = c.head_ones[:, :].rearrange("p (h k) -> p h k", k=DH)
                pool.affine_select(out=heads, in_=heads, compare_op=ALU.is_ge, fill=0.0,
                                   base=0, pattern=[[-DH, H], [0, DH]], channel_multiplier=1).then_inc(pool_chain, 1)
                pool.wait_ge(pool_chain, 5)
                pool.affine_select(out=heads, in_=heads, compare_op=ALU.is_ge, fill=0.0,
                                   base=DH - 1, pattern=[[DH, H], [0, DH]], channel_multiplier=-1).then_inc(const_done, 1)

            @block.tensor
            def _(pe):
                pe.wait_ge(const_done, 1)
                for g, blocks in enumerate(groups):
                    pe.wait_ge(mat_in[of_mat[g]], 16)
                    if g >= 2:
                        pe.wait_ge(lo_done, g - 1)
                    for n, b in enumerate(blocks):
                        last = nc.tensor.transpose(ps[g % 2][:, n, :], b, c.ident[:, :])
                    last.then_inc(tr_done, 1)
                pe.wait_ge(squares_in, NS)
                for n in range(4):
                    last = nc.tensor.transpose(ps_s[:, n, :], nats[:, n, :], c.ident[:, :])
                last.then_inc(small_tr, 1)
                pe.wait_ge(small_cp, 2)
                nc.tensor.transpose(ps_s[:, 0, :], nats[:, 4, :], c.ident[:, :])
                nc.tensor.transpose(ps_s[0:RANK, 1, :], natr[:, 0, :], c.ident[:, :])
                nc.tensor.transpose(ps_s[0:RANK, 2, :], natr[:, 1, :], c.ident[:, :]).then_inc(small_tr, 1)
                pe.wait_ge(small_cp, 4)
                nc.tensor.matmul(ps_s[:, 3, :], nats[:, 5, :], c.ident[:, :], start=True, stop=False)
                nc.tensor.matmul(ps_s[:, 3, :], vr_t[:, 0, :], vr_t[:, 1, :], start=False, stop=True).then_inc(weff, 1)
                pe.wait_ge(dec_ready, 1)
                for n in range(NT):
                    last = nc.tensor.transpose(ps_d[:, n, :], dec_t[:, n * P:(n + 1) * P], c.ident[:, :])
                last.then_inc(dec_tr, 1)
                pe.wait_ge(peak_done, 1)
                pe.wait_ge(lo_done, NG)
                nc.tensor.transpose(ps[0][0:1, 0, :], peak[:, :], c.ident[:, :]).then_inc(peak_tr, 1)

            @block.scalar
            def _(act):
                for i in (1, 3):
                    act.dma_start(*mats[i]).then_inc(mat_in[i], 16)
                for dst, src in squares:
                    act.dma_start(dst, src).then_inc(squares_in, 16)
                for g in range(NG):
                    act.wait_ge(tr_done, g + 1)
                    act.activation(c.w_hi[:, NB * g:NB * g + NB, :], ps[g % 2][:, :, :], ACT.Copy).then_inc(hi_done, 1)
                act.wait_ge(loaded, NL)
                act.activation(work[:, 0:1], par[:, 0:1], ACT.Exp, scale=-1.0)
                act.activation(work[:, 1:2], par[:, 1:2], ACT.Tanh)
                act.activation(work[:, 2:3], par[:, 3:4], ACT.Exp, scale=-1.0).then_inc(exps, 1)
                act.wait_ge(small_tr, 1)
                act.activation(c.ws_t[:, :], ps_s[:, 0, :], ACT.Copy).then_inc(small_cp, 1)
                act.activation(c.w_second[:, 0:3 * P].rearrange("p (n k) -> p n k", n=3), ps_s[:, 1:4, :], ACT.Copy).then_inc(small_cp, 1)
                act.wait_ge(small_tr, 2)
                act.activation(c.wo_t[:, :], ps_s[:, 0, :], ACT.Copy).then_inc(small_cp, 1)
                act.activation(vr_t[:, :, :], ps_s[0:RANK, 1:3, :], ACT.Copy).then_inc(small_cp, 1)
                act.wait_ge(weff, 1)
                act.activation(c.w_second[:, 3 * P:4 * P], ps_s[:, 3, :], ACT.Copy)
                act.wait_ge(dec_tr, 1)
                act.activation(c.dec[:, :, :], ps_d[:, :, :], ACT.Copy)

            @block.vector
            def _(dve):
                chain = [0]

                def link(ins):
                    chain[0] += 1
                    ins.then_inc(vec, 1)
                    dve.wait_ge(vec, chain[0])

                dve.memset(biases[:, :, :], 0.0).then_inc(zeroed, 1)
                dve.memset(ones[:, :], 1.0)
                link(dve.memset(dec_t[:, 0:1], 1.0))
                def largest(g):
                    return dve.tensor_reduce(peaks[:, g:g + 1], c.w_lo[:, NB * g:NB * g + NB, :].bitcast(F32), AX.XY, ALU.max,
                                             apply_absolute_value=True)

                for g in range(NG):
                    dve.wait_ge(hi_done, g + 1)
                    lo = c.w_lo[:, NB * g:NB * g + NB, :]
                    ins = dve.tensor_tensor(lo, ps[g % 2][:, :, :], c.w_hi[:, NB * g:NB * g + NB, :].bitcast(F32), ALU.subtract)
                    ins.then_inc(lo_done, 1)
                    if g > 0:
                        dve.wait_ge(lo_done, g)
                        largest(g - 1)
                dve.wait_ge(lo_done, NG)
                link(largest(NG - 1))
                dve.tensor_reduce(peak[:, :], peaks[:, :], AX.X, ALU.max).then_inc(peak_done, 1)
                dve.wait_ge(exps, 1)
                link(dve.tensor_scalar_add(work[:, 5:6], work[:, 0:1], 1.0))
                link(dve.tensor_scalar_add(work[:, 6:7], work[:, 2:3], 1.0))
                link(dve.reciprocal(work[:, 3:4], work[:, 5:6]))
                link(dve.reciprocal(work[:, 4:5], work[:, 6:7]))
                link(dve.tensor_scalar(work[:, 7:8], work[:, 3:4], -1.0, 1.0, ALU.mult, ALU.add))
                link(dve.tensor_tensor(work[:, 8:9], work[:, 7:8], work[:, 1:2], ALU.mult))
                link(dve.tensor_scalar(c.gate[:, :], work[:, 8:9], 1.0 / DH, None, ALU.mult))
                link(dve.memset(c.kfac[:, 3:4], 1.0))
                link(dve.tensor_scalar(c.pfac[:, 0:1], c.gate[:, :], work[:, 3:4], None, ALU.mult))
                for i in range(1, BLK):
                    link(dve.tensor_scalar(c.pfac[:, i:i + 1], c.pfac[:, i - 1:i], work[:, 3:4], None, ALU.mult))
                    link(dve.tensor_scalar(c.kfac[:, 3 - i:4 - i], c.kfac[:, 4 - i:5 - i], work[:, 3:4], None, ALU.mult))
                link(dve.tensor_tensor(work[:, 9:10], work[:, 4:5], work[:, 4:5], ALU.mult))
                link(dve.tensor_tensor(c.lam4[:, :], work[:, 9:10], work[:, 9:10], ALU.mult))
                dve.tensor_tensor_scan(dec_t[:, 1:L], par[:, 2:3].to_broadcast([P, L - 1]), ones[:, 0:L - 1], 1.0,
                                       ALU.mult, ALU.mult).then_inc(dec_ready, 1)
                link(dve.tensor_tensor(biases[:, 3, :], biases[:, 3, :], biases[:, 4, :], ALU.add))
                all_biases = biases[:, 0:4, :].rearrange("p a b -> p (a b)")
                link(dve.tensor_copy(b_hi[:, :], all_biases))
                dve.tensor_copy(c.b_second[0:ROW, :], b_hi[0:ROW, :].bitcast(F32))
                dve.tensor_tensor(c.b_second[ROW:2 * ROW, :], all_biases[ROW:2 * ROW, :], b_hi[ROW:2 * ROW, :].bitcast(F32), ALU.subtract)
                dve.tensor_copy(c.one_rows[:, :], ones[0:2 * ROW, 0:P])

                dve.wait_ge(peak_tr, 1)
                link(dve.tensor_reduce(ftmp[:, 0:1], ps[0][0:1, 0, :], AX.X, ALU.max))
                link(dve.tensor_scalar(ftmp[:, 1:2], ftmp[:, 0:1], 0.0, None, ALU.is_gt))
                dve.tensor_copy(c.flag[:, :], ftmp[:, 1:2])


class Sequence:

    def __init__(self, turn, off):
        self.turn, self.off, self.slot = turn, off, off % 2

    def count(self, each, more):
        if self.turn is None:
            return self.off * each + more
        return self.turn * (2 * each) + (self.off * each + more)

    def loads(self):
        if self.turn is None:
            return 64 * (self.off // 2 + 1)
        return self.turn * 64 + 64 * (self.off // 2 + 1)

    def stores(self):
        if self.turn is None:
            return 16 * (self.off // 2 + 1)
        return self.turn * 16 + 16 * (self.off // 2 + 1)

    def row(self, more=0):
        return bass.ds(self.count(1, more), 1)


def at(s, stage, *more):
    if s is not None:
        stage(s, *more)


def prepare(nc, io, scr, c):
    ctx = ExitStack()
    NBLK = L // BLK
    SWEEPS = 2 * (BLK - 1)
    with ctx:
        def sb(name, shape, dt=F32):
            return ctx.enter_context(nc.sbuf_tensor("p_" + name, shape, dt))

        def sem(name):
            return ctx.enter_context(nc.semaphore("p_" + name))

        def two(name, shape):
            return [sb(name + "0", shape), sb(name + "1", shape)]

        def two_sems(name):
            return [sem(name + "0"), sem(name + "1")]

        def pb(name):
            return ctx.enter_context(nc.psum_tensor("p_" + name, [P, NT, P], F32))

        tile = [P, NT, P]
        x_in = two("x", tile)
        stats = sb("stats", [P, NT, 6])
        mv = sb("mv", [P, NT, 2])
        std, rstd, nm = sb("std", [P, NT]), sb("rstd", [P, NT]), sb("nm", [P, NT])
        xn = two("xn", tile)
        sq = sb("sq", tile)
        ssq, rms, rrms = sb("ssq", [P, NT * H]), sb("rms", [P, NT * H]), sb("rrms", [P, NT * H])
        keys_t = sb("keys", tile)
        xnT, kT = two("xnT", [P, L]), two("kT", [P, L])
        k2 = sb("k2", [P, L])
        fac, kout = two("fac", [P, L]), two("kout", [P, L])
        prod = sb("prod", [P, BLK - 1, BLK - 1, NBLK])
        coup = two("coup", [P, BLK - 1, BLK - 1, NBLK])
        rr, pp = two("rr", [P, L]), two("pp", [P, L])
        tmp_r, tmp_p = sb("tmp_r", [P, BLK - 1, NBLK]), sb("tmp_p", [P, BLK - 1, NBLK])
        ps_x, ps_k, ps_s, ps_f = pb("ps_x"), pb("ps_k"), pb("ps_s"), pb("ps_f")
        ps_n = [pb(f"ps_n{d}") for d in range(1, BLK)]

        x_ready = two_sems("x_ready")
        stat, aggregating, stat_ok, std_ok, rstd_ok, nm_ok = (sem("stat"), sem("aggregating"), sem("stat_ok"), sem("std_ok"),
                                                              sem("rstd_ok"), sem("nm_ok"))
        xn_ok, sq_ok, ssq_ok, rms_ok, rrms_ok, keys_ok = (sem("xn_ok"), sem("sq_ok"), sem("ssq_ok"), sem("rms_ok"),
                                                          sem("rrms_ok"), sem("keys_ok"))
        x_tr, k_tr, xT_ok, kT_ok = sem("x_tr"), sem("k_tr"), sem("xT_ok"), sem("kT_ok")
        s_mm, r_in = sem("s_mm"), sem("r_in")
        k2_ok, f_mm, fac_ok = sem("k2_ok"), sem("f_mm"), sem("fac_ok")
        prod_ok, n_mm, coup_ok = sem("prod_ok"), sem("n_mm"), sem("coup_ok")
        p_in, kout_ok = sem("p_in"), sem("kout_ok")
        r_step, p_step = sem("r_step"), sem("p_step")
        st_x, st_f, st_k, st_r, st_p = (two_sems("st_x"), two_sems("st_f"), two_sems("st_k"), two_sems("st_r"),
                                        two_sems("st_p"))

        def by_pos(ap):
            return ap.rearrange("p (b i) -> p i b", i=BLK)

        def sweep(eng, n, ap, tmp, step, j):
            rest = BLK - 1 - j
            if j > 0:
                eng.wait_ge(step, n.count(SWEEPS, 2 * SWEEPS + 2 * j))
            eng.tensor_tensor(tmp[:, 0:rest, :], coup[n.slot][:, 0:rest, j, :],
                              by_pos(ap)[:, j:j + 1, :].to_broadcast([P, rest, NBLK]), ALU.mult).then_inc(step, 1)
            eng.wait_ge(step, n.count(SWEEPS, 2 * SWEEPS + 2 * j + 1))
            later = by_pos(ap)[:, j + 1:BLK, :]
            eng.tensor_tensor(later, later, tmp[:, 0:rest, :], ALU.add).then_inc(step, 1)

        def walk(engine, step):
            def outside(k):
                step(*[Sequence(None, k + d) if 0 <= k + d < B else None for d in range(3)])

            for k in (-2, -1):
                outside(k)
            with engine.Fori(0, B // 2 - 1) as turn:
                for k in (0, 1):
                    step(*[Sequence(turn, k + d) for d in range(3)])
            for k in (B - 2, B - 1):
                outside(k)

        with nc.Block() as block:
            @block.sync
            def _(sp):
                def load(s):
                    if s.turn is not None or s.off >= 2:
                        sp.wait_ge(xn_ok, s.count(1, -1))
                    sp.dma_start(x_in[s.slot][:, :, :], io["L0_attn_x"][s.row(), :, :].rearrange("b (t p) d -> p (b t) d", p=P)
                                 ).then_inc(x_ready[s.slot], 16)

                def store(n):
                    def put(name, tile, done):
                        sp.dma_start(scr[name][n.row(), :, :].rearrange("b p t -> p (b t)"), tile[n.slot][:, :]).then_inc(done[n.slot], 16)
                    sp.wait_ge(xT_ok, n.count(1, 2))
                    put("xnT", xnT, st_x)
                    sp.wait_ge(kout_ok, n.count(1, 3))
                    put("K", kout, st_k)
                    sp.wait_ge(fac_ok, n.count(1, 2))
                    put("fac", fac, st_f)
                    sp.wait_ge(r_step, n.count(SWEEPS, 3 * SWEEPS))
                    put("R", rr, st_r)
                    sp.wait_ge(p_step, n.count(SWEEPS, 3 * SWEEPS))
                    put("P", pp, st_p)

                for off in range(3):
                    load(Sequence(None, off))
                with sp.Fori(0, B // 2 - 2) as turn:
                    for off in range(2):
                        load(Sequence(turn, off + 3))
                        store(Sequence(turn, off))
                load(Sequence(None, B - 1))
                for off in range(B - 4, B):
                    store(Sequence(None, off))
                sp.dma_start(scr["xnT"][B, :, :], xnT[(B - 1) % 2][:, :]).then_inc(st_x[(B - 1) % 2], 16)
                for done in (st_x, st_k, st_f, st_r, st_p):
                    for u in range(2):
                        more = 16 if done is st_x and u == (B - 1) % 2 else 0
                        sp.wait_ge(done[u], 16 * (B // 2) + 16 + more)

            @block.gpsimd
            def _(pool):
                def scaled(n):
                    pool.wait_ge(kT_ok, n.count(1, 2))
                    pool.wait_ge(st_p[n.slot], n.stores())
                    pool.tensor_tensor(by_pos(pp[n.slot][:, :]), by_pos(kT[n.slot][:, :]),
                                       c.pfac[:, :].unsqueeze(2).to_broadcast([P, BLK, NBLK]), ALU.mult).then_inc(p_in, 1)

                def solve(n):
                    pool.wait_ge(coup_ok, n.count(1, 2))
                    pool.wait_ge(p_in, n.count(1, 3))
                    for j in range(BLK - 1):
                        sweep(pool, n, pp[n.slot][:, :], tmp_p, p_step, j)

                def step(n, m, l):
                    at(n, scaled)
                    at(n, solve)

                pool.sem_inc(p_in, 2)
                pool.sem_inc(p_step, 2 * SWEEPS)
                for u in range(2):
                    pool.sem_inc(st_p[u], 16)
                walk(pool, step)

            @block.scalar
            def _(act):
                def root(l):
                    act.wait_ge(stat_ok, l.count(1, 1))
                    act.activation(std[:, :], mv[:, :, 1], ACT.Sqrt, bias=c.eps_ln[:, :]).then_inc(std_ok, 1)

                def norm(l):
                    act.wait_ge(nm_ok, l.count(1, 1))
                    act.wait_ge(x_tr, l.count(1, 1))
                    for t in range(NT):
                        ins = act.activation(xn[l.slot][:, t, :], x_in[l.slot][:, t, :], ACT.Identity,
                                             scale=rstd[:, t:t + 1], bias=nm[:, t:t + 1])
                    ins.then_inc(xn_ok, 1)

                def square(l):
                    act.wait_ge(ssq_ok, l.count(1, 1))
                    act.wait_ge(xn_ok, l.count(1, 1))
                    act.activation(sq[:, :, :], xn[l.slot][:, :, :], ACT.Square).then_inc(sq_ok, 1)

                def root_mean(m):
                    act.wait_ge(ssq_ok, m.count(1, 2))
                    act.activation(rms[:, :], ssq[:, :], ACT.Sqrt, bias=c.eps_rms[:, :], scale=1.0 / DH).then_inc(rms_ok, 1)

                def normed(m):
                    act.wait_ge(st_x[m.slot], m.stores())
                    act.wait_ge(x_tr, m.count(1, 3))
                    act.activation(xnT[m.slot][:, :], ps_x[:, :, :].rearrange("p a b -> p (a b)"), ACT.Copy).then_inc(xT_ok, 1)

                def keys(m):
                    act.wait_ge(prod_ok, m.count(1, 1))
                    act.wait_ge(kout_ok, m.count(1, 1))
                    act.wait_ge(p_in, m.count(1, 1))
                    act.wait_ge(k_tr, m.count(1, 2))
                    act.activation(kT[m.slot][:, :], ps_k[:, :, :].rearrange("p a b -> p (a b)"), ACT.Copy, scale=c.knw[:, :]).then_inc(kT_ok, 1)

                def static(m):
                    act.wait_ge(st_r[m.slot], m.stores())
                    act.wait_ge(s_mm, m.count(1, 1))
                    act.activation(rr[m.slot][:, :], ps_s[:, :, :].rearrange("p a b -> p (a b)"), ACT.Copy).then_inc(r_in, 1)

                def key_squares(n):
                    act.wait_ge(kT_ok, n.count(1, 2))
                    act.activation(k2[:, :], kT[n.slot][:, :], ACT.Square).then_inc(k2_ok, 1)

                def couplings(n):
                    act.wait_ge(r_step, n.count(SWEEPS, SWEEPS))
                    act.wait_ge(p_step, n.count(SWEEPS, SWEEPS))
                    act.wait_ge(n_mm, n.count(1, 2))
                    for d in range(1, BLK):
                        ins = act.activation(coup[n.slot][:, d - 1, 0:BLK - d, :], ps_n[d - 1][:, 0:BLK - d, :], ACT.Copy,
                                             scale=c.pfac[:, d - 1:d])
                    ins.then_inc(coup_ok, 1)

                def factors(n):
                    act.wait_ge(st_f[n.slot], n.stores())
                    act.wait_ge(f_mm, n.count(1, 1))
                    act.activation(fac[n.slot][:, :], ps_f[:, :, :].rearrange("p a b -> p (a b)"), ACT.Identity,
                                   scale=c.gate[:, :], bias=1.0).then_inc(fac_ok, 1)

                def step(n, m, l):
                    at(n, key_squares)
                    at(m, normed)
                    at(m, root_mean)
                    at(l, root)
                    at(n, couplings)
                    at(n, factors)
                    at(l, norm)
                    at(m, keys)
                    at(l, square)
                    at(m, static)

                act.sem_inc(xT_ok, 1)
                act.sem_inc(kT_ok, 1)
                act.sem_inc(r_in, 1)
                act.sem_inc(coup_ok, 1)
                act.sem_inc(fac_ok, 1)
                for u in range(2):
                    act.sem_inc(st_x[u], 16)
                    act.sem_inc(st_f[u], 16)
                    act.sem_inc(st_r[u], 16)
                walk(act, step)

            @block.vector
            def _(dve):
                def statistics(l):
                    dve.wait_ge(x_ready[l.slot], l.stores())
                    for t in range(NT):
                        ins = dve.bn_stats(stats[:, t, :], x_in[l.slot][:, t, :])
                    ins.then_inc(stat, 1)

                def aggregate(l):
                    dve.wait_ge(stat, l.count(1, 1))
                    dve.sem_inc(aggregating, 1)
                    for t in range(NT):
                        ins = dve.bn_aggr(mv[:, t, :], stats[:, t, :])
                    ins.then_inc(stat_ok, 1)

                def scale(l):
                    dve.wait_ge(std_ok, l.count(1, 1))
                    dve.reciprocal(rstd[:, :], std[:, :]).then_inc(rstd_ok, 1)

                def offset(l):
                    dve.wait_ge(rstd_ok, l.count(1, 1))
                    dve.scalar_tensor_tensor(out=nm[:, :], in0=mv[:, :, 0], scalar=-1.0, in1=rstd[:, :],
                                             op0=ALU.mult, op1=ALU.mult).then_inc(nm_ok, 1)

                def square_sums(m):
                    dve.wait_ge(sq_ok, m.count(1, 1))
                    dve.wait_ge(rms_ok, m.count(1, 1))
                    dve.tensor_reduce(out=ssq[:, :], in_=sq[:, :, :].rearrange("p t (h k) -> p (t h) k", h=H),
                                      axis=AX.X, op=ALU.add).then_inc(ssq_ok, 1)

                def inverse_rms(m):
                    dve.wait_ge(rms_ok, m.count(1, 2))
                    dve.reciprocal(rrms[:, :], rms[:, :]).then_inc(rrms_ok, 1)

                def keys(m):
                    dve.wait_ge(k_tr, m.count(1, 1))
                    dve.wait_ge(rrms_ok, m.count(1, 1))
                    dve.tensor_tensor(keys_t[:, :, :].rearrange("p t (h k) -> p (t h) k", h=H),
                                      xn[m.slot][:, :, :].rearrange("p t (h k) -> p (t h) k", h=H),
                                      rrms[:, :].unsqueeze(2).to_broadcast([P, NT * H, DH]), ALU.mult).then_inc(keys_ok, 1)

                def products(n):
                    dve.wait_ge(n_mm, n.count(1, 1))
                    dve.wait_ge(kT_ok, n.count(1, 2))
                    k = by_pos(kT[n.slot][:, :])
                    for d in range(1, BLK):
                        ins = dve.tensor_tensor(prod[:, d - 1, 0:BLK - d, :], k[:, d:BLK, :], k[:, 0:BLK - d, :], ALU.mult)
                    ins.then_inc(prod_ok, 1)

                def outgoing(n):
                    dve.wait_ge(st_k[n.slot], n.stores())
                    dve.tensor_tensor(by_pos(kout[n.slot][:, :]), by_pos(kT[n.slot][:, :]),
                                      c.kfac[:, :].unsqueeze(2).to_broadcast([P, BLK, NBLK]), ALU.mult).then_inc(kout_ok, 1)

                def solve(n, j):
                    if j == 0:
                        dve.wait_ge(coup_ok, n.count(1, 2))
                        dve.wait_ge(r_in, n.count(1, 2))
                    sweep(dve, n, rr[n.slot][:, :], tmp_r, r_step, j)

                def step(n, m, l):
                    at(n, products)
                    at(m, square_sums)
                    at(l, statistics)
                    at(n, outgoing)
                    at(l, aggregate)
                    at(m, inverse_rms)
                    at(l, scale)
                    at(l, offset)
                    at(m, keys)
                    at(n, solve, 0)
                    at(n, solve, 1)
                    at(n, solve, 2)

                dve.sem_inc(rms_ok, 1)
                dve.sem_inc(ssq_ok, 1)
                dve.sem_inc(prod_ok, 2)
                dve.sem_inc(kout_ok, 2)
                for u in range(2):
                    dve.sem_inc(st_k[u], 16)
                dve.sem_inc(r_step, 2 * SWEEPS)
                walk(dve, step)

            @block.tensor
            def _(pe):
                def normed(m):
                    pe.wait_ge(xn_ok, m.count(1, 1))
                    pe.wait_ge(xT_ok, m.count(1, 1))
                    for t in range(NT):
                        ins = nc.tensor.transpose(ps_x[:, t, :], xn[m.slot][:, t, :], c.ident[:, :])
                    ins.then_inc(x_tr, 1)

                def keys(m):
                    pe.wait_ge(keys_ok, m.count(1, 1))
                    pe.wait_ge(kT_ok, m.count(1, 1))
                    for t in range(NT):
                        ins = nc.tensor.transpose(ps_k[:, t, :], keys_t[:, t, :], c.ident[:, :])
                    ins.then_inc(k_tr, 1)

                def static(m):
                    pe.wait_ge(xT_ok, m.count(1, 2))
                    pe.wait_ge(r_in, m.count(1, 1))
                    nc.tensor.matmul(ps_s[:, :, :].rearrange("p a b -> p (a b)"), c.ws_t[:, :], xnT[m.slot][:, :],
                                     start=True, stop=True).then_inc(s_mm, 1)

                def couplings(n):
                    pe.wait_ge(prod_ok, n.count(1, 3))
                    pe.wait_ge(coup_ok, n.count(1, 1))
                    for d in range(1, BLK):
                        ins = nc.tensor.matmul(ps_n[d - 1][:, 0:BLK - d, :], c.head_ones[:, :], prod[:, d - 1, 0:BLK - d, :],
                                               start=True, stop=True)
                    ins.then_inc(n_mm, 1)

                def factors(n):
                    pe.wait_ge(k2_ok, n.count(1, 1))
                    pe.wait_ge(fac_ok, n.count(1, 1))
                    nc.tensor.matmul(ps_f[:, :, :].rearrange("p a b -> p (a b)"), c.head_ones[:, :], k2[:, :],
                                     start=True, stop=True).then_inc(f_mm, 1)

                def step(n, m, l):
                    at(m, normed)
                    at(n, couplings)
                    at(n, factors)
                    at(m, keys)
                    at(m, static)

                pe.sem_inc(x_tr, 2)
                pe.sem_inc(k_tr, 1)
                pe.sem_inc(n_mm, 1)
                walk(pe, step)


def recur_and_feed_forward(nc, io, scr, c):
    ctx = ExitStack()
    SLOTS = B
    BPS = L // BLK // SLOTS
    BSEG = SEG // BLK
    SPS = BSEG // BPS
    NSEG = L // SEG
    with ctx:
        def sb(name, shape, dt=F32):
            return ctx.enter_context(nc.sbuf_tensor(name, shape, dt))

        def sem(name):
            return ctx.enter_context(nc.semaphore(name))

        seg_p = [sb(f"r_p{u}", [P, G, DH, SEG]) for u in range(2)]
        seg_k = [sb(f"r_k{u}", [P, G, DH, SEG]) for u in range(2)]
        seg_r = [sb(f"r_r{u}", [P, G, DH, SEG]) for u in range(2)]
        seg_w = [sb(f"r_w{u}", [P, G, DH, SEG]) for u in range(2)]
        state = [sb(f"r_g{g}", [P, DH, DH]) for g in range(G)]
        pg = sb("r_pg", [P, 2, G, BLK, DH, DH + 1])
        kw = [sb(f"r_kw{g}", [P, DH * DH, BLK + 1]) for g in range(G)]

        x_f = sb("f_x", [P, L])
        x_h, x_l = sb("f_xh", [P, L], F32R), sb("f_xl", [P, L], F32R)
        a_f = sb("f_a", [P, NB, L])
        b_f = sb("f_b", [P, L])
        g_f = sb("f_g", [P, NB, L])
        g_h, g_l = sb("f_gh", [P, NB, L], F32R), sb("f_gl", [P, NB, L], F32R)
        h_f = sb("f_h", [P, NB, L])
        h_h, h_l = sb("f_hh", [P, NB, L], F32R), sb("f_hl", [P, NB, L], F32R)
        e_f = sb("f_e", [P, NB, L])
        e_h, e_l = sb("f_eh", [P, NB, L], F32R), sb("f_el", [P, NB, L], F32R)
        y_t = sb("f_y", [P, L])
        z_ps = [ctx.enter_context(nc.psum_tensor(f"f_z{i}", [P, L], F32)) for i in range(4)]
        h_ps = [ctx.enter_context(nc.psum_tensor(f"f_h{i}", [P, L], F32)) for i in range(4)]

        seg_in = [sem(f"r_seg_in{u}") for u in range(2)]
        seg_done = sem("r_seg_done")
        w_out = [sem(f"r_w_out{u}") for u in range(2)]
        laying = sem("r_laying")
        r_laid = sem("r_laid")
        old_laid = [sem(f"r_old_laid{g}") for g in range(G)]
        m1 = [sem(f"r_m1_{g}") for g in range(G)]
        w_ok = [sem(f"r_w_{g}") for g in range(G)]
        m2 = [sem(f"r_m2_{g}") for g in range(G)]
        g_ok = [sem(f"r_g_{g}") for g in range(G)]
        ready = sem("f_ready")

        x_in = sem("f_x_in")
        xh_ok, xl_ok = sem("f_xh"), sem("f_xl")
        z1_mm, z2_mm = sem("f_z1_mm"), sem("f_z2_mm")
        a_ok = sem("f_a_ok")
        gate_ok = sem("f_gate")
        b_ok, last_gate_ok = sem("f_b_ok"), sem("f_last_gate")
        gh_ok, gl_ok = sem("f_gh_ok"), sem("f_gl_ok")
        h1_mm, h2_mm, y_mm = sem("f_h1_mm"), sem("f_h2_mm"), sem("f_y_mm")
        hh_ok, hl_ok = sem("f_hh_ok"), sem("f_hl_ok")
        eh_ok, el_ok = sem("f_eh_ok"), sem("f_el_ok")
        y_ok = sem("f_y_ok")
        y_out = sem("f_y_out")

        def over_groups(name):
            return scr[name].rearrange("(g b) (h k) t -> (b h) g k t", g=G, h=H)

        with nc.Block() as block:
            @block.sync
            def _(sp):
                def load(seg, u):
                    sp.wait_ge(seg_done, seg + 1)
                    for tile, name in ((seg_p, "P"), (seg_k, "K"), (seg_r, "R")):
                        for g in range(G):
                            sp.dma_start(tile[u][:, g, :, :], over_groups(name)[:, g, :, bass.ds(seg * SEG, SEG)]
                                         ).then_inc(seg_in[u], 16)

                def store(seg, u):
                    sp.wait_ge(seg_done, seg + 3)
                    for g in range(G):
                        sp.dma_start(over_groups("W")[:, g, :, bass.ds(seg * SEG, SEG)], seg_w[u][:, g, :, :]
                                     ).then_inc(w_out[u], 16)

                def load_x(slot):
                    sp.dma_start(x_f[:, :], scr["xnT"][bass.ds(slot, 1), :, :].rearrange("b p t -> p (b t)")).then_inc(x_in, 16)

                def store_y(slot):
                    sp.wait_ge(y_ok, slot + 2)
                    sp.dma_start(scr["ffnT"][bass.ds(slot, 1), :, :].rearrange("b p t -> p (b t)"), y_t[:, :]).then_inc(y_out, 16)

                def feed_forward(slot):
                    sp.wait_ge(xl_ok, slot + 1)
                    load_x(slot + 1)
                    store_y(slot)

                load_x(0)
                load(0, 0)
                load(1, 1)
                with sp.Fori(0, NSEG // 2 - 1) as it:
                    for u in range(2):
                        for q in range(SPS):
                            feed_forward(it * (2 * SPS) + (u * SPS + q))
                        store(it * 2 + u, u)
                        load(it * 2 + (u + 2), u)
                for u in range(2):
                    for q in range(SPS):
                        feed_forward((NSEG - 2 + u) * SPS + q)
                    store(NSEG - 2 + u, u)
                store_y(SLOTS)
                sp.wait_ge(y_out, 16 * SLOTS + 32)
                for u in range(2):
                    sp.wait_ge(w_out[u], 16 * G * (NSEG // 2) + 16 * G)

            @block.vector
            def _(dve):
                for u in range(2):
                    dve.sem_inc(w_out[u], 16 * G)
                dve.sem_inc(seg_done, 1)
                for g in range(G):
                    dve.sem_inc(w_ok[g], 2)
                    dve.memset(state[g][:, :, :], 0.0).then_inc(g_ok[g], 1)
                with dve.Fori(0, NSEG // 2) as it:
                    for u in range(2):
                        dve.wait_ge(seg_in[u], it * (48 * G) + 48 * G)
                        dve.wait_ge(w_out[u], it * (16 * G) + 16 * G)
                        for b in range(BSEG):
                            blk = it * (2 * BSEG) + (u * BSEG + b)
                            t = slice(b * BLK, b * BLK + BLK)
                            par = b % 2
                            for g in range(G):
                                dve.wait_ge(g_ok[g], blk + 1)
                                dve.tensor_tensor(pg[:, par, g, :, :, 0:DH],
                                                  state[g][:, :, :].unsqueeze(1).to_broadcast([P, BLK, DH, DH]),
                                                  seg_p[u][:, g, :, t].rearrange("p k i -> p i k").unsqueeze(2)
                                                  .to_broadcast([P, BLK, DH, DH]),
                                                  ALU.mult).then_inc(m1[g], 1)
                            if b % BPS == 0:
                                for g in range(G):
                                    dve.tensor_scalar(kw[g][:, :, BLK], state[g][:, :, :].rearrange("p v k -> p (v k)"),
                                                      c.lam4[:, :], None, ALU.mult).then_inc(old_laid[g], 1)
                            if b == 0:
                                dve.sem_inc(seg_done, 1)
                            dve.wait_ge(r_laid, blk + 1)
                            for g in range(G):
                                dve.wait_ge(m1[g], blk + 1)
                                dve.tensor_reduce(seg_w[u][:, g, :, t].rearrange("p v i -> p i v"),
                                                  pg[:, par, g, :, :, :], AX.X, ALU.add).then_inc(w_ok[g], 1)
                            for g in range(G):
                                dve.wait_ge(w_ok[g], blk + 3)
                                dve.tensor_tensor(kw[g][:, :, 0:BLK].rearrange("p (v k) i -> p v k i", k=DH),
                                                  seg_w[u][:, g, :, t].unsqueeze(2).to_broadcast([P, DH, DH, BLK]),
                                                  seg_k[u][:, g, :, t].unsqueeze(1).to_broadcast([P, DH, DH, BLK]),
                                                  ALU.mult).then_inc(m2[g], 1)
                            for g in range(G):
                                dve.wait_ge(m2[g], blk + 1)
                                dve.wait_ge(old_laid[g], blk + 1)
                                last = dve.tensor_reduce(state[g][:, :, :].rearrange("p v k -> p (v k)"),
                                                         kw[g][:, :, :], AX.X, ALU.add)
                                last.then_inc(g_ok[g], 1)
                            q, at = b // BPS, b % BPS
                            slot = it * (2 * SPS) + (u * SPS + q)
                            for j in {0: (0, 1), 2: (2,)}.get(at, ()):
                                dve.wait_ge(z2_mm, slot * NB + (j + 1))
                                dve.wait_ge(a_ok, slot * NB + (j + 1))
                                dve.scalar_tensor_tensor(out=g_f[:, j, :], in0=z_ps[2 * (j % 2) + 1][:, :],
                                                         scalar=c.s2[:, j:j + 1], in1=a_f[:, j, :],
                                                         op0=ALU.mult, op1=ALU.mult).then_inc(gate_ok, 1)
                for g in range(G):
                    dve.wait_ge(g_ok[g], NSEG * BSEG + 1)
                dve.sem_inc(seg_done, 1)

            @block.gpsimd
            def _(pool):
                def rest(full, upper, lower, done):
                    pool.tensor_tensor(lower, full, upper.bitcast(F32), ALU.subtract).then_inc(done, 1)

                def lay_r(blk, u, b):
                    for g in range(G):
                        pool.wait_ge(w_ok[g], blk + 1)
                    pool.sem_inc(laying, 1)
                    pool.tensor_copy(pg[:, b % 2, :, :, :, DH].rearrange("p g i v -> p g v i"),
                                     seg_r[u][:, :, :, b * BLK:b * BLK + BLK]).then_inc(r_laid, 1)

                def last_gate(slot):
                    pool.wait_ge(b_ok, slot + 1)
                    pool.wait_ge(a_ok, slot * NB + NB)
                    pool.tensor_tensor(g_f[:, NB - 1, :], a_f[:, NB - 1, :], b_f[:, :], ALU.mult).then_inc(last_gate_ok, 1)

                def gate_rest(slot, j):
                    pool.wait_ge(gh_ok, slot * NB + (j + 1))
                    rest(g_f[:, j, :], g_h[:, j, :], g_l[:, j, :], gl_ok)

                def hidden1_rest(slot, o):
                    pool.wait_ge(hh_ok, slot * NB + (o + NB + 1))
                    rest(h_f[:, o, :], h_h[:, o, :], h_l[:, o, :], hl_ok)

                def hidden2_rest(slot, o):
                    pool.wait_ge(eh_ok, slot * NB + (o + 1))
                    rest(e_f[:, o, :], e_h[:, o, :], e_l[:, o, :], el_ok)

                def input_rest(slot):
                    pool.wait_ge(xh_ok, slot + 1)
                    rest(x_f[:, :], x_h[:, :], x_l[:, :], xl_ok)

                pool.memset(h_h[:, :, :].bitcast(F32), 0.0)
                pool.memset(h_l[:, :, :].bitcast(F32), 0.0).then_inc(ready, 1)
                input_rest(0)
                with pool.Fori(0, NSEG // 2) as it:
                    pool.wait_ge(seg_in[0], it * (48 * G) + 48 * G)
                    lay_r(it * (2 * BSEG), 0, 0)
                    for u in range(2):
                        for q in range(SPS):
                            slot = it * (2 * SPS) + (u * SPS + q)
                            for at in range(BPS):
                                ahead = u * BSEG + q * BPS + at + 1
                                if ahead == BSEG:
                                    pool.wait_ge(seg_in[1], it * (48 * G) + 48 * G)
                                if ahead < 2 * BSEG:
                                    lay_r(it * (2 * BSEG) + ahead, ahead // BSEG, ahead % BSEG)
                                if at == 2:
                                    gate_rest(slot, 0)
                                    gate_rest(slot, 1)
                                if at == 3:
                                    last_gate(slot)
                                    gate_rest(slot, 2)
                                    gate_rest(slot, 3)
                                if at == 4:
                                    hidden2_rest(slot, 0)
                                    hidden2_rest(slot, 1)
                                if at == 5:
                                    hidden2_rest(slot, 2)
                                    hidden2_rest(slot, 3)
                                if at == 6:
                                    hidden1_rest(slot, 0)
                                    hidden1_rest(slot, 1)
                                if at == 7:
                                    hidden1_rest(slot, 2)
                                    input_rest(slot + 1)
                                    hidden1_rest(slot, 3)
                for o in range(NB):
                    hidden2_rest(SLOTS, o)

            @block.scalar
            def _(act):
                def input_upper(slot):
                    act.wait_ge(x_in, slot * 16 + 16)
                    act.activation(x_h[:, :], x_f[:, :], ACT.Copy).then_inc(xh_ok, 1)

                def silu(slot, j):
                    act.wait_ge(z1_mm, slot * NB + (j + 1))
                    act.activation(a_f[:, j, :], z_ps[2 * (j % 2)][:, :], ACT.Silu, scale=c.s1[:, j:j + 1]).then_inc(a_ok, 1)

                def last_factor(slot):
                    act.wait_ge(z2_mm, slot * NB + NB)
                    act.wait_ge(last_gate_ok, slot + 1)
                    act.activation(b_f[:, :], z_ps[3][:, :], ACT.Copy, scale=c.s2[:, NB - 1:NB]).then_inc(b_ok, 1)

                def gate_upper(slot, j):
                    if j < NB - 1:
                        act.wait_ge(gate_ok, slot * (NB - 1) + (j + 1))
                    else:
                        act.wait_ge(last_gate_ok, slot + 2)
                    act.activation(g_h[:, j, :], g_f[:, j, :], ACT.Copy).then_inc(gh_ok, 1)

                def gelu(src, scale, full, upper, done):
                    act.activation(full, src, ACT.Gelu, scale=scale)
                    act.activation(upper, src, ACT.Gelu, scale=scale).then_inc(done, 1)

                def hidden1(slot, o):
                    act.wait_ge(h1_mm, slot * NB + (o + 1))
                    gelu(h_ps[o][:, :], c.t1[:, o:o + 1], h_f[:, o, :], h_h[:, o, :], hh_ok)

                def hidden2(slot, o):
                    act.wait_ge(h2_mm, slot * NB + (o + 1))
                    gelu(h_ps[o][:, :], c.t2[:, o:o + 1], e_f[:, o, :], e_h[:, o, :], eh_ok)

                def result(slot):
                    act.wait_ge(y_mm, slot + 1)
                    act.wait_ge(y_out, slot * 16 + 16)
                    act.activation(y_t[:, :], z_ps[3][:, :], ACT.Identity, scale=c.s3[:, :], bias=c.ob[:, :]).then_inc(y_ok, 1)

                act.sem_inc(y_out, 16)
                act.sem_inc(y_ok, 1)
                act.sem_inc(hh_ok, NB)
                act.sem_inc(last_gate_ok, 1)
                input_upper(0)
                with act.Fori(0, SLOTS) as slot:
                    for at in range(BPS):
                        if at == 0:
                            silu(slot, 0)
                        else:
                            for g in range(G):
                                act.wait_ge(g_ok[g], slot * BPS + (at + 1))
                                act.activation(kw[g][:, :, BLK], state[g][:, :, :].rearrange("p v k -> p (v k)"),
                                               ACT.Copy, scale=c.lam4[:, :]).then_inc(old_laid[g], 1)
                        if at == 0:
                            silu(slot, 1)
                        if at == 1:
                            gate_upper(slot, 0)
                            gate_upper(slot, 1)
                        if at == 2:
                            silu(slot, 2)
                            silu(slot, 3)
                            last_factor(slot)
                        if at == 3:
                            gate_upper(slot, 2)
                            gate_upper(slot, 3)
                            hidden2(slot, 0)
                        if at == 4:
                            hidden2(slot, 1)
                            hidden2(slot, 2)
                        if at == 5:
                            hidden2(slot, 3)
                            hidden1(slot, 0)
                        if at == 6:
                            hidden1(slot, 1)
                            hidden1(slot, 2)
                            act.wait_ge(z2_mm, slot * NB + NB)
                            input_upper(slot + 1)
                        if at == 7:
                            hidden1(slot, 3)
                            result(slot)
                for o in range(NB):
                    hidden2(SLOTS, o)
                result(SLOTS)

            @block.tensor
            def _(pe):
                general = pe.value_load(c.flag[0:1, 0:1], min_val=0, max_val=1)

                def product(bank, weights, upper, lower, done):
                    n = len(weights)
                    for k in range(n):
                        nc.tensor.matmul(bank, c.w_hi[:, weights[k], :], upper[k], start=k == 0, stop=False)
                        if k < n - 1:
                            nc.tensor.matmul(bank, c.w_hi[:, weights[k], :], lower[k], start=False, stop=False)
                    with pe.If(general > 0):
                        for k in range(n):
                            nc.tensor.matmul(bank, c.w_lo[:, weights[k], :], upper[k], start=False, stop=False)
                            nc.tensor.matmul(bank, c.w_lo[:, weights[k], :], lower[k], start=False, stop=False)
                    nc.tensor.matmul(bank, c.w_hi[:, weights[n - 1], :], lower[n - 1], start=False, stop=True).then_inc(done, 1)

                def gates(slot, j):
                    if j == 0:
                        pe.wait_ge(xh_ok, slot + 1)
                        pe.wait_ge(xl_ok, slot + 1)
                    if j == 1:
                        pe.wait_ge(y_ok, slot + 1)
                    if j >= 2:
                        pe.wait_ge(gate_ok, slot * (NB - 1) + (j - 1))
                    product(z_ps[2 * (j % 2)][:, :], [W1 + j], [x_h[:, :]], [x_l[:, :]], z1_mm)
                    product(z_ps[2 * (j % 2) + 1][:, :], [W2 + j], [x_h[:, :]], [x_l[:, :]], z2_mm)

                parts = lambda t: [t[:, k, :] for k in range(NB)]

                def second(slot, o):
                    if o == 0:
                        pe.wait_ge(hh_ok, slot * NB + NB)
                        pe.wait_ge(hl_ok, slot * NB + NB)
                    product(h_ps[o][:, :], [H2 + NB * k + o for k in range(NB)], parts(h_h), parts(h_l), h2_mm)

                def first(slot, o):
                    if o == 0:
                        pe.wait_ge(gh_ok, slot * NB + NB)
                        pe.wait_ge(gl_ok, slot * NB + NB)
                    pe.wait_ge(eh_ok, slot * NB + (o + 1))
                    product(h_ps[o][:, :], [H1 + NB * k + o for k in range(NB)], parts(g_h), parts(g_l), h1_mm)

                def output(slot):
                    pe.wait_ge(eh_ok, slot * NB + NB)
                    pe.wait_ge(el_ok, slot * NB + NB)
                    product(z_ps[3][:, :], [W3 + k for k in range(NB)], parts(e_h), parts(e_l), y_mm)

                pe.sem_inc(hl_ok, NB)
                pe.wait_ge(ready, 1)
                with pe.Fori(0, SLOTS) as slot:
                    gates(slot, 0)
                    gates(slot, 1)
                    second(slot, 0)
                    second(slot, 1)
                    gates(slot, 2)
                    gates(slot, 3)
                    second(slot, 2)
                    second(slot, 3)
                    for o in range(NB):
                        first(slot, o)
                    output(slot)
                for o in range(NB):
                    second(SLOTS, o)
                output(SLOTS)


def second_layer(nc, io, scr, c, out):
    ctx = ExitStack()
    HW = DH * DH * H // 2
    HEADS = H // 2
    with ctx:
        def sb(name, shape):
            return ctx.enter_context(nc.sbuf_tensor("l1_" + name, shape, F32))

        def pb(name):
            return ctx.enter_context(nc.psum_tensor("l1_" + name, [P, NT, P], F32))

        def sem(name):
            return ctx.enter_context(nc.semaphore("l1_" + name))

        def two(name, shape):
            return [sb(name + "0", shape), sb(name + "1", shape)]

        tile = [P, NT, P]
        x_in, f_in = two("x_in", tile), two("f_in", [P, L])
        w_in, fac_in = two("w_in", [P, L]), two("fac_in", [P, L])
        y_t = sb("y_t", [P, L])
        stats = sb("stats", [P, NT, 6])
        mv1, mv2 = sb("mv1", [P, NT, 2]), sb("mv2", [P, NT, 2])
        sd1, sd2 = sb("sd1", [P, NT]), sb("sd2", [P, NT])
        rs1, rs2 = sb("rs1", [P, NT]), sb("rs2", [P, NT])
        nm1, nm2 = sb("nm1", [P, NT]), sb("nm2", [P, NT])
        yn, yw, xf, xn = sb("yn", tile), sb("yw", tile), sb("xf", tile), sb("xn", tile)
        x1 = two("x1", tile)
        x1b = two("x1b", tile)
        xnT = sb("xnT", tile)
        qkv = two("qkv", [P, NT, 4 * P])
        qd = two("qd", tile)
        qdT = two("qdT", tile)
        kv = two("kv", [P, 2, HW])
        qs = two("qs", [P, 2 * HW])
        o_in = two("o_in", tile)
        past = two("past", [P, NT - 1, P])
        oT = sb("oT", tile)
        res = sb("res", tile)

        ps_y, ps_x, ps_q, ps_o, ps_m, ps_kv = pb("ps_y"), pb("ps_x"), pb("ps_q"), pb("ps_o"), pb("ps_m"), pb("ps_kv")
        ps_s = ctx.enter_context(nc.psum_tensor("l1_ps_s", [P, 2, HW], F32))

        in_ok = [sem("in_ok0"), sem("in_ok1")]
        y_ok, y_tr, f_tr = sem("y_ok"), sem("y_tr"), sem("f_tr")
        stat, aggregating, st1, st2 = sem("stat"), sem("aggregating"), sem("st1"), sem("st2")
        sd1_ok, sd2_ok, rs1_ok, rs2_ok, nm1_ok, nm2_ok = (sem("sd1_ok"), sem("sd2_ok"), sem("rs1_ok"), sem("rs2_ok"),
                                                          sem("nm1_ok"), sem("nm2_ok"))
        yn_ok, yw_ok, xf_ok, x1_ok, x1b_ok = sem("yn_ok"), sem("yw_ok"), sem("xf_ok"), sem("x1_ok"), sem("x1b_ok")
        xn_ok, x_tr, xT_ok = sem("xn_ok"), sem("x_tr"), sem("xT_ok")
        qkv_mm, qkv_ok, qd_ok, q_tr, qT_ok = sem("qkv_mm"), sem("qkv_ok"), sem("qd_ok"), sem("q_tr"), sem("qT_ok")
        kv_ok, tri_mm, qs_ok, o_ok = sem("kv_ok"), sem("tri_mm"), sem("qs_ok"), sem("o_ok")
        past_mm, past_ok, o_mm, oT_ok = sem("past_mm"), sem("past_ok"), sem("o_mm"), sem("oT_ok")
        out_mm, res_ok, stored = sem("out_mm"), sem("res_ok"), sem("stored")

        def walk(engine, step):
            def outside(k):
                step(*[Sequence(None, k + d) if 0 <= k + d < B else None for d in (-1, 0, 1, 2)])

            for k in (-2, -1, 0):
                outside(k)
            with engine.Fori(0, B // 2 - 2) as turn:
                for k in (1, 2):
                    step(*[Sequence(turn, k + d) for d in (-1, 0, 1, 2)])
            for k in range(B - 3, B + 1):
                outside(k)

        with nc.Block() as block:
            @block.sync
            def _(sp):
                def load(l):
                    if l.turn is not None or l.off >= 2:
                        sp.wait_ge(xf_ok, l.count(1, -1))
                    by_token = io["L0_attn_x"][l.row(), :, :].rearrange("b (t p) d -> p (b t) d", p=P)
                    sp.dma_start(w_in[l.slot][:, :], scr["W"][l.row(), :, :].rearrange("b p t -> p (b t)")).then_inc(in_ok[l.slot], 16)
                    sp.dma_start(fac_in[l.slot][:, :], scr["fac"][l.row(), :, :].rearrange("b p t -> p (b t)")).then_inc(in_ok[l.slot], 16)
                    sp.dma_start(f_in[l.slot][:, :], scr["ffnT"][l.row(1), :, :].rearrange("b p t -> p (b t)")).then_inc(in_ok[l.slot], 16)
                    sp.dma_start(x_in[l.slot][:, :, :], by_token).then_inc(in_ok[l.slot], 16)

                def store(f):
                    sp.wait_ge(res_ok, f.count(1, 3))
                    sp.dma_start(out[f.row(), :, :].rearrange("b (t p) d -> p (b t) d", p=P), res[:, :, :]).then_inc(stored, 16)

                for off in range(4):
                    load(Sequence(None, off))
                with sp.Fori(0, B // 2 - 2) as turn:
                    for off in range(2):
                        store(Sequence(turn, off))
                        load(Sequence(turn, off + 4))
                for off in range(B - 4, B):
                    store(Sequence(None, off))
                sp.wait_ge(stored, 16 * B + 16)

            @block.gpsimd
            def _(pool):
                def outputs(l):
                    pool.wait_ge(in_ok[l.slot], l.loads())
                    pool.wait_ge(y_tr, l.count(1, 1))
                    pool.tensor_tensor(y_t[:, :], w_in[l.slot][:, :], fac_in[l.slot][:, :], ALU.mult).then_inc(y_ok, 1)

                def weighted(l):
                    pool.wait_ge(yn_ok, l.count(1, 2))
                    pool.tensor_tensor(yw[:, :, :], yn[:, :, :], c.ow[:, :].unsqueeze(1).to_broadcast(tile), ALU.mult).then_inc(yw_ok, 1)

                def residual(l):
                    pool.wait_ge(xf_ok, l.count(1, 1))
                    pool.wait_ge(xn_ok, l.count(1, 1))
                    pool.wait_ge(yw_ok, l.count(1, 2))
                    pool.tensor_tensor(x1[l.slot][:, :, :], yw[:, :, :], xf[:, :, :], ALU.add).then_inc(x1_ok, 1)

                def straight(n):
                    pool.wait_ge(x1_ok, n.count(1, 2))
                    pool.wait_ge(qkv_ok, n.count(NT, NT + 1))
                    pool.wait_ge(res_ok, n.count(1, 1))
                    pool.tensor_tensor(x1b[n.slot][:, :, :], x1[n.slot][:, :, :], qkv[n.slot][:, :, 3 * P:4 * P], ALU.add).then_inc(x1b_ok, 1)

                def decayed(m, t):
                    pool.wait_ge(qkv_ok, m.count(NT, t + 2))
                    pool.tensor_tensor(qd[m.slot][:, t, :], qkv[m.slot][:, t, 0:P], c.dec[:, t, :], ALU.mult).then_inc(qd_ok, 1)

                def outer(n, t):
                    pool.wait_ge(qkv_ok, n.count(NT, t + 2))
                    pool.wait_ge(tri_mm, n.count(NT, t + 1))
                    k = qkv[n.slot][:, t, P:2 * P].rearrange("p (h k) -> p h k", h=H).unsqueeze(3).to_broadcast([P, H, DH, DH])
                    v = qkv[n.slot][:, t, 2 * P:3 * P].rearrange("p (h v) -> p h v", h=H).unsqueeze(2).to_broadcast([P, H, DH, DH])
                    dst = kv[t % 2][:, :, :].rearrange("p a (h k v) -> p (a h) k v", h=HEADS, k=DH)
                    pool.tensor_tensor(dst, k, v, ALU.mult).then_inc(kv_ok, 1)

                def step(f, n, m, l):
                    at(l, outputs)
                    at(n, outer, 2)
                    at(n, outer, 3)
                    at(n, straight)
                    at(l, weighted)
                    at(m, outer, 0)
                    at(l, residual)
                    at(m, decayed, 0)
                    at(m, decayed, 1)
                    at(m, outer, 1)
                    at(m, decayed, 2)
                    at(m, decayed, 3)

                pool.sem_inc(yw_ok, 1)
                pool.sem_inc(x1_ok, 1)
                pool.sem_inc(x1b_ok, 2)
                walk(pool, step)

            @block.scalar
            def _(act):
                def root1(l):
                    act.wait_ge(st1, l.count(1, 1))
                    act.activation(sd1[:, :], mv1[:, :, 1], ACT.Sqrt, bias=c.eps_ln[:, :]).then_inc(sd1_ok, 1)

                def norm1(l):
                    act.wait_ge(nm1_ok, l.count(1, 1))
                    act.wait_ge(yw_ok, l.count(1, 1))
                    for t in range(NT):
                        ins = act.activation(yn[:, t, :], ps_y[:, t, :], ACT.Identity, scale=rs1[:, t:t + 1], bias=nm1[:, t:t + 1])
                    ins.then_inc(yn_ok, 1)

                def root2(l):
                    act.wait_ge(st2, l.count(1, 1))
                    act.activation(sd2[:, :], mv2[:, :, 1], ACT.Sqrt, bias=c.eps_ln[:, :]).then_inc(sd2_ok, 1)

                def norm2(m):
                    act.wait_ge(nm2_ok, m.count(1, 1))
                    act.wait_ge(x_tr, m.count(1, 1))
                    for t in range(NT):
                        ins = act.activation(xn[:, t, :], x1[m.slot][:, t, :], ACT.Identity, scale=rs2[:, t:t + 1], bias=nm2[:, t:t + 1])
                    ins.then_inc(xn_ok, 1)

                def normed(m):
                    act.wait_ge(x_tr, m.count(1, 2))
                    act.wait_ge(qkv_mm, m.count(NT, 1))
                    act.activation(xnT[:, :, :], ps_x[:, :, :], ACT.Copy).then_inc(xT_ok, 1)

                def project(m, t):
                    act.wait_ge(qkv_mm, m.count(NT, t + 2))
                    act.wait_ge(x1b_ok, m.count(1, 1))
                    act.activation(qkv[m.slot][:, t, :], ps_q[:, :, :].rearrange("p a b -> p (a b)"), ACT.Copy).then_inc(qkv_ok, 1)

                def attended(f):
                    act.wait_ge(o_mm, f.count(1, 3))
                    act.wait_ge(out_mm, f.count(1, 1))
                    act.activation(oT[:, :, :], ps_o[:, :, :], ACT.Copy).then_inc(oT_ok, 1)

                def queries(n):
                    act.wait_ge(q_tr, n.count(1, 1))
                    act.activation(qdT[n.slot][:, 1:NT, :], ps_m[:, 1:NT, :], ACT.Copy).then_inc(qT_ok, 1)

                def step(f, n, m, l):
                    at(m, norm2)
                    at(f, attended)
                    at(n, queries)
                    at(m, normed)
                    at(l, root1)
                    at(m, project, 0)
                    at(l, norm1)
                    at(m, project, 1)
                    at(m, project, 2)
                    at(m, project, 3)
                    at(l, root2)

                act.sem_inc(xT_ok, 1)
                act.sem_inc(oT_ok, 1)
                act.sem_inc(qkv_ok, 1)
                act.sem_inc(yn_ok, 1)
                act.sem_inc(xn_ok, 2)
                act.sem_inc(stored, 16)
                walk(act, step)

            @block.vector
            def _(dve):
                def statistics(l, src, mv, done, links):
                    for t in range(NT):
                        ins = dve.bn_stats(out=stats[:, t, :], in_=src[:, t, :])
                    ins.then_inc(stat, 1)
                    dve.wait_ge(stat, l.count(2, links))
                    dve.sem_inc(aggregating, 1)
                    for t in range(NT):
                        ins = dve.bn_aggr(out=mv[:, t, :], in_=stats[:, t:t + 1, :])
                    ins.then_inc(done, 1)

                def stats1(l):
                    dve.wait_ge(y_tr, l.count(1, 2))
                    statistics(l, ps_y, mv1, st1, 1)

                def scale1(l):
                    dve.wait_ge(sd1_ok, l.count(1, 1))
                    dve.wait_ge(yn_ok, l.count(1, 1))
                    dve.reciprocal(rs1[:, :], sd1[:, :]).then_inc(rs1_ok, 1)
                    dve.wait_ge(rs1_ok, l.count(1, 1))
                    dve.scalar_tensor_tensor(out=nm1[:, :], in0=mv1[:, :, 0], scalar=-1.0, in1=rs1[:, :],
                                             op0=ALU.mult, op1=ALU.mult).then_inc(nm1_ok, 1)

                def branches(l):
                    dve.wait_ge(in_ok[l.slot], l.loads())
                    dve.wait_ge(f_tr, l.count(1, 1))
                    dve.wait_ge(x1_ok, l.count(1, 1))
                    dve.tensor_tensor(xf[:, :, :], x_in[l.slot][:, :, :], ps_x[:, :, :], ALU.add).then_inc(xf_ok, 1)

                def stats2(l):
                    dve.wait_ge(x1_ok, l.count(1, 2))
                    statistics(l, x1[l.slot], mv2, st2, 2)

                def scale2(m):
                    dve.wait_ge(sd2_ok, m.count(1, 1))
                    dve.reciprocal(rs2[:, :], sd2[:, :]).then_inc(rs2_ok, 1)
                    dve.wait_ge(rs2_ok, m.count(1, 1))
                    dve.scalar_tensor_tensor(out=nm2[:, :], in0=mv2[:, :, 0], scalar=-1.0, in1=rs2[:, :],
                                             op0=ALU.mult, op1=ALU.mult).then_inc(nm2_ok, 1)

                def scores(n, t):
                    dve.wait_ge(qd_ok, n.count(NT, t + 1))
                    dve.wait_ge(tri_mm, n.count(NT, t + 3))
                    q = qd[n.slot][:, t, :].rearrange("p (h k) -> p h k", h=H).unsqueeze(3).to_broadcast([P, H, DH, DH])
                    dve.tensor_tensor(qs[t % 2][:, :].rearrange("p (h k v) -> p h k v", h=H, k=DH),
                                      ps_s[:, :, :].rearrange("p a (h k v) -> p (a h) k v", h=HEADS, k=DH), q, ALU.mult).then_inc(qs_ok, 1)
                    dve.wait_ge(qs_ok, n.count(NT, t + 2))
                    dve.wait_ge(o_mm, n.count(1, 1))
                    dve.tensor_reduce(out=o_in[n.slot][:, t, :].rearrange("p (h v) -> p h v", h=H),
                                      in_=qs[t % 2][:, :].rearrange("p (h k v) -> p h v k", h=H, k=DH), axis=AX.X, op=ALU.add).then_inc(o_ok, 1)

                def state(n, t):
                    dve.wait_ge(past_mm, n.count(NT - 1, t + 1))
                    dve.tensor_tensor(past[n.slot][:, t, :], ps_kv[:, 0, :], c.head_ones[:, :], ALU.mult).then_inc(past_ok, 1)

                def result(f):
                    dve.wait_ge(out_mm, f.count(1, 2))
                    dve.wait_ge(x1b_ok, f.count(1, 3))
                    dve.wait_ge(stored, f.count(16, 16))
                    dve.tensor_tensor(res[:, :, :], ps_m[:, :, :], x1b[f.slot][:, :, :], ALU.add).then_inc(res_ok, 1)

                def step(f, n, m, l):
                    at(m, scale2)
                    at(n, scores, 0)
                    at(n, state, 0)
                    at(l, stats1)
                    at(n, scores, 1)
                    at(n, state, 1)
                    at(l, scale1)
                    at(l, branches)
                    at(n, scores, 2)
                    at(n, state, 2)
                    at(f, result)
                    at(n, scores, 3)
                    at(l, stats2)

                dve.sem_inc(qs_ok, 1)
                dve.sem_inc(past_ok, 1)
                dve.sem_inc(res_ok, 2)
                walk(dve, step)

            @block.tensor
            def _(pe):
                def outputs(l):
                    pe.wait_ge(y_ok, l.count(1, 1))
                    pe.wait_ge(yn_ok, l.count(1, 1))
                    for t in range(NT):
                        ins = nc.tensor.transpose(ps_y[:, t, :], y_t[:, t * P:(t + 1) * P], c.ident[:, :])
                    ins.then_inc(y_tr, 1)

                def branches(l):
                    pe.wait_ge(in_ok[l.slot], l.loads())
                    pe.wait_ge(xT_ok, l.count(1, 1))
                    for t in range(NT):
                        ins = nc.tensor.transpose(ps_x[:, t, :], f_in[l.slot][:, t * P:(t + 1) * P], c.ident[:, :])
                    ins.then_inc(f_tr, 1)

                def normed(m):
                    pe.wait_ge(xn_ok, m.count(1, 3))
                    pe.wait_ge(xf_ok, m.count(1, 1))
                    for t in range(NT):
                        ins = nc.tensor.transpose(ps_x[:, t, :], xn[:, t, :], c.ident[:, :])
                    ins.then_inc(x_tr, 1)

                def project(m, t):
                    pe.wait_ge(xT_ok, m.count(1, 2))
                    pe.wait_ge(qkv_ok, m.count(NT, t + 1))
                    bank = ps_q[:, :, :].rearrange("p a b -> p (a b)")
                    nc.tensor.matmul(bank, xnT[:, t, :], c.w_second[:, :], start=True, stop=False)
                    nc.tensor.matmul(bank, c.one_rows[:, :], c.b_second[:, :], start=False, stop=True).then_inc(qkv_mm, 1)

                def queries(n):
                    pe.wait_ge(qd_ok, n.count(NT, NT))
                    pe.wait_ge(res_ok, n.count(1, 1))
                    for t in range(1, NT):
                        ins = nc.tensor.transpose(ps_m[:, t, :], qd[n.slot][:, t, :], c.ident[:, :])
                    ins.then_inc(q_tr, 1)

                def running(n, t):
                    pe.wait_ge(kv_ok, n.count(NT, t + 1))
                    pe.wait_ge(qs_ok, n.count(NT, t + 1))
                    nc.tensor.matmul(ps_s[:, 0, :], c.tri[:, :], kv[t % 2][:, 0, :], start=True, stop=True)
                    nc.tensor.matmul(ps_s[:, 1, :], c.tri[:, :], kv[t % 2][:, 1, :], start=True, stop=True).then_inc(tri_mm, 1)

                def state(n, t):
                    pe.wait_ge(past_ok, n.count(NT - 1, t + 1))
                    pe.wait_ge(qkv_ok, n.count(NT, t + 2))
                    nc.tensor.matmul(ps_kv[:, 0, :], qkv[n.slot][:, t, P:2 * P], qkv[n.slot][:, t, 2 * P:3 * P],
                                     start=t == 0, stop=True, skip_group_check=True).then_inc(past_mm, 1)

                def attended(f):
                    pe.wait_ge(qT_ok, f.count(1, 1))
                    pe.wait_ge(past_ok, f.count(NT - 1, NT))
                    pe.wait_ge(oT_ok, f.count(1, 1))
                    for t in range(NT):
                        pe.wait_ge(o_ok, f.count(NT, t + 1))
                        if t > 0:
                            nc.tensor.matmul(ps_o[:, t, :], past[f.slot][:, t - 1, :], qdT[f.slot][:, t, :], start=True, stop=False)
                        ins = nc.tensor.matmul(ps_o[:, t, :], o_in[f.slot][:, t, :], c.ident[:, :], start=t == 0, stop=True)
                    ins.then_inc(o_mm, 1)

                def final(f):
                    pe.wait_ge(oT_ok, f.count(1, 2))
                    if f.turn is not None or f.off < B - 1:
                        pe.wait_ge(qT_ok, f.count(1, 2))
                    for t in range(NT):
                        ins = nc.tensor.matmul(ps_m[:, t, :], oT[:, t, :], c.wo_t[:, :], start=True, stop=True)
                    ins.then_inc(out_mm, 1)

                def step(f, n, m, l):
                    at(n, running, 0)
                    at(n, state, 0)
                    at(f, attended)
                    at(n, queries)
                    at(l, outputs)
                    at(m, normed)
                    at(n, running, 1)
                    at(n, state, 1)
                    at(m, project, 0)
                    at(l, branches)
                    at(n, running, 2)
                    at(n, state, 2)
                    at(m, project, 1)
                    at(f, final)
                    at(n, running, 3)
                    at(m, project, 2)
                    at(m, project, 3)

                pe.sem_inc(y_tr, 1)
                pe.sem_inc(x_tr, 1)
                pe.sem_inc(tri_mm, 2)
                pe.sem_inc(o_mm, 2)
                pe.sem_inc(out_mm, 1)
                pe.sem_inc(qkv_mm, 1)
                walk(pe, step)


_INS = ("L0_attn_x", "L0_attn_W", "L0_attn_k_norm_w", "L0_attn_o_norm_w", "L0_attn_o_norm_b", "L0_attn_eta_raw",
        "L0_attn_lam_logit", "L0_ffn_w1_w", "L0_ffn_w1_s", "L0_ffn_w2_w", "L0_ffn_w2_s", "L0_ffn_h1_w", "L0_ffn_h1_s",
        "L0_ffn_h2_w", "L0_ffn_h2_s", "L0_ffn_w3_w", "L0_ffn_w3_s", "L1_attn_Wq", "L1_attn_bq", "L1_attn_Wk",
        "L1_attn_bk", "L1_attn_Wv", "L1_attn_bv", "L1_attn_Wo", "L1_attn_bo", "L1_attn_gamma", "L1_ffn_W", "L1_ffn_b",
        "L1_ffn_V_r", "L1_ffn_C")


def kernel(**inputs):
    import numpy as _np
    import concourse.bacc as _bacc
    from concourse import mybir as _mybir
    from concourse.bass_utils import run_bass_kernel_spmd as _run

    nc = _bacc.Bacc("TRN2", target_bir_lowering=False, num_devices=1)
    arrays, io = {}, {}
    for name in _INS:
        a = _np.ascontiguousarray(inputs[name])
        arrays[f"in_{name}_dram"] = a
        io[name] = nc.dram_tensor(f"in_{name}_dram", a.shape, _mybir.dt.from_np(a.dtype), kind="ExternalInput").ap()
    out = nc.dram_tensor("out_0_dram", (B, L, D), F32, kind="ExternalOutput").ap()
    build(nc, io, out)
    r = _run(nc, [arrays], core_ids=[0])
    return r.results[0]["out_0_dram"]
```
